# Optimizing a Trainium2 kernel written in Bass

```python
import numpy as np
import jax
import jax.numpy as jnp

def _softmax(x, axis=-1):
    return jax.nn.softmax(x, axis=axis)

def _gelu(x):
    return jax.nn.gelu(x, approximate=True)

def _silu(x):
    return jax.nn.silu(x)

def _sigmoid(x):
    return jax.nn.sigmoid(x)

def _layernorm(x, axis=-1, eps=1e-05):
    m = jnp.mean(x, axis=axis, keepdims=True)
    v = jnp.var(x, axis=axis, keepdims=True)
    return (x - m) / jnp.sqrt(v + eps)

def _scatter_add(tgt, idx, src, axis=0):
    return tgt.at[idx].add(src)

def _segment_sum(src, seg, n):
    return jax.ops.segment_sum(src, seg, n)
kernel_name = 'mk_flamingo_gated_d4_seqx_r4_15564c'

def setup_inputs(seed: int=0):
    np.random.seed(seed)
    _w = jnp.asarray

    def _rec_inputs():
        import jax
        import jax.numpy as jnp
        _rk = jax.random.key(seed)
        x = -0.0002928 + 1 * jax.random.normal(jax.random.fold_in(_rk, 1), (8, 256, 256), jnp.float32)
        _lenS = 256 - jax.random.randint(jax.random.fold_in(_rk, 7), (8,), 0, max(1, 256 // 4) + 1, jnp.int32)
        _lenS2 = 256 - jax.random.randint(jax.random.fold_in(_rk, 8), (8,), 0, max(1, 256 // 4) + 1, jnp.int32)
        _ctx_1024P = jax.random.normal(jax.random.fold_in(_rk, 11), (8, 16, 256), jnp.float32)
        _ctx_1024c = jax.random.dirichlet(jax.random.fold_in(_rk, 511), 0.3 * jnp.ones((16,), jnp.float32), (8, 256))
        _ctx_1024t = jnp.einsum('bsk,bkd->bsd', _ctx_1024c, _ctx_1024P)
        _ctx_1024t = _ctx_1024t * jax.lax.rsqrt(jnp.mean(jnp.square(_ctx_1024t)) + 1e-12) * 0.953939
        ctx_1024 = -1.39393e-06 + 0.999914 * (_ctx_1024t + 0.3 * jax.random.normal(jax.random.fold_in(_rk, 611), (8, 256, 256), jnp.float32))
        itok_SxS2_0_2016 = jax.random.randint(jax.random.fold_in(_rk, 12), (256, 256), 0, 2017, jnp.int32)
        _g = jax.random.normal(jax.random.fold_in(_rk, 9001), (2, 4), jnp.float32)
        _g = jnp.sign(_g) * jnp.maximum(jnp.abs(_g), 1.0) + (_g == 0) * 1.0
        g_xattn = _g[0]
        g_ffn = _g[1]
        return (x, ctx_1024, itok_SxS2_0_2016, g_xattn, g_ffn)
    x, ctx_1024, itok_SxS2_0_2016, g_xattn, g_ffn = _rec_inputs()

    def _L0_xattn_setup():
        import jax, jax.numpy as jnp
        import numpy as np
        import math
        EPS = 1e-08
        LN_EPS = 1e-05
        B, S, E, NH = (2, 512, 256, 4)
        DH = E // NH

        def _mlstm_cell(q, k, v, igate_w, igate_b, fgate_w, fgate_b, out_w):
            Bq, Sq, Eq = q.shape
            if_in = jnp.concatenate([q, k, v], axis=-1)
            ig = jnp.einsum('bsf,hf->bsh', if_in, igate_w) + igate_b
            fg = jnp.einsum('bsf,hf->bsh', if_in, fgate_w) + fgate_b
            ig = jnp.transpose(ig, (0, 2, 1))[..., None]
            fg = jnp.transpose(fg, (0, 2, 1))[..., None]
            qh = q.reshape(Bq, Sq, NH, DH).transpose(0, 2, 1, 3)
            kh = k.reshape(Bq, Sq, NH, DH).transpose(0, 2, 1, 3)
            vh = v.reshape(Bq, Sq, NH, DH).transpose(0, 2, 1, 3)
            log_fg = jax.nn.log_sigmoid(fg)
            cs = jnp.cumsum(log_fg, axis=2)
            cs_shift = jnp.concatenate([jnp.zeros_like(cs[:, :, :1]), cs[:, :, :-1]], axis=2)
            logfg_mat = cs - jnp.swapaxes(cs_shift, -2, -1)
            ltr = jnp.tril(jnp.ones((Sq, Sq), dtype=bool))
            logfg_mat = jnp.where(ltr, logfg_mat, -jnp.inf)
            log_D = logfg_mat + jnp.swapaxes(ig, -2, -1)
            max_log_D = jnp.max(log_D, axis=-1, keepdims=True)
            D = jnp.exp(log_D - max_log_D)
            qk = jnp.einsum('bhsd,bhtd->bhst', qh, kh / math.sqrt(DH))
            C = qk * D
            sum_C_abs = jnp.abs(jnp.sum(C, axis=-1, keepdims=True))
            normaliser = jnp.maximum(sum_C_abs, jnp.exp(-max_log_D))
            C_norm = C / (normaliser + EPS)
            h = jnp.einsum('bhst,bhtd->bhsd', C_norm, vh)
            mean = jnp.mean(h, axis=-1, keepdims=True)
            var = jnp.mean((h - mean) ** 2, axis=-1, keepdims=True)
            h_norm = (h - mean) / jnp.sqrt(var + LN_EPS)
            scale = (1.0 + out_w).reshape(1, NH, 1, DH)
            h_norm = h_norm * scale
            return h_norm.transpose(0, 2, 1, 3).reshape(Bq, Sq, Eq)
        key = jax.random.key(seed)
        ks = jax.random.split(key, 7)
        std_g = math.sqrt(2.0 / (5.0 * 3 * E))
        return {'q': jax.random.normal(ks[0], (B, S, E), dtype=jnp.float32), 'k': jax.random.normal(ks[1], (B, S, E), dtype=jnp.float32), 'v': jax.random.normal(ks[2], (B, S, E), dtype=jnp.float32), 'igate_w': jax.random.normal(ks[3], (NH, 3 * E), dtype=jnp.float32) * std_g, 'igate_b': jax.random.normal(ks[4], (NH,), dtype=jnp.float32) * 0.1, 'fgate_w': jax.random.normal(ks[5], (NH, 3 * E), dtype=jnp.float32) * std_g, 'fgate_b': jnp.linspace(3.4, 6.0, NH, dtype=jnp.float32), 'out_w': jnp.zeros((E,), dtype=jnp.float32)}
    _L0_xattn_all = _L0_xattn_setup()
    _L0_xattn_in = {k: v for k, v in _L0_xattn_all.items() if k in ('igate_w', 'igate_b', 'fgate_w', 'fgate_b', 'out_w')}
    del _L0_xattn_all

    def _L0_ffn_setup():
        import jax, jax.numpy as jnp
        import numpy as np
        key = jax.random.key(seed)
        k1, k2, k3 = jax.random.split(key, 3)
        B, S, D, E, H = (4, 512, 256, 8, 256)
        x = jax.random.normal(k1, (B, S, D), dtype=jnp.float32)
        Wg = jax.random.normal(k2, (D, E), dtype=jnp.float32) / np.sqrt(D)
        We = jax.random.normal(k3, (E, D, H), dtype=jnp.float32) / np.sqrt(D)
        be = jnp.zeros((E, H), dtype=jnp.float32)
        return {'x': x, 'Wg': Wg, 'We': We, 'be': be}
    _L0_ffn_all = _L0_ffn_setup()
    _L0_ffn_in = {k: v for k, v in _L0_ffn_all.items() if k in ('Wg', 'We', 'be')}
    del _L0_ffn_all

    def _L1_xattn_setup():
        import jax, jax.numpy as jnp
        import numpy as np
        D_MODEL = 256
        H = 16
        D_K = D_MODEL // H
        B = 4
        S = 512
        key = jax.random.key(seed)
        ks = jax.random.split(key, 11)
        s = 1.0 / np.sqrt(D_MODEL)
        return {'q': jax.random.normal(ks[0], (B, S, D_MODEL), jnp.float32), 'k': jax.random.normal(ks[1], (B, S, D_MODEL), jnp.float32), 'v': jax.random.normal(ks[2], (B, S, D_MODEL), jnp.float32), 'w_q': jax.random.normal(ks[3], (D_MODEL, D_MODEL), jnp.float32) * s, 'b_q': jnp.zeros((D_MODEL,), jnp.float32), 'w_k': jax.random.normal(ks[4], (D_MODEL, D_MODEL), jnp.float32) * s, 'b_k': jnp.zeros((D_MODEL,), jnp.float32), 'w_v': jax.random.normal(ks[5], (D_MODEL, D_MODEL), jnp.float32) * s, 'b_v': jnp.zeros((D_MODEL,), jnp.float32), 'w_o': jax.random.normal(ks[6], (D_MODEL, D_MODEL), jnp.float32) * s, 'b_o': jnp.zeros((D_MODEL,), jnp.float32)}
    _L1_xattn_all = _L1_xattn_setup()
    _L1_xattn_in = {k: v for k, v in _L1_xattn_all.items() if k in ('w_q', 'b_q', 'w_k', 'b_k', 'w_v', 'b_v', 'w_o', 'b_o')}
    del _L1_xattn_all

    def _L1_ffn_setup():
        import jax, jax.numpy as jnp
        import numpy as np
        E = 8
        H = 256
        D = 256
        TOP_K = 2
        key = jax.random.key(seed)
        k0, k1, k2, k3 = jax.random.split(key, 4)
        x = jax.random.normal(k0, (1, 512, H), dtype=jnp.float32)
        router_w = jax.random.normal(k1, (E, H), dtype=jnp.float32) * (1.0 / np.sqrt(H))
        up_proj = jax.random.normal(k2, (E, H, 2 * D), dtype=jnp.float32) * (1.0 / np.sqrt(H))
        down_proj = jax.random.normal(k3, (E, D, H), dtype=jnp.float32) * (1.0 / np.sqrt(D))
        return {'x': x, 'router_w': router_w, 'up_proj': up_proj, 'down_proj': down_proj}
    _L1_ffn_all = _L1_ffn_setup()
    _L1_ffn_in = {k: v for k, v in _L1_ffn_all.items() if k in ('router_w', 'up_proj', 'down_proj')}
    del _L1_ffn_all

    def _L2_xattn_setup():
        import jax, jax.numpy as jnp
        import numpy as np
        EMBED_DIM = 256
        NUM_HEADS = 16
        HEAD_DIM = EMBED_DIM // NUM_HEADS
        key = jax.random.key(seed)
        ks = jax.random.split(key, 8)
        B, S, D = (4, 512, EMBED_DIM)
        scale = 1.0 / np.sqrt(D)
        return {'values': jax.random.normal(ks[0], (B, S, D), jnp.float32), 'keys': jax.random.normal(ks[1], (B, S, D), jnp.float32), 'query': jax.random.normal(ks[2], (B, S, D), jnp.float32), 'Wv': jax.random.normal(ks[3], (D, D), jnp.float32) * scale, 'Wk': jax.random.normal(ks[4], (D, D), jnp.float32) * scale, 'Wq': jax.random.normal(ks[5], (D, D), jnp.float32) * scale, 'Wo': jax.random.normal(ks[6], (D, D), jnp.float32) * scale, 'bo': jnp.zeros((D,), jnp.float32)}
    _L2_xattn_all = _L2_xattn_setup()
    _L2_xattn_in = {k: v for k, v in _L2_xattn_all.items() if k in ('Wv', 'Wk', 'Wq', 'Wo', 'bo')}
    del _L2_xattn_all

    def _L2_ffn_setup():
        import jax, jax.numpy as jnp
        import numpy as np
        EPS = 1e-09
        key = jax.random.key(seed)
        k0, k1, k2, k3 = jax.random.split(key, 4)
        B, S, H, F, E = (4, 512, 256, 512, 8)
        return {'hidden_states': jax.random.normal(k0, (B, S, H), dtype=jnp.float32), 'router_w': jax.random.normal(k1, (H, E), dtype=jnp.float32) * 0.02, 'w1': jax.random.normal(k2, (E, H, F), dtype=jnp.float32) * 0.02, 'w2': jax.random.normal(k3, (E, F, H), dtype=jnp.float32) * 0.02}
    _L2_ffn_all = _L2_ffn_setup()
    _L2_ffn_in = {k: v for k, v in _L2_ffn_all.items() if k in ('router_w', 'w1', 'w2')}
    del _L2_ffn_all

    def _L3_xattn_setup():
        import jax, jax.numpy as jnp
        import numpy as np
        B, S, DIM, NH = (64, 64, 256, 8)
        DH = DIM // NH
        EPS = 1e-06
        LN_EPS = 1e-05

        def _make_hops(n):
            hops = np.zeros((n, n), dtype=np.int64)
            cur = 1
            for i in range(n):
                for j in range(i + 1, n):
                    hops[i, j] = cur
                    hops[j, i] = cur
                    cur += 1
            return (hops, cur)

        def _mlstm_forward(q, k, v, igate_w, igate_b, fgate_w, fgate_b, rpe, ln_w, ln_b, hops):
            Bq, Sq, _ = q.shape
            pos_emb = rpe[hops]
            gate_in = jnp.concatenate([q, k, v], axis=-1)
            ig = gate_in @ igate_w.T + igate_b
            fg = gate_in @ fgate_w.T + fgate_b
            ig = jnp.transpose(ig, (0, 2, 1))
            fg = jnp.transpose(fg, (0, 2, 1))
            qh = q.reshape(Bq, Sq, NH, DH).transpose(0, 2, 1, 3)
            kh = k.reshape(Bq, Sq, NH, DH).transpose(0, 2, 1, 3)
            vh = v.reshape(Bq, Sq, NH, DH).transpose(0, 2, 1, 3)
            log_f = jax.nn.log_sigmoid(fg)
            csum = jnp.cumsum(log_f, axis=-1)
            csum = jnp.concatenate([jnp.zeros((Bq, NH, 1), csum.dtype), csum], axis=-1)
            lfm = csum[:, :, :, None] - csum[:, :, None, :]
            ltr = jnp.tril(jnp.ones((Sq, Sq), dtype=bool))
            log_fg_matrix = jnp.where(ltr, lfm[:, :, 1:, 1:], -jnp.inf)
            log_D = log_fg_matrix + ig[:, :, None, :]
            max_log_D = jnp.max(log_D, axis=-1, keepdims=True)
            D = jnp.exp(log_D - max_log_D)
            k_scaled = kh / np.sqrt(DH).astype(np.float32)
            pe = pos_emb.reshape(Sq, Sq, NH, DH)
            k_hop = jnp.einsum('bhvc,vmhc->bhvm', qh, pe)
            qk = jnp.einsum('bhsd,bhtd->bhst', qh, k_scaled)
            C = (qk + k_hop) * D
            normalizer = jnp.maximum(jnp.abs(jnp.sum(C, axis=-1, keepdims=True)), jnp.exp(-max_log_D))
            Cn = C / (normalizer + EPS)
            h = Cn @ vh
            mu = jnp.mean(h, axis=-1, keepdims=True)
            var = jnp.mean(jnp.square(h - mu), axis=-1, keepdims=True)
            hn = (h - mu) / jnp.sqrt(var + LN_EPS)
            w = (1.0 + ln_w).reshape(NH, DH)
            b = ln_b.reshape(NH, DH)
            hn = hn * w[None, :, None, :] + b[None, :, None, :]
            return hn.transpose(0, 2, 1, 3).reshape(Bq, Sq, DIM)
        key = jax.random.key(seed)
        ks = jax.random.split(key, 8)
        hops_np, curnum = _make_hops(S)
        return {'q': jax.random.normal(ks[0], (B, S, DIM), dtype=jnp.float32), 'k': jax.random.normal(ks[1], (B, S, DIM), dtype=jnp.float32), 'v': jax.random.normal(ks[2], (B, S, DIM), dtype=jnp.float32), 'igate_w': jax.random.normal(ks[3], (NH, 3 * DIM), dtype=jnp.float32) * 0.02, 'igate_b': jax.random.normal(ks[4], (NH,), dtype=jnp.float32) * 0.1, 'fgate_w': jax.random.normal(ks[5], (NH, 3 * DIM), dtype=jnp.float32) * 0.02, 'fgate_b': jnp.linspace(3.0, 6.0, NH, dtype=jnp.float32), 'rpe': jax.random.normal(ks[6], (curnum, DIM), dtype=jnp.float32) * 0.02, 'ln_w': jax.random.normal(ks[7], (DIM,), dtype=jnp.float32) * 0.1, 'ln_b': jnp.zeros((DIM,), dtype=jnp.float32), 'hops': jnp.asarray(hops_np)}
    _L3_xattn_all = _L3_xattn_setup()
    _L3_xattn_in = {k: v for k, v in _L3_xattn_all.items() if k in ('igate_w', 'igate_b', 'fgate_w', 'fgate_b', 'rpe', 'ln_w', 'ln_b')}
    del _L3_xattn_all

    def _L3_ffn_setup():
        import jax, jax.numpy as jnp
        import numpy as np
        B, S, D, H, E, K = (4, 256, 256, 512, 8, 2)
        key = jax.random.key(seed)
        ks = jax.random.split(key, 5)
        s = 0.02
        return {'x': jax.random.normal(ks[0], (B, S, D), jnp.float32), 'W1': jax.random.normal(ks[1], (E, H, D), jnp.float32) * s, 'b1': jnp.zeros((E, H), jnp.float32), 'W2': jax.random.normal(ks[2], (E, D, H), jnp.float32) * s, 'b2': jnp.zeros((E, D), jnp.float32), 'Wg': jax.random.normal(ks[3], (E, D), jnp.float32) * s, 'bg': jnp.zeros((E,), jnp.float32)}
    _L3_ffn_all = _L3_ffn_setup()
    _L3_ffn_in = {k: v for k, v in _L3_ffn_all.items() if k in ('W1', 'b1', 'W2', 'b2', 'Wg', 'bg')}
    del _L3_ffn_all
    return {'x': x, 'ctx_1024': ctx_1024, 'itok_SxS2_0_2016': itok_SxS2_0_2016, 'g_xattn': g_xattn, 'g_ffn': g_ffn, 'L0_xattn_igate_w': _L0_xattn_in['igate_w'], 'L0_xattn_igate_b': _L0_xattn_in['igate_b'], 'L0_xattn_fgate_w': _L0_xattn_in['fgate_w'], 'L0_xattn_fgate_b': _L0_xattn_in['fgate_b'], 'L0_xattn_out_w': _L0_xattn_in['out_w'], 'L0_ffn_Wg': _L0_ffn_in['Wg'], 'L0_ffn_We': _L0_ffn_in['We'], 'L0_ffn_be': _L0_ffn_in['be'], 'L1_xattn_w_q': _L1_xattn_in['w_q'], 'L1_xattn_b_q': _L1_xattn_in['b_q'], 'L1_xattn_w_k': _L1_xattn_in['w_k'], 'L1_xattn_b_k': _L1_xattn_in['b_k'], 'L1_xattn_w_v': _L1_xattn_in['w_v'], 'L1_xattn_b_v': _L1_xattn_in['b_v'], 'L1_xattn_w_o': _L1_xattn_in['w_o'], 'L1_xattn_b_o': _L1_xattn_in['b_o'], 'L1_ffn_router_w': _L1_ffn_in['router_w'], 'L1_ffn_up_proj': _L1_ffn_in['up_proj'], 'L1_ffn_down_proj': _L1_ffn_in['down_proj'], 'L2_xattn_Wv': _L2_xattn_in['Wv'], 'L2_xattn_Wk': _L2_xattn_in['Wk'], 'L2_xattn_Wq': _L2_xattn_in['Wq'], 'L2_xattn_Wo': _L2_xattn_in['Wo'], 'L2_xattn_bo': _L2_xattn_in['bo'], 'L2_ffn_router_w': _L2_ffn_in['router_w'], 'L2_ffn_w1': _L2_ffn_in['w1'], 'L2_ffn_w2': _L2_ffn_in['w2'], 'L3_xattn_igate_w': _L3_xattn_in['igate_w'], 'L3_xattn_igate_b': _L3_xattn_in['igate_b'], 'L3_xattn_fgate_w': _L3_xattn_in['fgate_w'], 'L3_xattn_fgate_b': _L3_xattn_in['fgate_b'], 'L3_xattn_rpe': _L3_xattn_in['rpe'], 'L3_xattn_ln_w': _L3_xattn_in['ln_w'], 'L3_xattn_ln_b': _L3_xattn_in['ln_b'], 'L3_ffn_W1': _L3_ffn_in['W1'], 'L3_ffn_b1': _L3_ffn_in['b1'], 'L3_ffn_W2': _L3_ffn_in['W2'], 'L3_ffn_b2': _L3_ffn_in['b2'], 'L3_ffn_Wg': _L3_ffn_in['Wg'], 'L3_ffn_bg': _L3_ffn_in['bg']}

def reference(x, ctx_1024, itok_SxS2_0_2016, g_xattn, g_ffn, L0_xattn_igate_w, L0_xattn_igate_b, L0_xattn_fgate_w, L0_xattn_fgate_b, L0_xattn_out_w, L0_ffn_Wg, L0_ffn_We, L0_ffn_be, L1_xattn_w_q, L1_xattn_b_q, L1_xattn_w_k, L1_xattn_b_k, L1_xattn_w_v, L1_xattn_b_v, L1_xattn_w_o, L1_xattn_b_o, L1_ffn_router_w, L1_ffn_up_proj, L1_ffn_down_proj, L2_xattn_Wv, L2_xattn_Wk, L2_xattn_Wq, L2_xattn_Wo, L2_xattn_bo, L2_ffn_router_w, L2_ffn_w1, L2_ffn_w2, L3_xattn_igate_w, L3_xattn_igate_b, L3_xattn_fgate_w, L3_xattn_fgate_b, L3_xattn_rpe, L3_xattn_ln_w, L3_xattn_ln_b, L3_ffn_W1, L3_ffn_b1, L3_ffn_W2, L3_ffn_b2, L3_ffn_Wg, L3_ffn_bg):
    import jax
    import jax.numpy as jnp

    def _L0_xattn_ref(q, k, v, igate_w, igate_b, fgate_w, fgate_b, out_w):
        import jax, jax.numpy as jnp
        import numpy as np
        import math
        EPS = 1e-08
        LN_EPS = 1e-05
        B, S, E, NH = (2, 512, 256, 4)
        DH = E // NH

        def _mlstm_cell(q, k, v, igate_w, igate_b, fgate_w, fgate_b, out_w):
            Bq, Sq, Eq = q.shape
            if_in = jnp.concatenate([q, k, v], axis=-1)
            ig = jnp.einsum('bsf,hf->bsh', if_in, igate_w) + igate_b
            fg = jnp.einsum('bsf,hf->bsh', if_in, fgate_w) + fgate_b
            ig = jnp.transpose(ig, (0, 2, 1))[..., None]
            fg = jnp.transpose(fg, (0, 2, 1))[..., None]
            qh = q.reshape(Bq, Sq, NH, DH).transpose(0, 2, 1, 3)
            kh = k.reshape(Bq, Sq, NH, DH).transpose(0, 2, 1, 3)
            vh = v.reshape(Bq, Sq, NH, DH).transpose(0, 2, 1, 3)
            log_fg = jax.nn.log_sigmoid(fg)
            cs = jnp.cumsum(log_fg, axis=2)
            cs_shift = jnp.concatenate([jnp.zeros_like(cs[:, :, :1]), cs[:, :, :-1]], axis=2)
            logfg_mat = cs - jnp.swapaxes(cs_shift, -2, -1)
            ltr = jnp.tril(jnp.ones((Sq, Sq), dtype=bool))
            logfg_mat = jnp.where(ltr, logfg_mat, -jnp.inf)
            log_D = logfg_mat + jnp.swapaxes(ig, -2, -1)
            max_log_D = jnp.max(log_D, axis=-1, keepdims=True)
            D = jnp.exp(log_D - max_log_D)
            qk = jnp.einsum('bhsd,bhtd->bhst', qh, kh / math.sqrt(DH))
            C = qk * D
            sum_C_abs = jnp.abs(jnp.sum(C, axis=-1, keepdims=True))
            normaliser = jnp.maximum(sum_C_abs, jnp.exp(-max_log_D))
            C_norm = C / (normaliser + EPS)
            h = jnp.einsum('bhst,bhtd->bhsd', C_norm, vh)
            mean = jnp.mean(h, axis=-1, keepdims=True)
            var = jnp.mean((h - mean) ** 2, axis=-1, keepdims=True)
            h_norm = (h - mean) / jnp.sqrt(var + LN_EPS)
            scale = (1.0 + out_w).reshape(1, NH, 1, DH)
            h_norm = h_norm * scale
            return h_norm.transpose(0, 2, 1, 3).reshape(Bq, Sq, Eq)
        return _mlstm_cell(q, k, v, igate_w, igate_b, fgate_w, fgate_b, out_w)

    def _L0_ffn_ref(x, Wg, We, be):
        import jax, jax.numpy as jnp
        import numpy as np
        B, S, D = x.shape
        E = Wg.shape[1]
        T = B * S
        xf = x.reshape(T, D)
        gates = jax.nn.softmax(xf @ Wg, axis=-1)
        top_g, top_i = jax.lax.top_k(gates, 2)
        top_g = top_g / jnp.sum(top_g, axis=-1, keepdims=True)
        tok = jnp.arange(T)
        dispatch = jnp.zeros((E, T), dtype=gates.dtype)
        for i in range(2):
            dispatch = dispatch.at[top_i[:, i], tok].add(top_g[:, i])
        y = jnp.einsum('td,edh->eth', xf, We) + be[:, None, :]
        out = jnp.einsum('et,eth->th', dispatch, y)
        return out.reshape(B, S, -1)

    def _L1_xattn_ref(q, k, v, w_q, b_q, w_k, b_k, w_v, b_v, w_o, b_o):
        import jax, jax.numpy as jnp
        import numpy as np
        D_MODEL = 256
        H = 16
        D_K = D_MODEL // H
        B = 4
        S = 512
        Bq, Sq, _ = q.shape
        query = q @ w_q.T + b_q
        key_ = k @ w_k.T + b_k
        value = v @ w_v.T + b_v
        query = query.reshape(Bq, Sq, H, D_K).transpose(0, 2, 1, 3)
        key_ = key_.reshape(Bq, Sq, H, D_K).transpose(0, 2, 1, 3)
        value = value.reshape(Bq, Sq, H, D_K).transpose(0, 2, 1, 3)
        scale = 1.0 / jnp.sqrt(jnp.asarray(D_K, query.dtype))
        scores = jnp.einsum('bhqd,bhkd->bhqk', query, key_) * scale
        causal = jnp.tril(jnp.ones((Sq, Sq), bool))
        scores = jnp.where(causal[None, None], scores, -jnp.inf)
        attn = jax.nn.softmax(scores, axis=-1)
        x = jnp.einsum('bhqk,bhkd->bhqd', attn, value)
        x = x.transpose(0, 2, 1, 3).reshape(Bq, Sq, H * D_K)
        return x @ w_o.T + b_o

    def _L1_ffn_ref(x, router_w, up_proj, down_proj):
        import jax, jax.numpy as jnp
        import numpy as np
        E = 8
        H = 256
        D = 256
        TOP_K = 2
        B, T, _ = x.shape
        xt = x.reshape(-1, H)
        N = xt.shape[0]
        logits = jnp.einsum('nh,eh->ne', xt, router_w)
        probs = jax.nn.softmax(logits, axis=-1)
        scores, expert_idx = jax.lax.top_k(probs, TOP_K)
        scores = scores / jnp.sum(scores, axis=-1, keepdims=True)
        gate = jnp.zeros((N, E), dtype=xt.dtype).at[jnp.arange(N)[:, None], expert_idx].add(scores)
        h = jnp.einsum('nh,ehd->end', xt, up_proj)
        hidden = jax.nn.silu(h[..., :D]) * h[..., D:]
        out_e = jnp.einsum('end,edh->enh', hidden, down_proj)
        out = jnp.einsum('ne,enh->nh', gate, out_e)
        return out.reshape(B, T, H)

    def _L2_xattn_ref(values, keys, query, Wv, Wk, Wq, Wo, bo):
        import jax, jax.numpy as jnp
        import numpy as np
        EMBED_DIM = 256
        NUM_HEADS = 16
        HEAD_DIM = EMBED_DIM // NUM_HEADS
        N = query.shape[0]
        H, Dh = (NUM_HEADS, HEAD_DIM)
        v = (values @ Wv.T).reshape(N, -1, H, Dh)
        k = (keys @ Wk.T).reshape(N, -1, H, Dh)
        q = (query @ Wq.T).reshape(N, -1, H, Dh)
        energy = jnp.einsum('nqhd,nkhd->nhqk', q, k)
        attn = jax.nn.softmax(energy / jnp.sqrt(jnp.float32(EMBED_DIM)), axis=3)
        out = jnp.einsum('nhql,nlhd->nqhd', attn, v).reshape(N, -1, H * Dh)
        return out @ Wo.T + bo

    def _L2_ffn_ref(hidden_states, router_w, w1, w2):
        import jax, jax.numpy as jnp
        import numpy as np
        EPS = 1e-09
        TOP_K = 2
        orig_shape = hidden_states.shape
        H = orig_shape[-1]
        E = router_w.shape[-1]
        flat = hidden_states.reshape(-1, H)
        T = flat.shape[0]
        gate_logits = flat @ router_w
        gate_probs = jax.nn.softmax(gate_logits, axis=-1)
        topk_w, topk_idx = jax.lax.top_k(gate_probs, TOP_K)
        topk_w = topk_w / jnp.clip(topk_w.sum(-1, keepdims=True), EPS)
        cw = jnp.zeros((T, E), dtype=flat.dtype).at[jnp.arange(T)[:, None], topk_idx].add(topk_w)
        h = jax.nn.silu(jnp.einsum('td,edf->etf', flat, w1))
        y = jnp.einsum('etf,efd->etd', h, w2)
        out = jnp.einsum('etd,te->td', y, cw)
        return out.reshape(orig_shape)

    def _L3_xattn_ref(q, k, v, igate_w, igate_b, fgate_w, fgate_b, rpe, ln_w, ln_b, hops):
        import jax, jax.numpy as jnp
        import numpy as np
        B, S, DIM, NH = (64, 64, 256, 8)
        DH = DIM // NH
        EPS = 1e-06
        LN_EPS = 1e-05

        def _make_hops(n):
            hops = np.zeros((n, n), dtype=np.int64)
            cur = 1
            for i in range(n):
                for j in range(i + 1, n):
                    hops[i, j] = cur
                    hops[j, i] = cur
                    cur += 1
            return (hops, cur)

        def _mlstm_forward(q, k, v, igate_w, igate_b, fgate_w, fgate_b, rpe, ln_w, ln_b, hops):
            Bq, Sq, _ = q.shape
            pos_emb = rpe[hops]
            gate_in = jnp.concatenate([q, k, v], axis=-1)
            ig = gate_in @ igate_w.T + igate_b
            fg = gate_in @ fgate_w.T + fgate_b
            ig = jnp.transpose(ig, (0, 2, 1))
            fg = jnp.transpose(fg, (0, 2, 1))
            qh = q.reshape(Bq, Sq, NH, DH).transpose(0, 2, 1, 3)
            kh = k.reshape(Bq, Sq, NH, DH).transpose(0, 2, 1, 3)
            vh = v.reshape(Bq, Sq, NH, DH).transpose(0, 2, 1, 3)
            log_f = jax.nn.log_sigmoid(fg)
            csum = jnp.cumsum(log_f, axis=-1)
            csum = jnp.concatenate([jnp.zeros((Bq, NH, 1), csum.dtype), csum], axis=-1)
            lfm = csum[:, :, :, None] - csum[:, :, None, :]
            ltr = jnp.tril(jnp.ones((Sq, Sq), dtype=bool))
            log_fg_matrix = jnp.where(ltr, lfm[:, :, 1:, 1:], -jnp.inf)
            log_D = log_fg_matrix + ig[:, :, None, :]
            max_log_D = jnp.max(log_D, axis=-1, keepdims=True)
            D = jnp.exp(log_D - max_log_D)
            k_scaled = kh / np.sqrt(DH).astype(np.float32)
            pe = pos_emb.reshape(Sq, Sq, NH, DH)
            k_hop = jnp.einsum('bhvc,vmhc->bhvm', qh, pe)
            qk = jnp.einsum('bhsd,bhtd->bhst', qh, k_scaled)
            C = (qk + k_hop) * D
            normalizer = jnp.maximum(jnp.abs(jnp.sum(C, axis=-1, keepdims=True)), jnp.exp(-max_log_D))
            Cn = C / (normalizer + EPS)
            h = Cn @ vh
            mu = jnp.mean(h, axis=-1, keepdims=True)
            var = jnp.mean(jnp.square(h - mu), axis=-1, keepdims=True)
            hn = (h - mu) / jnp.sqrt(var + LN_EPS)
            w = (1.0 + ln_w).reshape(NH, DH)
            b = ln_b.reshape(NH, DH)
            hn = hn * w[None, :, None, :] + b[None, :, None, :]
            return hn.transpose(0, 2, 1, 3).reshape(Bq, Sq, DIM)
        return _mlstm_forward(q, k, v, igate_w, igate_b, fgate_w, fgate_b, rpe, ln_w, ln_b, hops)

    def _L3_ffn_ref(x, W1, b1, W2, b2, Wg, bg):
        import jax, jax.numpy as jnp
        import numpy as np
        B, S, D, H, E, K = (4, 256, 256, 512, 8, 2)
        b, s, d = x.shape
        xt = x.reshape(-1, d)
        gate_logits = xt @ Wg.T + bg
        w, idx = jax.lax.top_k(gate_logits, K)
        w = jax.nn.softmax(w, axis=1)
        h = jax.nn.relu(jnp.einsum('td,ehd->eth', xt, W1) + b1[:, None, :])
        y = jnp.einsum('eth,eoh->eto', h, W2) + b2[:, None, :]
        comb = (jax.nn.one_hot(idx, E, dtype=xt.dtype) * w[..., None]).sum(axis=1)
        out = jnp.einsum('eto,te->to', y, comb)
        return out.reshape(b, s, d)
    x = x + jnp.tanh(g_xattn[0]) * _L0_xattn_ref(_layernorm(x, axis=-1), ctx_1024, ctx_1024, L0_xattn_igate_w, L0_xattn_igate_b, L0_xattn_fgate_w, L0_xattn_fgate_b, L0_xattn_out_w)
    x = x + jnp.tanh(g_ffn[0]) * _L0_ffn_ref(_layernorm(x, axis=-1), L0_ffn_Wg, L0_ffn_We, L0_ffn_be)
    x = x + jnp.tanh(g_xattn[1]) * _L1_xattn_ref(_layernorm(x, axis=-1), ctx_1024, ctx_1024, L1_xattn_w_q, L1_xattn_b_q, L1_xattn_w_k, L1_xattn_b_k, L1_xattn_w_v, L1_xattn_b_v, L1_xattn_w_o, L1_xattn_b_o)
    x = x + jnp.tanh(g_ffn[1]) * _L1_ffn_ref(_layernorm(x, axis=-1), L1_ffn_router_w, L1_ffn_up_proj, L1_ffn_down_proj)
    x = x + jnp.tanh(g_xattn[2]) * _L2_xattn_ref(ctx_1024, ctx_1024, _layernorm(x, axis=-1), L2_xattn_Wv, L2_xattn_Wk, L2_xattn_Wq, L2_xattn_Wo, L2_xattn_bo)
    x = x + jnp.tanh(g_ffn[2]) * _L2_ffn_ref(_layernorm(x, axis=-1), L2_ffn_router_w, L2_ffn_w1, L2_ffn_w2)
    x = x + jnp.tanh(g_xattn[3]) * _L3_xattn_ref(_layernorm(x, axis=-1), ctx_1024, ctx_1024, L3_xattn_igate_w, L3_xattn_igate_b, L3_xattn_fgate_w, L3_xattn_fgate_b, L3_xattn_rpe, L3_xattn_ln_w, L3_xattn_ln_b, itok_SxS2_0_2016)
    x = x + jnp.tanh(g_ffn[3]) * _L3_ffn_ref(_layernorm(x, axis=-1), L3_ffn_W1, L3_ffn_b1, L3_ffn_W2, L3_ffn_b2, L3_ffn_Wg, L3_ffn_bg)
    return x

_drawn_inputs = setup_inputs


def setup_inputs(seed=0):
    import zlib

    import numpy as np

    out = dict(_drawn_inputs(seed))
    spreads = {'L0_xattn_out_w': (0.0, 0.1),
     'L0_ffn_be': (0.0, 0.1),
     'L1_xattn_b_q': (0.0, 0.307),
     'L1_xattn_b_k': (0.0, 2.0),
     'L1_xattn_b_v': (0.0, 0.1),
     'L1_xattn_b_o': (0.0, 0.1),
     'L2_xattn_bo': (0.0, 0.1),
     'L3_xattn_ln_b': (0.0, 0.1),
     'L3_ffn_b1': (0.0, 0.596),
     'L3_ffn_b2': (0.0, 0.1),
     'L3_ffn_bg': (0.0, 0.1)}
    factors = {'g_ffn': 36.248, 'L0_xattn_igate_b': 64.0, 'L3_xattn_igate_b': 64.0, 'L3_xattn_rpe': 3.324}
    for name, (base, spread) in spreads.items():
        noise = np.random.default_rng([zlib.crc32(name.encode()), seed]).standard_normal(out[name].shape)
        drawn = base * np.exp(spread * noise) if base else spread * noise
        out[name] = jnp.asarray(drawn.astype(out[name].dtype))
    for name, factor in factors.items():
        out[name] = (out[name] * factor).astype(out[name].dtype)
    return out
```

```python
from contextlib import ExitStack, contextmanager

import concourse.bass as bass
from concourse import mybir

F32 = mybir.dt.float32
BF16 = mybir.dt.bfloat16
I32 = mybir.dt.int32
ALU = mybir.AluOpType
ACT = mybir.ActivationFunctionType
AX = mybir.AxisListType

P = 128
B, S, D = 8, 256, 256
T = B * S
NT = T // P
HALVES = S // P
KC = D // P
E = 8
LN_EPS = 1e-5
BIG = 1e30

SUBLAYERS = (0, 1, 2, 3, 4, 5, 6, 7)


def ds(start, size):
    return bass.ds(start, size)


class Chain:

    def __init__(self, eng, sem):
        self.eng, self.sem, self.base, self.n = eng, sem, 0, 0

    def start(self, base=0):
        self.base, self.n = base, 0

    def link(self, ins):
        self.n += 1
        ins.then_inc(self.sem, 1)
        self.eng.wait_ge(self.sem, self.base + self.n)


def wait_apart(eng, sem, value, passed):
    eng.wait_ge(sem, value)
    eng.sem_inc(passed, 1)


class Stage:

    def __init__(self, k):
        self.k, self.sems = k, []

    def sem(self, name):
        s = self.k.shared_sem(f"{type(self).__name__}_{name}")
        self.sems.append(s)
        return s

    def tensor(self, pe):
        pass

    def vector(self, dve):
        pass

    def scalar(self, act):
        pass

    def gpsimd(self, pool):
        pass

    def sync(self, sp):
        pass


class LayerNorm(Stage):

    GROUP = 4
    PAIRS = NT // GROUP // 2

    def __init__(self, k, tag):
        super().__init__(k)
        self.stats_done = self.sem("stats_done")
        self.own = self.sem("chain")
        self.inv_ready = self.sem("inv_ready")
        self.rstd_ready = self.sem("rstd_ready")
        self.normed = self.sem("normed")
        self.transposed = self.sem("transposed")
        self.copied0 = self.sem("copied0")
        self.copied1 = self.sem("copied1")

    def vector(self, dve):
        k, G = self.k, self.GROUP
        chain = Chain(dve, self.own)
        with dve.Fori(0, NT // G) as i:
            for j in range(G):
                dve.bn_stats(k.ln_stats[:, ds(i * G * 6 + j * 6, 6)],
                             k.x[:, ds(i * G * D + j * D, D)]).then_inc(self.stats_done, 1)
        dve.wait_ge(self.stats_done, NT)
        for t in range(NT):
            ins = dve.bn_aggr(k.ln_mv[:, t, :], k.ln_stats[:, t * 6:(t + 1) * 6])
        chain.link(ins)
        chain.link(dve.tensor_scalar(k.ln_inv[:], k.ln_mv[:, :, 1], LN_EPS, None, ALU.add))
        dve.reciprocal(k.ln_inv[:], k.ln_inv[:]).then_inc(self.inv_ready, 1)
        chain.link(dve.tensor_copy(k.ln_mean[:], k.ln_mv[:, :, 0]))
        dve.sem_inc(self.copied1, 1)
        dve.wait_ge(self.rstd_ready, 1)
        with dve.Fori(0, self.PAIRS) as i:
            for u in range(2):
                g = i * 2 + u
                for j in range(G):
                    if j == 0:
                        dve.wait_ge(self.transposed, i * 2 + 1)
                    ins = dve.tensor_scalar(k.ln_x[u][:, j, :], k.x[:, ds(g * G * D + j * D, D)],
                                            k.ln_mean[:, ds(g * G + j, 1)], k.ln_rstd[:, ds(g * G + j, 1)],
                                            ALU.subtract, ALU.mult)
                ins.then_inc(self.normed, 1)
            for u in range(2):
                g = i * 2 + u
                dve.wait_ge(self.transposed, g + 2)
                dve.tensor_copy(k.lnT[:, ds(g * G * P + T, G * P)], k.bank[2 * u + 1][:]).then_inc(self.copied1, 1)

    def scalar(self, act):
        k, G = self.k, self.GROUP
        act.wait_ge(self.inv_ready, 1)
        act.activation(k.ln_rstd[:], k.ln_inv[:], ACT.Sqrt).then_inc(self.rstd_ready, 1)
        act.sem_inc(self.copied0, 1)
        with act.Fori(0, self.PAIRS) as i:
            for u in range(2):
                g = i * 2 + u
                act.wait_ge(self.transposed, g + 2)
                act.copy(k.lnT[:, ds(g * G * P, G * P)], k.bank[2 * u][:]).then_inc(self.copied0, 1)

    def tensor(self, pe):
        k, G = self.k, self.GROUP
        pe.sem_inc(self.transposed, 1)
        with pe.Fori(0, self.PAIRS) as i:
            for u in range(2):
                g = i * 2 + u
                pe.wait_ge(self.copied0, i * 2 + 1)
                pe.wait_ge(self.copied1, i * 2 + 1)
                pe.wait_ge(self.normed, g + 1)
                for c in range(KC):
                    for j in range(G):
                        ins = pe.transpose(k.bank[2 * u + c][:, j * P:(j + 1) * P],
                                           k.ln_x[u][:, j, c * P:(c + 1) * P], k.ident[:])
                ins.then_inc(self.transposed, 1)


class Router(Stage):

    def __init__(self, k, tag, wg, g, bias=None):
        super().__init__(k)
        self.wg_dram, self.g, self.bias_dram = wg, g, bias
        self.loaded = self.sem("loaded")
        self.logits_ready = self.sem("logits_ready")
        self.own = self.sem("chain")
        self.diff_ready = self.sem("diff_ready")
        self.exp_ready = self.sem("exp_ready")

    def sync(self, sp):
        k = self.k
        sp.dma_start(k.wg[:], self.wg_dram.rearrange("(c p) e -> p c e", p=P)).then_inc(self.loaded, 16)
        if self.bias_dram is not None:
            sp.dma_start(k.bg[:], self.bias_dram.partition_broadcast(P)).then_inc(self.loaded, 16)

    def tensor(self, pe):
        k = self.k
        pe.wait_ge(self.loaded, 16 * (1 + (self.bias_dram is not None)))
        for t in range(NT):
            for c in range(KC):
                ins = pe.matmul(k.bank[0][:, t * E:(t + 1) * E], k.lnT[:, c * T + t * P:c * T + (t + 1) * P],
                                k.wg[:, c, :], start=c == 0, stop=c == KC - 1)
        ins.then_inc(self.logits_ready, 1)

    def vector(self, dve):
        k = self.k
        full = [P, NT, E]
        over_e = lambda a: a.unsqueeze(2).to_broadcast(full)
        over_t = lambda a: a.unsqueeze(1).to_broadcast(full)
        chain = Chain(dve, self.own)
        logits = k.rt[:, 0]
        eq, key, sel1, sel2 = k.rt[:, 1], k.rt[:, 2], k.rt[:, 3], k.rt[:, 4]
        m1, m2, kmax, diff, w1, w2 = (k.rs[:, n] for n in range(6))
        ps = k.bank[0][:, 0:NT * E].rearrange("p (t e) -> p t e", e=E)
        dve.wait_ge(self.logits_ready, 1)
        if self.bias_dram is not None:
            chain.link(dve.tensor_tensor(logits, ps, over_t(k.bg[:]), ALU.add))
        else:
            chain.link(dve.tensor_copy(logits, ps))
        for m, sel, nxt in ((m1, sel1, key), (m2, sel2, None)):
            left = logits if nxt is not None else k.rt[:, 5]
            chain.link(dve.tensor_reduce(m, left, AX.X, ALU.max))
            chain.link(dve.tensor_tensor(eq, left, over_e(m), ALU.is_equal))
            chain.link(dve.tensor_tensor(key, eq, over_t(k.rank[:]), ALU.mult))
            chain.link(dve.tensor_reduce(kmax, key, AX.X, ALU.max))
            chain.link(dve.tensor_tensor(sel, key, over_e(kmax), ALU.is_equal))
            if nxt is not None:
                chain.link(dve.scalar_tensor_tensor(out=k.rt[:, 5], in0=sel, scalar=-BIG, in1=logits,
                                                    op0=ALU.mult, op1=ALU.add))
        dve.tensor_tensor(diff, m2, m1, ALU.subtract).then_inc(self.diff_ready, 1)
        dve.wait_ge(self.exp_ready, 1)
        chain.link(dve.tensor_scalar(w1, k.rexp[:], 1.0, None, ALU.add))
        chain.link(dve.reciprocal(w1, w1))
        chain.link(dve.tensor_scalar(w1, w1, k.tanh_g[:, self.g:self.g + 1], None, ALU.mult))
        chain.link(dve.tensor_tensor(w2, k.rexp[:], w1, ALU.mult))
        chain.link(dve.tensor_tensor(sel1, sel1, over_e(w1), ALU.mult))
        chain.link(dve.tensor_tensor(sel2, sel2, over_e(w2), ALU.mult))
        chain.link(dve.tensor_tensor(k.gate3, sel1, sel2, ALU.add))

    def scalar(self, act):
        k = self.k
        act.wait_ge(self.diff_ready, 1)
        act.activation(k.rexp[:], k.rs[:, 3], ACT.Exp).then_inc(self.exp_ready, 1)


class GateBias(Stage):

    def __init__(self, k, tag, bias):
        super().__init__(k)
        self.bias_dram = bias
        self.loaded = self.sem("loaded")
        self.turned = self.sem("turned")
        self.gate_ready = self.sem("gate_ready")
        self.y_ready = self.sem("y_ready")
        self.added = self.sem("added")

    def sync(self, sp):
        sp.dma_start(self.k.ebias[:], self.bias_dram).then_inc(self.loaded, 16)

    def tensor(self, pe):
        k = self.k
        for t in range(NT):
            ins = pe.transpose(k.bank[t // 4][0:E, (t % 4) * P:(t % 4 + 1) * P], k.gate[:, t * E:(t + 1) * E], k.ident[:])
        ins.then_inc(self.turned, 1)
        pe.wait_ge(self.gate_ready, 4)
        pe.wait_ge(self.loaded, 16)
        for t in range(NT):
            if t >= 4:
                pe.wait_ge(self.added, t - 3)
            pe.matmul(k.bank[4 + t % 4][:, 0:D], k.gateT[:, t * P:(t + 1) * P], k.ebias[:],
                      start=True, stop=True).then_inc(self.y_ready, 1)

    def vector(self, dve):
        k = self.k
        dve.wait_ge(self.turned, 1)
        for n in range(4):
            dve.tensor_copy(k.gateT[:, n * 4 * P:(n + 1) * 4 * P], k.bank[n][0:E, :]).then_inc(self.gate_ready, 1)
        for t in range(NT):
            dve.wait_ge(self.y_ready, t + 1)
            dve.tensor_tensor(k.x[:, t * D:(t + 1) * D], k.bank[4 + t % 4][:, 0:D], k.x[:, t * D:(t + 1) * D],
                              ALU.add).then_inc(self.added, 1)


class LinearExperts(Stage):

    RING = 8

    def __init__(self, k, tag, we):
        super().__init__(k)
        self.we = we.rearrange("e (c p) h -> e p c h", p=P)
        self.landed = [self.sem(f"landed{u}") for u in range(2)]
        self.used = self.sem("used")
        self.y_ready = self.sem("y_ready")
        self.added = self.sem("added")
        self.col = self.sem("col")

    def sync(self, sp):
        k = self.k
        for u in range(2):
            sp.dma_start(k.up[u][:, :, 0:D], self.we[u]).then_inc(self.landed[u], 16)
        with sp.Fori(1, E // 2) as i:
            for u in range(2):
                sp.wait_ge(self.used, i * 2 + (u - 1))
                sp.dma_start(k.up[u][:, :, 0:D], self.we[ds(i * 2 + u, 1)].rearrange("e p c h -> (e p) c h")).then_inc(self.landed[u], 16)

    def tensor(self, pe):
        k = self.k

        def expert(e, round_, u, first):
            pe.wait_ge(self.landed[u], round_ * 16 + 16)
            for t in range(NT):
                if not (first and t < self.RING):
                    pe.wait_ge(self.added, e * NT + (t - self.RING + 1))
                for c in range(KC):
                    ins = pe.matmul(k.bank[t % self.RING][:, 0:D], k.lnT[:, c * T + t * P:c * T + (t + 1) * P],
                                    k.up[u][:, c, 0:D], start=c == 0, stop=c == KC - 1)
                if t < NT - 1:
                    ins.then_inc(self.y_ready, 1)
            ins.then_inc(self.y_ready, 1)
            pe.wait_ge(self.y_ready, e * NT + NT)
            pe.sem_inc(self.used, 1)

        for u in range(2):
            expert(u, 0, u, u == 0)
        with pe.Fori(1, E // 2) as i:
            for u in range(2):
                expert(i * 2 + u, i, u, False)

    def vector(self, dve):
        k = self.k
        with dve.Fori(0, E // 2) as i:
            for u in range(2):
                e = i * 2 + u
                dve.tensor_copy(k.gcol[u][:].unsqueeze(2), k.gate3[:, :, ds(e, 1)]).then_inc(self.col, 1)
                dve.wait_ge(self.col, e + 1)
                for t in range(NT):
                    dve.wait_ge(self.y_ready, e * NT + (t + 1))
                    dve.scalar_tensor_tensor(out=k.x[:, t * D:(t + 1) * D], in0=k.bank[t % self.RING][:, 0:D],
                                             scalar=k.gcol[u][:, t:t + 1], in1=k.x[:, t * D:(t + 1) * D],
                                             op0=ALU.mult, op1=ALU.add).then_inc(self.added, 1)


class Experts(Stage):

    GT = 512
    NG = T // GT
    TG = GT // P

    def __init__(self, k, tag, kind, up, down, b1=None):
        super().__init__(k)
        self.kind = kind
        self.up = up.rearrange("e (c p) f -> e p c f", p=P)
        self.down = down.rearrange("e (c p) h -> e p c h", p=P)
        self.b1 = b1
        self.UF = up.shape[2] // P
        self.HF = down.shape[1] // P
        self.loads = 3 if b1 is not None else 2
        self.landed = [self.sem(f"landed{u}") for u in range(2)]
        self.used = self.sem("used")
        self.up_ready = self.sem("up_ready")
        self.silu_ready = self.sem("silu_ready")
        self.hid_ready = self.sem("hid_ready")
        self.y_ready = self.sem("y_ready")
        self.added = self.sem("added")
        self.col = self.sem("col")
        self.PER = self.NG * self.UF
        self.HPER = self.NG * self.HF

    def load(self, sp, u, e):
        k = self.k
        at = lambda a: a[e] if isinstance(e, int) else a[ds(e, 1)].rearrange(
            "e p c f -> (e p) c f" if len(a.shape) == 4 else "e p c -> (e p) c")
        sp.dma_start(k.up[u][:, :, 0:self.UF * P], at(self.up)).then_inc(self.landed[u], 16)
        sp.dma_start(k.down[u][:, 0:self.HF, :], at(self.down)).then_inc(self.landed[u], 16)
        if self.b1 is not None:
            sp.dma_start(k.b1[u][:], at(self.b1)).then_inc(self.landed[u], 16)

    def sync(self, sp):
        for u in range(2):
            self.load(sp, u, u)
        with sp.Fori(1, E // 2) as i:
            for u in range(2):
                sp.wait_ge(self.used, i * 2 + (u - 1))
                self.load(sp, u, i * 2 + u)

    def up_free(self, eng, e, n, first):
        if first and n < 4:
            return
        if self.kind == "glu":
            eng.wait_ge(self.hid_ready, e * self.HPER + (n // 4) * 2)
        else:
            eng.wait_ge(self.hid_ready, e * self.HPER + (n - 3))

    def tensor(self, pe):
        k = self.k

        def ups(e, u, g, first):
            for f in range(self.UF):
                n = g * self.UF + f
                if self.kind != "glu" or f == 0:
                    self.up_free(pe, e, n, first)
                for c in range(KC):
                    ins = pe.matmul(k.bank[f][:], k.up[u][:, c, f * P:(f + 1) * P],
                                    k.lnT[:, c * T + g * self.GT:c * T + (g + 1) * self.GT],
                                    start=c == 0, stop=c == KC - 1)
                ins.then_inc(self.up_ready, 1)

        def downs(e, u, g, first):
            pe.wait_ge(self.hid_ready, e * self.HPER + (g + 1) * self.HF)
            for j in range(self.TG):
                n = g * self.TG + j
                if not (first and n < 4):
                    pe.wait_ge(self.added, e * NT + (n - 3))
                for f in range(self.HF):
                    ins = pe.matmul(k.bank[4 + j][:, 0:D], k.hid[g % 2][:, f, j * P:(j + 1) * P],
                                    k.down[u][:, f, :], start=f == 0, stop=f == self.HF - 1)
                ins.then_inc(self.y_ready, 1)

        def pair(e0, round_, first):
            steps = [(u, g) for u in range(2) for g in range(self.NG)]
            for n in range(len(steps) + 1):
                if n < len(steps):
                    u, g = steps[n]
                    if g == 0:
                        pe.wait_ge(self.landed[u], round_ * (16 * self.loads) + 16 * self.loads)
                    ups(e0 + u, u, g, first and u == 0)
                if n >= 1:
                    u, g = steps[n - 1]
                    downs(e0 + u, u, g, first and u == 0)
                    if g == self.NG - 1:
                        pe.wait_ge(self.y_ready, (e0 + u) * NT + NT)
                        pe.sem_inc(self.used, 1)

        pair(0, 0, True)
        with pe.Fori(1, E // 2) as i:
            pair(i * 2, i, False)

    def scalar(self, act):
        k = self.k

        def expert(e, u, first):
            for g in range(self.NG):
                for f in range(self.HF):
                    n = g * self.UF + f
                    hid = k.hid[g % 2][:, f, :]
                    act.wait_ge(self.up_ready, e * self.PER + (n + 1))
                    if self.kind == "glu":
                        if not (first and g == 0):
                            act.wait_ge(self.hid_ready, e * self.HPER + ((g - 1) * self.HF + f + 1))
                        act.activation(k.glu_s[f][:], k.bank[f][:], ACT.Silu).then_inc(self.silu_ready, 1)
                        continue
                    if not (first and g < 2) and f == 0:
                        act.wait_ge(self.y_ready, e * NT + (g - 1) * self.TG)
                    if self.kind == "silu":
                        act.activation(hid, k.bank[f][:], ACT.Silu).then_inc(self.hid_ready, 1)
                    else:
                        act.activation(hid, k.bank[f][:], ACT.Relu, bias=k.b1[u][:, f:f + 1]).then_inc(self.hid_ready, 1)

        for u in range(2):
            expert(u, u, u == 0)
        with act.Fori(1, E // 2) as i:
            for u in range(2):
                expert(i * 2 + u, u, False)

    def vector(self, dve):
        k = self.k

        def glu(e, u, g, first):
            for f in range(self.HF):
                if not (first and g < 2) and f == 0:
                    dve.wait_ge(self.y_ready, e * NT + (g - 1) * self.TG)
                dve.wait_ge(self.silu_ready, e * self.HPER + (g * self.HF + f + 1))
                dve.wait_ge(self.up_ready, e * self.PER + (g * self.UF + self.HF + f + 1))
                dve.tensor_tensor(k.hid[g % 2][:, f, :], k.glu_s[f][:], k.bank[self.HF + f][:],
                                  ALU.mult).then_inc(self.hid_ready, 1)

        def add(e, u, g):
            for j in range(self.TG):
                t = g * self.TG + j
                dve.wait_ge(self.y_ready, e * NT + (t + 1))
                dve.scalar_tensor_tensor(out=k.x[:, t * D:(t + 1) * D], in0=k.bank[4 + j][:, 0:D],
                                         scalar=k.gcol[u][:, t:t + 1], in1=k.x[:, t * D:(t + 1) * D],
                                         op0=ALU.mult, op1=ALU.add).then_inc(self.added, 1)

        def pair(e0, first):
            if not first:
                dve.wait_ge(self.added, e0 * NT)
            for u in range(2):
                dve.tensor_copy(k.gcol[u][:].unsqueeze(2), k.gate3[:, :, ds(e0 + u, 1)]).then_inc(self.col, 1)
            dve.wait_ge(self.col, e0 + 2)
            steps = [(u, g) for u in range(2) for g in range(self.NG)]
            for n in range(len(steps) + 1):
                if n < len(steps) and self.kind == "glu":
                    u, g = steps[n]
                    glu(e0 + u, u, g, first and u == 0)
                if n >= 1:
                    u, g = steps[n - 1]
                    add(e0 + u, u, g)

        pair(0, True)
        with dve.Fori(1, E // 2) as i:
            pair(i * 2, False)


class Attention(Stage):

    H, DH = 16, 16
    UNITS = HALVES * H // 2

    def __init__(self, k, tag, g, causal, wq, wk, wv, wo, bo, bq=None, bk=None, bv=None):
        super().__init__(k)
        self.g, self.causal = g, causal
        self.w = (wq, wk, wv, wo)
        self.b = (bq, bk, bv, bo)
        self.qmask = 0 if causal else 2
        S_ = self.sem
        self.w_landed = S_("w_landed")
        self.ctx_landed = [S_(f"ctx_landed{u}") for u in range(2)]
        self.proj_ready = S_("proj_ready")
        self.k_ready, self.q_ready, self.v_ready = S_("k_ready"), S_("q_ready"), S_("v_ready")
        self.scores_ready = S_("scores_ready")
        self.max_ready, self.exp_ready = S_("max_ready"), S_("exp_ready")
        self.turned = S_("turned")
        self.pt_ready = [S_(f"pt_ready{u}") for u in range(2)]
        self.pv_done = S_("pv_done")
        self.rsum_ready, self.o_ready = S_("rsum_ready"), S_("o_ready")
        self.o_turned, self.ot_ready = S_("o_turned"), S_("ot_ready")
        self.y_ready, self.added = S_("y_ready"), S_("added")
        sb = k.scoped
        self.wt = [sb(f"{tag}_w{n}", [P, KC, D], F32) for n in range(4)]
        self.bqk = sb(tag + "_bqk", [P, 2, KC], F32)
        self.bvb = sb(tag + "_bvb", [P, D], F32)
        self.bo = sb(tag + "_bo", [1, D], F32)
        self.cT = [sb(f"{tag}_cT{u}", [P, KC, S], F32) for u in range(2)]
        self.kT = [sb(f"{tag}_kT{u}", [P, KC * S], F32) for u in range(2)]
        self.qT = [[sb(f"{tag}_qT{u}{m}", [P, KC * S], F32) for m in range(2)] for u in range(2)]
        self.v = [sb(f"{tag}_v{u}", [P, HALVES, D], F32) for u in range(2)]
        self.p = [sb(f"{tag}_p{u}", [P, 2, S], F32) for u in range(2)]
        self.pT = [sb(f"{tag}_pT{u}", [P, 4 * P], F32) for u in range(2)]
        self.nmax = [sb(f"{tag}_nmax{u}", [P, HALVES * self.H], F32) for u in range(2)]
        self.sum = [sb(f"{tag}_sum{u}", [P, HALVES * self.H], F32) for u in range(2)]
        self.o = sb(tag + "_o", [P, HALVES * D], F32)
        self.oT = sb(tag + "_oT", [P, KC * S], F32)
        self.n_loads = 5 + 3 * (bq is not None)

    def unit(self, n):
        sb, hp = divmod(n, self.H // 2)
        tb = sb + 1 if self.causal else HALVES
        return sb, hp, tb * P, tb

    def sync(self, sp):
        k = self.k
        for wt, w in zip(self.wt, self.w):
            sp.dma_start(wt[:], w.rearrange("(c p) f -> p c f", p=P)).then_inc(self.w_landed, 16)
        bq, bk, bv, bo = self.b
        sp.dma_start(self.bo[:], bo.unsqueeze(0)).then_inc(self.w_landed, 16)
        if bq is not None:
            sp.dma_start(self.bqk[:, 0, :], bq).then_inc(self.w_landed, 16)
            sp.dma_start(self.bqk[:, 1, :], bk).then_inc(self.w_landed, 16)
            sp.dma_start(self.bvb[:], bv.partition_broadcast(P)).then_inc(self.w_landed, 16)
        ctxT = k.ins["ctxT"].rearrange("(c p) t -> p c t", p=P)
        with sp.Fori(0, B // 2) as i:
            for u in range(2):
                sp.wait_ge(self.proj_ready, i * 6 + 3 * u + 1)
                sp.dma_start(self.cT[u][:], ctxT[:, :, ds(i * 2 * S + u * S, S)]).then_inc(self.ctx_landed[u], 16)

    def tensor(self, pe):
        k = self.k
        wq, wk, wv, wo = self.wt
        pe.sem_inc(self.proj_ready, 4)
        pe.sem_inc(self.turned, 2)
        pe.sem_inc(self.pv_done, 2)
        pe.sem_inc(self.o_turned, 1)
        pe.sem_inc(self.y_ready, 1)
        pe.wait_ge(self.w_landed, 16 * self.n_loads)

        def proj(i, u):
            b = i * 2 + u
            pe.wait_ge(self.ctx_landed[u], i * 16 + 16)
            pe.wait_ge(self.ot_ready, i * 2 + 1)
            pe.wait_ge(self.k_ready, b * 2 + 1)
            for f in range(KC):
                for c in range(KC):
                    ins = pe.matmul(k.bank[5][:, f * S:(f + 1) * S], wk[:, c, f * P:(f + 1) * P],
                                    self.cT[u][:, c, :], start=c == 0, stop=c == KC - 1)
            ins.then_inc(self.proj_ready, 1)
            pe.wait_ge(self.q_ready, b * 4 + 1)
            for f in range(KC):
                for c in range(KC):
                    ins = pe.matmul(k.bank[6][:, f * S:(f + 1) * S], wq[:, c, f * P:(f + 1) * P],
                                    k.lnT[:, ds(i * 2 * S + (c * T + u * S), S)], start=c == 0, stop=c == KC - 1)
            ins.then_inc(self.proj_ready, 1)
            pe.wait_ge(self.v_ready, b + 1)
            pe.wait_ge(self.added, i * 2 + 1)
            for tb in range(HALVES):
                for c in range(KC):
                    ins = pe.matmul(k.bank[7][:, tb * D:(tb + 1) * D], self.cT[u][:, c, tb * P:(tb + 1) * P],
                                    wv[:, c, :], start=c == 0, stop=c == KC - 1)
            ins.then_inc(self.proj_ready, 1)

        def scores(i, u, n):
            sb, hp, width, _ = self.unit(n)
            b = i * 2 + u
            if n == 0:
                pe.wait_ge(self.k_ready, b * 2 + 3)
                pe.wait_ge(self.q_ready, b * 4 + 5)
            pe.wait_ge(self.exp_ready, b * self.UNITS + (n + 1))
            c, strip = divmod(hp, 4)
            at = slice(32 * strip, 32 * strip + 32)
            for m in range(2):
                out = k.bank[n % 2][:, m * S:m * S + width]
                ins = pe.matmul(out, self.qT[u][m][at, c * S + sb * P:c * S + (sb + 1) * P],
                                self.kT[u][at, c * S:c * S + width], start=True, stop=not self.causal)
                if self.causal:
                    ins = pe.matmul(k.bank[n % 2][:, m * S + sb * P:m * S + (sb + 1) * P], k.ident_bf[:],
                                    k.causal_bf[:], start=False, stop=True)
            ins.then_inc(self.scores_ready, 1)

        def turn(i, u, n):
            _, _, _, tb = self.unit(n)
            b = i * 2 + u
            pe.wait_ge(self.exp_ready, b * self.UNITS + (n + 3))
            pe.wait_ge(self.pt_ready[n % 2], b * (self.UNITS // 2) + (n // 2 + 1))
            for m in range(2):
                for q in range(tb):
                    ins = pe.transpose(k.bank[2 + n % 2][:, (m * tb + q) * P:(m * tb + q + 1) * P],
                                       self.p[n % 2][:, m, q * P:(q + 1) * P], k.ident[:])
            ins.then_inc(self.turned, 1)

        def pv(i, u, n):
            sb, hp, _, tb = self.unit(n)
            b = i * 2 + u
            if n == 0:
                pe.wait_ge(self.v_ready, b + 2)
                pe.wait_ge(self.o_ready, b + 1)
            pe.wait_ge(self.pt_ready[n % 2], b * (self.UNITS // 2) + (n // 2 + 2))
            for m in range(2):
                h = 2 * hp + m
                for q in range(tb):
                    ins = pe.matmul(k.bank[4][:, sb * D + h * self.DH:sb * D + (h + 1) * self.DH],
                                    self.pT[n % 2][:, (m * tb + q) * P:(m * tb + q + 1) * P],
                                    self.v[u][:, q, h * self.DH:(h + 1) * self.DH], start=q == 0, stop=q == tb - 1)
            ins.then_inc(self.pv_done, 1)

        def turn_o(i, u):
            b = i * 2 + u
            pe.wait_ge(self.o_ready, b + 2)
            pe.wait_ge(self.k_ready, b * 2 + (3 if u == 1 else 5))
            for c in range(KC):
                for sb in range(HALVES):
                    ins = pe.transpose(k.bank[5][:, c * S + sb * P:c * S + (sb + 1) * P],
                                       self.o[:, sb * D + c * P:sb * D + (c + 1) * P], k.ident[:])
            ins.then_inc(self.o_turned, 1)

        def out(i, u):
            b = i * 2 + u
            pe.wait_ge(self.ot_ready, b + 2)
            pe.wait_ge(self.v_ready, b + (2 if u == 1 else 3))
            for sb in range(HALVES):
                pe.matmul(k.bank[7][:, sb * D:(sb + 1) * D], k.ones_row[:], self.bo[:], start=True, stop=False)
                for c in range(KC):
                    ins = pe.matmul(k.bank[7][:, sb * D:(sb + 1) * D], self.oT[:, c * S + sb * P:c * S + (sb + 1) * P],
                                    wo[:, c, :], start=False, stop=c == KC - 1)
            ins.then_inc(self.y_ready, 1)

        N = self.UNITS
        with pe.Fori(0, B // 2) as i:
            proj(i, 0)
            for n in range(2 * N + 2):
                if n < 2 * N:
                    scores(i, n // N, n % N)
                if 1 <= n < 2 * N + 1:
                    turn(i, (n - 1) // N, (n - 1) % N)
                if n >= 2:
                    pv(i, (n - 2) // N, (n - 2) % N)
                if n == N - 4:
                    proj(i, 1)
                if n == N + 3:
                    turn_o(i, 0)
                if n == N + 5:
                    out(i, 0)
            turn_o(i, 1)
            out(i, 1)

    def scalar(self, act):
        k = self.k
        act.sem_inc(self.exp_ready, 2)
        act.sem_inc(self.pt_ready[0], 1)
        act.sem_inc(self.k_ready, 1)
        act.sem_inc(self.ot_ready, 1)
        bias = self.b[0] is not None

        def k_out(i, u):
            b = i * 2 + u
            act.wait_ge(self.proj_ready, b * 3 + 5)
            for c in range(KC):
                src, dst = k.bank[5][:, c * S:(c + 1) * S], self.kT[u][:, c * S:(c + 1) * S]
                if bias:
                    ins = act.activation(dst, src, ACT.Identity, bias=self.bqk[:, 1, c:c + 1])
                else:
                    ins = act.copy(dst, src)
                ins.then_inc(self.k_ready, 1)

        def exps(i, u, n):
            sb, hp, width, _ = self.unit(n)
            N = (i * 2 + u) * self.UNITS
            act.wait_ge(self.max_ready, N + (n + 1))
            act.wait_ge(self.turned, N + (n + 1))
            for m in range(2):
                col = sb * self.H + 2 * hp + m
                ins = act.activation(self.p[n % 2][:, m, 0:width], k.bank[n % 2][:, m * S:m * S + width], ACT.Exp,
                                     bias=self.nmax[u][:, col:col + 1], accum_out=self.sum[u][:, col:col + 1])
            ins.then_inc(self.exp_ready, 1)

        def pt_out(i, u, n):
            tb = self.unit(n)[3]
            N = (i * 2 + u) * self.UNITS
            act.wait_ge(self.turned, N + (n + 3))
            act.wait_ge(self.pv_done, N + (n + 1))
            act.copy(self.pT[n % 2][:, 0:2 * tb * P], k.bank[2 + n % 2][:, 0:2 * tb * P]).then_inc(self.pt_ready[n % 2], 1)

        def o_out(i, u):
            act.wait_ge(self.o_turned, i * 2 + (u + 2))
            act.wait_ge(self.y_ready, i * 2 + (u + 1))
            act.copy(self.oT[:], k.bank[5][:]).then_inc(self.ot_ready, 1)

        N = self.UNITS
        with act.Fori(0, B // 2) as i:
            k_out(i, 0)
            for n in range(2 * N + 1):
                if n < 2 * N:
                    exps(i, n // N, n % N)
                if n >= 1 and (n - 1) % 2 == 0:
                    pt_out(i, (n - 1) // N, (n - 1) % N)
                if n == N - 4:
                    k_out(i, 1)
                if n == N + 4:
                    o_out(i, 0)
            o_out(i, 1)

    def vector(self, dve):
        k = self.k
        dve.sem_inc(self.q_ready, 1)
        dve.sem_inc(self.v_ready, 1)
        dve.sem_inc(self.pt_ready[1], 1)
        dve.sem_inc(self.o_ready, 1)
        dve.sem_inc(self.added, 1)
        bias = self.b[0] is not None
        if bias:
            dve.wait_ge(self.w_landed, 16 * self.n_loads)

        def qv_out(i, u):
            b = i * 2 + u
            dve.wait_ge(self.proj_ready, b * 3 + 6)
            for c in range(KC):
                for m in range(2):
                    mask = k.qmask[:, self.qmask + m:self.qmask + m + 1]
                    src, dst = k.bank[6][:, c * S:(c + 1) * S], self.qT[u][m][:, c * S:(c + 1) * S]
                    if bias:
                        ins = dve.tensor_scalar(dst, src, self.bqk[:, 0, c:c + 1], mask, ALU.add, ALU.mult)
                    else:
                        ins = dve.tensor_scalar(dst, src, mask, None, ALU.mult)
                    ins.then_inc(self.q_ready, 1)
            dve.wait_ge(self.proj_ready, b * 3 + 7)
            v_ps = k.bank[7][:].rearrange("p (s d) -> p s d", d=D)
            if bias:
                ins = dve.tensor_tensor(self.v[u][:], v_ps, self.bvb[:].unsqueeze(1).to_broadcast([P, HALVES, D]), ALU.add)
            else:
                ins = dve.tensor_copy(self.v[u][:], v_ps)
            ins.then_inc(self.v_ready, 1)

        def maxes(i, u, n):
            sb, hp, width, _ = self.unit(n)
            dve.wait_ge(self.scores_ready, (i * 2 + u) * self.UNITS + (n + 1))
            col = sb * self.H + 2 * hp
            dve.tensor_reduce(self.nmax[u][:, col:col + 2],
                              k.bank[n % 2][:].rearrange("p (m t) -> p m t", m=2)[:, :, 0:width], AX.X, ALU.max,
                              negate=True).then_inc(self.max_ready, 1)

        def pt_out(i, u, n):
            tb = self.unit(n)[3]
            N = (i * 2 + u) * self.UNITS
            dve.wait_ge(self.turned, N + (n + 3))
            dve.wait_ge(self.pv_done, N + (n + 1))
            dve.tensor_copy(self.pT[n % 2][:, 0:2 * tb * P],
                            k.bank[2 + n % 2][:, 0:2 * tb * P]).then_inc(self.pt_ready[n % 2], 1)

        def normalise(i, u):
            b = i * 2 + u
            dve.wait_ge(self.pv_done, b * self.UNITS + (self.UNITS + 2))
            dve.reciprocal(self.sum[u][:], self.sum[u][:]).then_inc(self.rsum_ready, 1)
            dve.wait_ge(self.rsum_ready, b + 1)
            dve.wait_ge(self.o_turned, b + 1)
            dve.tensor_tensor(self.o[:].rearrange("p (h d) -> p h d", d=self.DH),
                              k.bank[4][:].rearrange("p (h d) -> p h d", d=self.DH),
                              self.sum[u][:].unsqueeze(2).to_broadcast([P, HALVES * self.H, self.DH]),
                              ALU.mult).then_inc(self.o_ready, 1)

        def add(i, u):
            b = i * 2 + u
            dve.wait_ge(self.y_ready, b + 2)
            xb = k.x[:, ds(i * 4 * D + u * 2 * D, 2 * D)]
            dve.scalar_tensor_tensor(out=xb, in0=k.bank[7][:], scalar=k.tanh_g[:, self.g:self.g + 1], in1=xb,
                                     op0=ALU.mult, op1=ALU.add).then_inc(self.added, 1)

        N = self.UNITS
        with dve.Fori(0, B // 2) as i:
            qv_out(i, 0)
            for n in range(2 * N + 1):
                if n < 2 * N:
                    maxes(i, n // N, n % N)
                if n >= 1 and (n - 1) % 2 == 1:
                    pt_out(i, (n - 1) // N, (n - 1) % N)
                if n == N + 2:
                    normalise(i, 0)
                if n == N - 4:
                    qv_out(i, 1)
                if n == N + 6:
                    add(i, 0)
            normalise(i, 1)
            add(i, 1)


class MlstmGates(Stage):

    def __init__(self, k, tag, NH, w, bias, shifted, cols, negm):
        super().__init__(k)
        self.NH, self.R, self.shifted = NH, B * NH, shifted
        self.w, self.bias, self.cols, self.negm = w, bias, cols, negm
        S_ = self.sem
        self.landed, self.logits_ready, self.own = S_("landed"), S_("logits_ready"), S_("chain")
        self.abs_ready, self.exp_ready, self.ln_ready = S_("abs_ready"), S_("exp_ready"), S_("ln_ready")
        self.g_ready, self.rows_turned = S_("g_ready"), S_("rows_turned")
        self.negm_ready, self.m_ready, self.en_ready = S_("negm_ready"), S_("m_ready"), S_("en_ready")
        self.cols_turned, self.negm_stored = S_("cols_turned"), S_("negm_stored")
        sb, R = k.scoped, self.R
        self.ctxT = sb(tag + "_ctxT", [P, KC * T], F32)
        self.wg = sb(tag + "_wg", [P, 3 * KC, 2 * NH], F32)
        self.bg = sb(tag + "_bg", [P, 2 * NH], F32)
        self.g = [sb(f"{tag}_g{n}", [P, HALVES * R], F32) for n in range(2)]
        self.t = sb(tag + "_t", [P, HALVES * R], F32)
        self.rows = sb(tag + "_rows", [R, 2 * S], F32)
        self.ones = sb(tag + "_ones", [R, S], F32)
        self.cs, self.a, self.M, self.m, self.nm, self.en = (sb(f"{tag}_{n}", [R, S], F32)
                                                             for n in ("cs", "a", "M", "m", "nm", "en"))

    def sync(self, sp):
        k = self.k
        sp.dma_start(self.wg[:], self.w.rearrange("(c p) g -> p c g", p=P)).then_inc(self.landed, 16)
        sp.dma_start(self.bg[:], self.bias.partition_broadcast(P)).then_inc(self.landed, 16)
        sp.dma_start(self.ctxT[:].rearrange("p (c t) -> p c t", c=KC),
                     k.ins["ctxT"].rearrange("(c p) t -> p c t", p=P)).then_inc(self.landed, 16)
        sp.wait_ge(self.negm_ready, 1)
        sp.dma_start(self.negm, self.nm[:]).then_inc(self.negm_stored, 16)
        sp.wait_ge(self.negm_stored, 16)

    def tensor(self, pe):
        k, R, G = self.k, self.R, 2 * self.NH
        pe.wait_ge(self.landed, 48)
        for t in range(NT):
            for n in range(3 * KC):
                src = k.lnT if n < KC else self.ctxT
                c = n % KC
                ins = pe.matmul(k.bank[0][:, t * G:(t + 1) * G], src[:, c * T + t * P:c * T + (t + 1) * P],
                                self.wg[:, n, :], start=n == 0, stop=n == 3 * KC - 1)
        ins.then_inc(self.logits_ready, 1)
        pe.wait_ge(self.g_ready, 2)
        for kind in range(2):
            for half in range(HALVES):
                n = kind * HALVES + half
                ins = pe.transpose(k.bank[1][0:R, n * P:(n + 1) * P], self.g[kind][:, half * R:(half + 1) * R], k.ident[:])
        ins.then_inc(self.rows_turned, 1)
        pe.wait_ge(self.negm_ready, 1)
        pe.wait_ge(self.en_ready, 1)
        for n, rows in enumerate((self.a, self.en)):
            for half in range(HALVES):
                at = (n * HALVES + half) * R
                ins = pe.transpose(k.bank[2][:, at:at + R], rows[:, half * P:(half + 1) * P], k.ident[0:R, 0:R])
        ins.then_inc(self.cols_turned, 1)

    def vector(self, dve):
        k, R, NH = self.k, self.R, self.NH
        chain = Chain(dve, self.own)
        dve.memset(self.ones[:], 1.0)
        dve.wait_ge(self.logits_ready, 1)
        ps = k.bank[0][:, 0:NT * 2 * NH].rearrange("p (b s k h) -> p s b k h", s=HALVES, k=2, h=NH)
        for kind in range(2):
            for half in range(HALVES):
                bias = self.bg[:, kind * NH:(kind + 1) * NH].unsqueeze(1).to_broadcast([P, B, NH])
                ins = dve.tensor_tensor(self.g[kind][:, half * R:(half + 1) * R].rearrange("p (b h) -> p b h", h=NH),
                                        ps[:, half, :, kind, :], bias, ALU.add)
                chain.link(ins)
        fg = self.g[1]
        dve.sem_inc(self.g_ready, 1)
        dve.wait_ge(self.ln_ready, 1)
        dve.scalar_tensor_tensor(out=fg[:], in0=fg[:], scalar=0.0, in1=self.t[:], op0=ALU.min,
                                 op1=ALU.subtract).then_inc(self.g_ready, 1)
        dve.wait_ge(self.rows_turned, 1)
        chain.link(dve.tensor_copy(self.rows[:], k.bank[1][0:R, :]))
        ig, lf = self.rows[:, 0:S], self.rows[:, S:2 * S]
        chain.link(dve.tensor_tensor_scan(self.cs[:], self.ones[:], lf, 0.0, ALU.mult, ALU.add))
        if self.shifted:
            dve.tensor_copy(self.a[:, 0:1], ig[:, 0:1])
            chain.link(dve.tensor_tensor(self.a[:, 1:S], ig[:, 1:S], self.cs[:, 0:S - 1], ALU.subtract))
        else:
            chain.link(dve.tensor_tensor(self.a[:], ig, self.cs[:], ALU.subtract))
        chain.link(dve.tensor_tensor_scan(self.M[:], self.ones[:], self.a[:], -3e38, ALU.mult, ALU.max))
        dve.tensor_tensor(self.m[:], self.cs[:], self.M[:], ALU.add).then_inc(self.m_ready, 1)
        dve.tensor_scalar(self.nm[:], self.M[:], -1.0, None, ALU.mult).then_inc(self.negm_ready, 1)
        dve.wait_ge(self.cols_turned, 1)
        dve.tensor_copy(self.cols[:], k.bank[2][:, 0:2 * HALVES * R])

    def scalar(self, act):
        act.wait_ge(self.g_ready, 1)
        act.activation(self.t[:], self.g[1][:], ACT.Abs).then_inc(self.abs_ready, 1)
        act.wait_ge(self.abs_ready, 1)
        act.activation(self.t[:], self.t[:], ACT.Exp, scale=-1.0).then_inc(self.exp_ready, 1)
        act.wait_ge(self.exp_ready, 1)
        act.activation(self.t[:], self.t[:], ACT.Ln, bias=1.0).then_inc(self.ln_ready, 1)
        act.wait_ge(self.m_ready, 1)
        act.activation(self.en[:], self.m[:], ACT.Exp, scale=-1.0).then_inc(self.en_ready, 1)


class Hops(Stage):

    VI = 8
    VB = 2 * VI

    def __init__(self, k, tag, kh, rpe, hopsT):
        super().__init__(k)
        self.kh, self.rpe = kh, rpe
        self.hopsT = hopsT.rearrange("(m p) v -> p m v", p=P)
        S_ = self.sem
        self.idx_landed = [S_(f"idx_landed{u}") for u in range(2)]
        self.gathered = [[S_(f"gathered{mb}{u}") for u in range(2)] for mb in range(2)]
        self.issued = S_("issued")
        self.turned = S_("turned")
        self.peT_ready = [S_(f"peT_ready{u}") for u in range(2)]
        self.q_ready = S_("q_ready")
        self.kmm_done = S_("kmm_done")
        self.kh_out = [S_(f"kh_out{u}") for u in range(2)]
        sb = k.scoped
        self.idx = [sb(f"{tag}_idx{u}", [P, 2, self.VI], I32) for u in range(2)]
        self.pe_rows = [[sb(f"{tag}_pe{u}{j}", [P, 2, D], F32) for j in range(self.VI)] for u in range(2)]
        self.peT = [sb(f"{tag}_peT{u}", [P, 4 * P], F32) for u in range(4)]
        self.q = [sb(f"{tag}_q{u}", [P, KC, self.VI, 32], F32) for u in range(2)]

    def phases(self, eng):
        for phase in range(2):
            with eng.Fori(0, P // self.VB) as i:
                yield phase, i, i * self.VB + phase * P

    def sync(self, sp):
        for phase, i, v0 in self.phases(sp):
            for u in range(2):
                sp.wait_ge(self.issued, i * 2 + (1 + u + phase * 16))
                sp.dma_start(self.idx[u][:], self.hopsT[:, :, ds(v0 + u * self.VI, self.VI)]).then_inc(self.idx_landed[u], 16)

    def gpsimd(self, pool):
        pool.sem_inc(self.issued, 2)
        for phase, i, v0 in self.phases(pool):
            for u in range(2):
                pool.wait_ge(self.idx_landed[u], i * 16 + (16 + phase * 128))
                wait_apart(pool, self.turned, v0 + (u * self.VI + 8), self.k.passed)
                for j in range(self.VI):
                    for mb in range(phase + 1):
                        pool.indirect_dma_start(self.pe_rows[u][j][:, mb, :], None, self.rpe,
                                                bass.IndirectOffsetOnAxis(ap=self.idx[u][:, mb, j:j + 1], axis=0)
                                                ).then_inc(self.gathered[phase][u], 16)
                pool.wait_ge(self.gathered[phase][u], i * (128 * (phase + 1)) + 128 * (phase + 1))
                pool.sem_inc(self.issued, 1)

    def tensor(self, pe):
        k = self.k
        pe.sem_inc(self.turned, 16)
        pe.sem_inc(self.kmm_done, 16)

        def turn(phase, i, v0, n):
            u, j = divmod(n, self.VI)
            if j == 0:
                pe.wait_ge(self.gathered[phase][u], i * (128 * (phase + 1)) + 128 * (phase + 1))
            pe.wait_ge(self.peT_ready[n % 2], i * self.VI + (phase * 64 + n // 2 + 1))
            for mb in range(phase + 1):
                for c in range(KC):
                    ins = pe.transpose(k.bank[n % 4][:, (mb * KC + c) * P:(mb * KC + c + 1) * P],
                                       self.pe_rows[u][j][:, mb, c * P:(c + 1) * P], k.ident[:])
            ins.then_inc(self.turned, 1)

        def mult(phase, i, v0, n):
            u, j = divmod(n, self.VI)
            pe.wait_ge(self.peT_ready[n % 2], i * self.VI + (phase * 64 + n // 2 + 3))
            if j == 0:
                pe.wait_ge(self.q_ready, i * 4 + (phase * 32 + 2 * u + 2))
            g = n // 4
            if n % 4 == 0:
                pe.wait_ge(self.kh_out[g % 2], i * 2 + (phase * 16 + g // 2 + 1))
            for mb in range(phase + 1):
                for c in range(KC):
                    at = mb * 256 + (n % 4) * 64 + c * 32
                    ins = pe.matmul(k.bank[4 + g][:, at:at + 32], self.peT[n % 4][:, (mb * KC + c) * P:(mb * KC + c + 1) * P],
                                    self.q[u][:, c, j, :], start=True, stop=True)
            ins.then_inc(self.kmm_done, 1)

        for phase, i, v0 in self.phases(pe):
            for n in range(self.VB + 2):
                if n < self.VB:
                    turn(phase, i, v0, n)
                if n >= 2:
                    mult(phase, i, v0, n - 2)

    def peT_out(self, eng, copy, phase, i, v0, n):
        w = (phase + 1) * KC * P
        eng.wait_ge(self.turned, v0 + (n + 17))
        eng.wait_ge(self.kmm_done, v0 + (n + 13))
        copy(self.peT[n % 4][:, 0:w], self.k.bank[n % 4][:, 0:w]).then_inc(self.peT_ready[n % 2], 1)

    def kh_to_sbuf(self, eng, copy, phase, i, v0, g):
        k = self.k
        eng.wait_ge(self.kmm_done, v0 + (g * 4 + 4 + 16))
        for mb in range(phase + 1):
            at = v0 * 64 + (g * 256 - mb * P * 64)
            ins = copy(self.kh[mb][:, ds(at, 256)], k.bank[4 + g][:, mb * 256:(mb + 1) * 256])
        ins.then_inc(self.kh_out[g % 2], 1)

    def scalar(self, act):
        act.sem_inc(self.peT_ready[0], 2)
        act.sem_inc(self.kh_out[0], 1)
        for phase, i, v0 in self.phases(act):
            for n in range(self.VB + 4):
                if n < self.VB and n % 2 == 0:
                    self.peT_out(act, act.copy, phase, i, v0, n)
                if n >= 7 and (n - 7) % 8 == 0:
                    self.kh_to_sbuf(act, act.copy, phase, i, v0, (n - 7) // 4)

    def vector(self, dve):
        k = self.k
        dve.sem_inc(self.peT_ready[1], 2)
        dve.sem_inc(self.kh_out[1], 1)

        def spread(phase, i, v0, u):
            dve.wait_ge(self.kmm_done, v0 + (u * self.VI + 8))
            full = [P, self.VI, B, 4]
            for c in range(KC):
                src = k.lnT[:].rearrange("p (c b s) -> p c s b", c=KC, b=B)[:, c, ds(v0 + u * self.VI, self.VI), :]
                dve.tensor_tensor(self.q[u][:, c].rearrange("p v (b r) -> p v b r", r=4),
                                  src.unsqueeze(3).to_broadcast(full),
                                  k.strip[:].unsqueeze(1).unsqueeze(1).to_broadcast(full), ALU.mult).then_inc(self.q_ready, 1)

        for phase, i, v0 in self.phases(dve):
            for n in range(self.VB + 4):
                if n in (0, self.VI):
                    spread(phase, i, v0, n // self.VI)
                if n < self.VB and n % 2 == 1:
                    self.peT_out(dve, dve.tensor_copy, phase, i, v0, n)
                if n >= 7 and (n - 7) % 8 == 4:
                    self.kh_to_sbuf(dve, dve.tensor_copy, phase, i, v0, (n - 7) // 4)


class Mlstm(Stage):

    def __init__(self, k, tag, NH, eps, cols, negm, var, kh=None):
        super().__init__(k)
        self.NH, self.R, self.DH, self.NS = NH, B * NH, D // NH, NH // 2
        self.eps, self.cols, self.negm, self.var, self.kh = eps, cols, negm, var, kh
        self.scale = float(self.DH) ** -0.5
        S_ = self.sem
        self.landed = [S_(f"landed{u}") for u in range(2)]
        self.q_ready, self.arg1_ready, self.arg_ready = S_("q_ready"), S_("arg1_ready"), S_("arg_ready")
        self.d_ready, self.masked = S_("d_ready"), S_("masked")
        self.qk_ready, self.qk_read, self.ct_ready = S_("qk_ready"), S_("qk_read"), S_("ct_ready")
        self.hm_done, self.h_ready, self.h_read = S_("hm_done"), S_("h_ready"), S_("h_read")
        self.own = S_("chain")
        self.cent_ready, self.cent_kept, self.sq_ready, self.var_done = S_("cent_ready"), S_("cent_kept"), S_("sq_ready"), S_("var_done")
        sb, DH = k.scoped, self.DH
        self.cT = [sb(f"{tag}_cT{u}", [P, KC, S], F32) for u in range(2)]
        self.qT = [sb(f"{tag}_qT{u}", [P, KC, S], F32) for u in range(2)]
        self.v = [sb(f"{tag}_v{u}", [P, HALVES, NH, DH + 1], F32) for u in range(2)]
        self.d0 = [sb(f"{tag}_d0{u}", [P, NH, S], F32) for u in range(2)]
        self.d1 = [sb(f"{tag}_d1{u}", [P, NH, P], F32) for u in range(2)]
        self.ct = [sb(f"{tag}_ct{u}", [P, 2 * S + 2 * P], F32) for u in range(2)]
        self.tmp = [sb(f"{tag}_tmp{u}", [P, 2 * S + 2 * P], F32) for u in range(2)] if kh else None
        self.den = sb(tag + "_den", [P, HALVES, NH], F32)
        self.mu = sb(tag + "_mu", [P, HALVES * NH], F32)
        self.h1 = sb(tag + "_h1", [P, HALVES * NH, DH], F32)
        self.sq = sb(tag + "_sq", [P, HALVES * NH, DH], F32)

    def sync(self, sp):
        k, NH = self.k, self.NH
        ctxT = k.ins["ctxT"].rearrange("(c p) t -> p c t", p=P)
        ctx = k.ins["ctx_1024"].rearrange("b (s p) (h d) -> p b s h d", p=P, h=NH)
        negm = self.negm.rearrange("r s -> (r s)")
        with sp.Fori(0, B // 2) as i:
            for u in range(2):
                b = i * 2 + u
                sp.wait_ge(self.h_ready, b + 1)
                sp.dma_start(self.d0[u][:].rearrange("p h s -> p (h s)"),
                             negm[ds(i * 2 * NH * S + u * NH * S, NH * S)].partition_broadcast(P)).then_inc(self.landed[u], 16)
                sp.dma_start(self.cT[u][:], ctxT[:, :, ds(i * 2 * S + u * S, S)]).then_inc(self.landed[u], 16)
                for s in range(HALVES):
                    sp.dma_start(self.v[u][:, s, :, 0:self.DH],
                                 ctx[:, ds(b, 1), s].rearrange("p o h d -> p (o h) d")).then_inc(self.landed[u], 16)

    def tensor(self, pe):
        k, DH, NS, NH = self.k, self.DH, self.NS, self.NH
        pe.sem_inc(self.h_ready, 2)
        pe.sem_inc(self.hm_done, 2)

        def qk(i, u, r):
            n = (i * 2 + u) * NS
            pair = (u * NS + r) % 2
            if r == 0:
                pe.wait_ge(self.landed[u], i * 64 + 64)
                pe.wait_ge(self.q_ready, i * 2 + (u + 1))
            pe.wait_ge(self.qk_read, n + (r + 1))
            at = slice(r * DH, (r + 1) * DH)
            for c in range(KC):
                pe.matmul(k.bank[2 * pair][:, c * S:(c + 1) * S], self.cT[u][at, c, 0:P], self.qT[u][at, c, :],
                          start=True, stop=True)
            for c in range(KC):
                ins = pe.matmul(k.bank[2 * pair + 1][:, c * P:(c + 1) * P], self.cT[u][at, c, P:S],
                                self.qT[u][at, c, P:S], start=True, stop=True)
            ins.then_inc(self.qk_ready, 1)

        def hm(i, u, r):
            n = (i * 2 + u) * NS
            ct = self.ct[(u * NS + r) % 2]
            if r == 0:
                pe.wait_ge(self.h_read, i * 2 + (u + 1))
            pe.wait_ge(self.ct_ready, n + (r + 1))
            for c in range(KC):
                h = c * NS + r
                cols = slice(h * (DH + 1), (h + 1) * (DH + 1))
                pe.matmul(k.bank[4 + 2 * u][:, cols], ct[:, c * S:c * S + P], self.v[u][:, 0, h, :], start=True, stop=True)
                pe.matmul(k.bank[5 + 2 * u][:, cols], ct[:, c * S + P:(c + 1) * S], self.v[u][:, 0, h, :], start=True, stop=False)
                ins = pe.matmul(k.bank[5 + 2 * u][:, cols], ct[:, 2 * S + c * P:2 * S + (c + 1) * P], self.v[u][:, 1, h, :],
                                start=False, stop=True)
            ins.then_inc(self.hm_done, 1)
            if r == NS - 1:
                pe.wait_ge(self.hm_done, n + (NS + 2))
                pe.sem_inc(self.h_ready, 1)

        steps = [(u, r) for u in range(2) for r in range(NS)]
        with pe.Fori(0, B // 2) as i:
            for n in range(len(steps) + 1):
                if n < len(steps):
                    qk(i, *steps[n])
                if n >= 1:
                    hm(i, *steps[n - 1])

    def scalar(self, act):
        k = self.k
        act.sem_inc(self.cent_kept, 1)
        lnT = k.lnT[:].rearrange("p (c t) -> p c t", c=KC)

        def q_in(i, u):
            wait_apart(act, self.h_ready, i * 2 + (u + 1), k.passed)
            act.copy(self.qT[u][:], lnT[:, :, ds(i * 2 * S + u * S, S)]).then_inc(self.q_ready, 1)

        def decay(i, u):
            act.wait_ge(self.arg1_ready, i * 2 + (u + 1))
            act.activation(self.d1[u][:], self.d1[u][:], ACT.Exp).then_inc(self.d_ready, 1)
            act.wait_ge(self.arg_ready, i * 2 + (u + 1))
            act.activation(self.d0[u][:], self.d0[u][:], ACT.Exp).then_inc(self.d_ready, 1)

        def keep(i, u):
            b = i * 2 + u
            act.wait_ge(self.cent_ready, b + 1)
            act.activation(self.sq[:], self.h1[:], ACT.Square).then_inc(self.sq_ready, 1)
            wait_apart(act, self.q_ready, b + 1, k.passed)
            act.copy(lnT[:, :, ds(i * 2 * S + u * S, S)],
                     self.h1[:].rearrange("p (s h) d -> p s (h d)", s=HALVES)).then_inc(self.cent_kept, 1)

        with act.Fori(0, B // 2) as i:
            q_in(i, 0)
            decay(i, 0)
            q_in(i, 1)
            decay(i, 1)
            keep(i, 0)
            keep(i, 1)

    def views(self, u, r, buf):
        NS = self.NS
        for t, (a, w) in enumerate(((0, S), (2 * S, P))):
            d = (self.d0 if t == 0 else self.d1)[u][:].rearrange("p (c r) s -> p c r s", r=NS)[:, :, r, :]
            yield t, w, buf[:, a:a + 2 * w].rearrange("p (c s) -> p c s", c=KC), d

    def vector(self, dve):
        k, DH, NS, NH, R = self.k, self.DH, self.NS, self.NH, self.R
        LINKS = 7
        chain = Chain(dve, self.own)
        dve.sem_inc(self.qk_read, 2)
        dve.sem_inc(self.h_read, 2)
        for u in range(2):
            ins = dve.memset(self.v[u][:, :, :, DH:DH + 1], 1.0)
        dve.sem_inc(self.var_done, 1)

        def args(i, u):
            b = i * 2 + u
            dve.wait_ge(self.landed[u], i * 64 + 64)
            for t in (1, 0):
                for h in range(NH):
                    dst = self.d1[u][:, h, :] if t else self.d0[u][:, h, :]
                    src = self.d0[u][:, h, P:S] if t else self.d0[u][:, h, :]
                    ins = dve.tensor_scalar(dst, src, self.cols[:, ds(i * 2 * NH + (t * R + u * NH + h), 1)], 0.0,
                                            ALU.add, ALU.min)
                ins.then_inc(self.arg1_ready if t else self.arg_ready, 1)
                if t:
                    dve.wait_ge(self.arg1_ready, b + 1)

        def ct(i, u, r):
            n = (i * 2 + u) * NS
            pair = (u * NS + r) % 2
            if r == 0 and not self.kh:
                dve.wait_ge(self.masked, i * 4 + (2 * u + 2))
            dve.wait_ge(self.qk_ready, n + (r + 1))
            dve.wait_ge(self.hm_done, n + (r + 1))
            buf = self.tmp[pair] if self.kh else self.ct[pair]
            for t, w, dst, d in self.views(u, r, buf):
                src = k.bank[2 * pair + t][:, 0:2 * w].rearrange("p (c s) -> p c s", c=KC)
                if self.kh:
                    hop = self.kh[t][:].rearrange("p (v c m) -> p c v m", c=KC, m=4 * B)
                    hop = hop[:, :, :, ds(i * 8 + (u * 4 + r), 1)].rearrange("p c v o -> p c (v o)")
                    ins = dve.scalar_tensor_tensor(out=dst, in0=src, scalar=self.scale, in1=hop, op0=ALU.mult, op1=ALU.add)
                else:
                    ins = dve.scalar_tensor_tensor(out=dst, in0=src, scalar=self.scale, in1=d, op0=ALU.mult, op1=ALU.mult)
            ins.then_inc(self.qk_read, 1)
            if not self.kh:
                dve.wait_ge(self.qk_read, n + (r + 3))
                dve.sem_inc(self.ct_ready, 1)

        def finish(i, u):
            b = i * 2 + u
            chain.start(i * 2 * LINKS + u * LINKS)
            dve.wait_ge(self.h_ready, b + 3)
            h_ps = k.ps[:, (4 + 2 * u) * 512:(6 + 2 * u) * 512].rearrange("p (s w) -> p s w", s=HALVES)
            h_ps = h_ps[:, :, 0:NH * (DH + 1)].rearrange("p s (h e) -> p s h e", e=DH + 1)
            en = self.cols[:, 2 * R:4 * R].rearrange("p (s r) -> p s r", s=HALVES)[:, :, ds(i * 2 * NH + u * NH, NH)]
            chain.link(dve.tensor_tensor(self.den[:], h_ps[:, :, :, DH], en, ALU.max))
            chain.link(dve.scalar_tensor_tensor(out=self.den[:], in0=h_ps[:, :, :, DH], scalar=-1.0, in1=self.den[:],
                                                op0=ALU.mult, op1=ALU.max))
            chain.link(dve.tensor_scalar(self.den[:], self.den[:], self.eps, None, ALU.add))
            chain.link(dve.reciprocal(self.den[:], self.den[:]))
            dve.wait_ge(self.cent_kept, b + 1)
            h1 = self.h1[:].rearrange("p (s h) d -> p s h d", s=HALVES)
            dve.tensor_tensor(h1, h_ps[:, :, :, 0:DH], self.den[:].unsqueeze(3).to_broadcast([P, HALVES, NH, DH]),
                              ALU.mult).then_inc(self.h_read, 1)
            dve.wait_ge(self.h_read, b + 3)
            chain.link(dve.tensor_reduce(self.mu[:], self.h1[:], AX.X, ALU.add))
            chain.link(dve.tensor_scalar(self.mu[:], self.mu[:], 1.0 / DH, None, ALU.mult))
            dve.tensor_tensor(self.h1[:], self.h1[:], self.mu[:].unsqueeze(2).to_broadcast([P, HALVES * NH, DH]),
                              ALU.subtract).then_inc(self.cent_ready, 1)
            dve.wait_ge(self.sq_ready, b + 1)
            chain.link(dve.tensor_reduce(self.var[:].rearrange("p (s r) -> p s r", s=HALVES)[:, :, ds(i * 2 * NH + u * NH, NH)],
                              self.sq[:].rearrange("p (s h) d -> p s h d", s=HALVES), AX.X, ALU.add))

        with dve.Fori(0, B // 2) as i:
            args(i, 0)
            args(i, 1)
            for r in range(NS):
                ct(i, 0, r)
            for r in range(NS):
                ct(i, 1, r)
            finish(i, 0)
            finish(i, 1)

    def gpsimd(self, pool):
        k, NS, NH = self.k, self.NS, self.NH

        def mask(i, u):
            cm = k.causal01[:].unsqueeze(1).to_broadcast([P, NH, P])
            for t, d in ((1, self.d1[u][:]), (0, self.d0[u][:, :, 0:P])):
                pool.wait_ge(self.d_ready, i * 4 + (2 * u + 2 - t))
                pool.tensor_tensor(d, d, cm, ALU.mult).then_inc(self.masked, 1)

        def ct(i, u, r):
            n = (i * 2 + u) * NS
            pair = (u * NS + r) % 2
            if r == 0:
                pool.wait_ge(self.masked, i * 4 + (2 * u + 2))
            pool.wait_ge(self.qk_read, n + (r + 3))
            pool.wait_ge(self.hm_done, n + (r + 1))
            for (t, w, dst, d), (_, _, src, _) in zip(self.views(u, r, self.ct[pair]), self.views(u, r, self.tmp[pair])):
                ins = pool.tensor_tensor(dst, src, d, ALU.mult)
            ins.then_inc(self.ct_ready, 1)

        with pool.Fori(0, B // 2) as i:
            mask(i, 0)
            if not self.kh:
                mask(i, 1)
            else:
                for r in range(NS):
                    ct(i, 0, r)
                mask(i, 1)
                for r in range(NS):
                    ct(i, 1, r)


class MlstmOut(Stage):

    def __init__(self, k, tag, NH, g, var, w, b=None):
        super().__init__(k)
        self.NH, self.R, self.DH, self.g, self.var, self.w_dram, self.b_dram = NH, B * NH, D // NH, g, var, w, b
        S_ = self.sem
        self.landed, self.own, self.inv_ready, self.rstd_ready = S_("landed"), S_("chain"), S_("inv_ready"), S_("rstd_ready")
        self.wrow = k.scoped(tag + "_wrow", [P, D], F32)
        self.brow = k.scoped(tag + "_brow", [P, D], F32)

    def sync(self, sp):
        sp.dma_start(self.wrow[:], self.w_dram.partition_broadcast(P)).then_inc(self.landed, 16)
        if self.b_dram is not None:
            sp.dma_start(self.brow[:], self.b_dram.partition_broadcast(P)).then_inc(self.landed, 16)

    def scalar(self, act):
        act.wait_ge(self.inv_ready, 1)
        act.activation(self.var[:], self.var[:], ACT.Sqrt).then_inc(self.rstd_ready, 1)

    def vector(self, dve):
        k, R, DH = self.k, self.R, self.DH
        chain = Chain(dve, self.own)
        tg = k.tanh_g[:, self.g:self.g + 1]
        chain.link(dve.tensor_scalar(self.var[:], self.var[:], 1.0 / DH, LN_EPS, ALU.mult, ALU.add))
        dve.reciprocal(self.var[:], self.var[:]).then_inc(self.inv_ready, 1)
        dve.wait_ge(self.landed, 16 * (1 + (self.b_dram is not None)))
        chain.link(dve.tensor_scalar(self.wrow[:], self.wrow[:], 1.0, tg, ALU.add, ALU.mult))
        if self.b_dram is not None:
            chain.link(dve.tensor_scalar(self.brow[:], self.brow[:], tg, None, ALU.mult))
        dve.wait_ge(self.rstd_ready, 1)
        for half in range(HALVES):
            h = k.lnT[:, half * T:half * T + B * D]
            chain.link(dve.tensor_tensor(h.rearrange("p (r d) -> p r d", d=DH), h.rearrange("p (r d) -> p r d", d=DH),
                                         self.var[:, half * R:(half + 1) * R].unsqueeze(2).to_broadcast([P, R, DH]), ALU.mult))
            h3 = h.rearrange("p (b d) -> p b d", d=D)
            row = lambda a: a[:].unsqueeze(1).to_broadcast([P, B, D])
            chain.link(dve.tensor_tensor(h3, h3, row(self.wrow), ALU.mult))
            x = k.x[:].rearrange("p (b s d) -> p s b d", s=HALVES, d=D)[:, half]
            chain.link(dve.tensor_tensor(x, h3, x, ALU.add))
            if self.b_dram is not None:
                chain.link(dve.tensor_tensor(x, x, row(self.brow), ALU.add))


class Kernel:
    def __init__(self, nc, ctx, ins, out):
        self.nc, self.ctx, self.ins, self.out = nc, ctx, ins, out
        self.stage_sems = {}
        sb, F = self.sb, F32
        self.x = sb("x", [P, NT * D], F)
        self.lnT = sb("lnT", [P, KC * T], F)
        self.ident = sb("ident", [P, P], F)
        self.rank = sb("rank", [P, E], F)
        self.graw = sb("graw", [P, 8], F)
        self.tanh_g = sb("tanh_g", [P, 8], F)
        self.ps = ctx.enter_context(nc.psum_tensor("ps", [P, 8 * 512], F))
        self.bank = [self.ps[:, n * 512:(n + 1) * 512] for n in range(8)]
        self.ident_bf = sb("ident_bf", [P, P], BF16)
        self.causal_bf = sb("causal_bf", [P, P], BF16)
        self.causal01 = sb("causal01", [P, P], F)
        self.ones_row = sb("ones_row", [1, P], F)
        self.prow = sb("prow", [P, 1], I32)
        self.pbits = sb("pbits", [P, 2], I32)
        self.pbitsf = sb("pbitsf", [P, 2], F)
        self.qmask = sb("qmask", [P, 4], F)
        self.strip = sb("strip", [P, 4], F)

        self.setup_loaded = self.sem("setup_loaded")
        self.setup_dve = self.sem("setup_dve")
        self.setup_pool = self.sem("setup_pool")
        self.setup_tanh = self.sem("setup_tanh")
        self.passed = self.sem("passed")
        self.stored = self.sem("stored")
        self.over = {e: self.sem(e + "_over") for e in ("pe", "act", "dve", "pool", "sp")}

    def sb(self, name, shape, dt):
        return self.ctx.enter_context(self.nc.sbuf_tensor(name, shape, dt))

    def ln_buffers(self, tag):
        self.ln_stats = self.scoped(tag + "_ln_stats", [P, NT * 6], F32)
        self.ln_mv = self.scoped(tag + "_ln_mv", [P, NT, 2], F32)
        self.ln_mean = self.scoped(tag + "_ln_mean", [P, NT], F32)
        self.ln_inv = self.scoped(tag + "_ln_inv", [P, NT], F32)
        self.ln_rstd = self.scoped(tag + "_ln_rstd", [P, NT], F32)
        self.ln_x = [self.scoped(tag + f"_ln_x{u}", [P, 4, D], F32) for u in range(2)]

    def ffn_buffers(self, tag):
        self.wg = self.scoped(tag + "_wg", [P, KC, E], F32)
        self.bg = self.scoped(tag + "_bg", [P, E], F32)
        self.rt = self.scoped(tag + "_rt", [P, 6, NT, E], F32)
        self.rs = self.scoped(tag + "_rs", [P, 6, NT], F32)
        self.rexp = self.scoped(tag + "_rexp", [P, NT], F32)
        self.gate = self.scoped(tag + "_gate", [P, NT * E], F32)
        self.gate3 = self.gate[:].rearrange("p (t e) -> p t e", e=E)
        self.gateT = self.scoped(tag + "_gateT", [E, T], F32)
        self.ebias = self.scoped(tag + "_ebias", [E, D], F32)
        self.gcol = [self.scoped(tag + f"_gcol{u}", [P, NT], F32) for u in range(2)]
        self.up = [self.scoped(tag + f"_up{u}", [P, KC, 512], F32) for u in range(2)]
        self.down = [self.scoped(tag + f"_down{u}", [P, 4, D], F32) for u in range(2)]
        self.b1 = [self.scoped(tag + f"_b1_{u}", [P, 4], F32) for u in range(2)]
        self.hid = [self.scoped(tag + f"_hid{u}", [P, 4, 512], F32) for u in range(2)]
        self.glu_s = [self.scoped(tag + f"_glu_s{u}", [P, 512], F32) for u in range(2)]


    def scoped(self, name, shape, dt):
        return self.scope.enter_context(self.nc.sbuf_tensor(name, shape, dt))

    def shared_sem(self, name):
        if name not in self.stage_sems:
            self.stage_sems[name] = self.sem(name)
        return self.stage_sems[name]

    def sem(self, name):
        return self.ctx.enter_context(self.nc.semaphore(name))


class Setup(Stage):

    def sync(self, sp):
        k = self.k
        x = k.ins["x"].rearrange("b s d -> (b s) d").rearrange("(t p) d -> p t d", p=P)
        sp.dma_start(k.x[:].rearrange("p (t d) -> p t d", d=D), x).then_inc(k.setup_loaded, 16)
        sp.dma_start(k.graw[:, 0:4], k.ins["g_xattn"].partition_broadcast(P)).then_inc(k.setup_loaded, 16)
        sp.dma_start(k.graw[:, 4:8], k.ins["g_ffn"].partition_broadcast(P)).then_inc(k.setup_loaded, 16)
        sp.wait_ge(k.setup_loaded, 48)

    def gpsimd(self, pool):
        k = self.k
        pool.memset(k.ident[:], 0.0).then_inc(k.setup_pool, 1)
        pool.wait_ge(k.setup_pool, 1)
        pool.affine_select(out=k.ident[:], in_=k.ident[:], compare_op=ALU.not_equal, fill=1.0, base=0,
                           pattern=[[-1, P]], channel_multiplier=1).then_inc(k.setup_pool, 1)
        for e in range(E):
            pool.memset(k.rank[:, e:e + 1], float(E - e)).then_inc(k.setup_pool, 1)
        pool.memset(k.causal_bf[:], 0.0).then_inc(k.setup_pool, 1)
        pool.memset(k.ones_row[:], 1.0).then_inc(k.setup_pool, 1)
        pool.memset(k.causal01[:], 1.0).then_inc(k.setup_pool, 1)
        pool.iota(k.prow[:], pattern=[[0, 1]], base=0, channel_multiplier=1).then_inc(k.setup_pool, 1)
        pool.wait_ge(k.setup_pool, 6 + E)
        pool.affine_select(out=k.causal_bf[:], in_=k.causal_bf[:], compare_op=ALU.is_ge, fill=-BIG, base=0,
                           pattern=[[-1, P]], channel_multiplier=1).then_inc(k.setup_pool, 1)
        pool.affine_select(out=k.causal01[:], in_=k.causal01[:], compare_op=ALU.is_ge, fill=0.0, base=0,
                           pattern=[[1, P]], channel_multiplier=-1).then_inc(k.setup_pool, 1)

    def vector(self, dve):
        k = self.k
        chain = Chain(dve, k.setup_dve)
        dve.wait_ge(k.setup_pool, 8 + E)
        chain.link(dve.tensor_copy(k.ident_bf[:], k.ident[:]))
        chain.link(dve.tensor_scalar(k.pbits[:, 0:1], k.prow[:], 16, None, ALU.bitwise_and))
        chain.link(dve.tensor_scalar(k.pbits[:, 1:2], k.prow[:], 96, None, ALU.bitwise_and))
        chain.link(dve.tensor_copy(k.pbitsf[:], k.pbits[:]))
        for n, scale in enumerate((0.25, 0.0625)):
            for m in range(2):
                dve.tensor_scalar(k.qmask[:, 2 * n + m:2 * n + m + 1], k.pbitsf[:, 0:1], 16.0 * m, scale,
                                  ALU.is_equal, ALU.mult)
        for r in range(4):
            dve.tensor_scalar(k.strip[:, r:r + 1], k.pbitsf[:, 1:2], 32.0 * r, None, ALU.is_equal)

    def scalar(self, act):
        k = self.k
        act.wait_ge(k.setup_loaded, 48)
        act.activation(k.tanh_g[:], k.graw[:], ACT.Tanh).then_inc(k.setup_tanh, 1)


class Store(Stage):
    def sync(self, sp):
        k = self.k
        out = k.out.rearrange("b s d -> (b s) d").rearrange("(t p) d -> p t d", p=P)
        sp.dma_start(out, k.x[:].rearrange("p (t d) -> p t d", d=D)).then_inc(k.stored, 16)
        sp.wait_ge(k.stored, 16)


def make_stages(k):
    I = k.ins
    stages = [Setup(k)]

    @contextmanager
    def scope():
        with ExitStack() as k.scope:
            yield

    def layer_norm(tag):
        with scope():
            k.ln_buffers(tag)
            stages.append(LayerNorm(k, tag))

    def mlstm(tag, layer, NH, eps, g, shifted, w, b=None, rpe=None, hopsT=None):
        R = B * NH
        negm = k.nc.dram_tensor(tag + "_negm", (R, S), F32, kind="Internal").ap()
        with ExitStack() as held:
            sb = lambda n, shape: held.enter_context(k.nc.sbuf_tensor(f"{tag}_{n}", shape, F32))
            cols, var = sb("cols", [P, 4 * R]), sb("var", [P, HALVES * R])
            kh = [sb("kh0", [P, S * 64]), sb("kh1", [P, P * 64])] if rpe is not None else None
            with scope():
                stages.append(MlstmGates(k, tag + "_mg", NH, I[layer + "_gate_w"], I[layer + "_gate_b"], shifted, cols, negm))
            if kh:
                with scope():
                    stages.append(Hops(k, tag + "_hp", kh, rpe, hopsT))
            with scope():
                stages.append(Mlstm(k, tag + "_ml", NH, eps, cols, negm, var, kh))
            with scope():
                stages.append(MlstmOut(k, tag + "_mo", NH, g, var, w, b))

    for n in SUBLAYERS:
        tag = f"s{n}"
        layer_norm(tag + "_ln")
        if n == 0:
            mlstm(tag, "L0", 4, 1e-8, 0, True, I["L0_xattn_out_w"])
        if n == 6:
            mlstm(tag, "L3", 8, 1e-6, 3, False, I["L3_xattn_ln_w"], I["L3_xattn_ln_b"],
                  I["L3_xattn_rpe"], I["hopsT"])
        with scope():
            if n == 2:
                stages.append(Attention(k, tag + "_at", 1, True, *(I["L1_xattn_w_" + m] for m in "qkvo"),
                                        *(I["L1_xattn_b_" + m] for m in "oqkv")))
            if n == 4:
                stages.append(Attention(k, tag + "_at", 2, False, *(I["L2_xattn_W" + m] for m in "qkvo"),
                                        I["L2_xattn_bo"]))
            if n % 2:
                k.ffn_buffers(tag)
                layer = f"L{n // 2}_ffn_"
                wg = {1: "Wg", 3: "router_w", 5: "router_w", 7: "Wg"}[n]
                stages.append(Router(k, tag + "_rt", I[layer + wg], 4 + n // 2, I["L3_ffn_bg"] if n == 7 else None))
                if n in (1, 7):
                    stages.append(GateBias(k, tag + "_gb", I[layer + {1: "be", 7: "b2"}[n]]))
            if n == 1:
                stages.append(LinearExperts(k, tag + "_ex", I["L0_ffn_We"]))
            if n == 3:
                stages.append(Experts(k, tag + "_ex", "glu", I["L1_ffn_up_proj"], I["L1_ffn_down_proj"]))
            if n == 5:
                stages.append(Experts(k, tag + "_ex", "silu", I["L2_ffn_w1"], I["L2_ffn_w2"]))
            if n == 7:
                stages.append(Experts(k, tag + "_ex", "relu", I["L3_ffn_W1"], I["L3_ffn_W2"], I["L3_ffn_b1"]))
    stages.append(Store(k))
    return stages


def flamingo_stack(nc, ins, out):
    with ExitStack() as ctx:
        k = Kernel(nc, ctx, ins, out)
        stages = make_stages(k)
        block = ctx.enter_context(nc.Block())

        def between(eng, name, n):
            eng.drain().then_inc(k.over[name], 1)
            for other, over in k.over.items():
                eng.wait_ge(over, n + 1)

        @block.sync
        def _(sp):
            for n, stage in enumerate(stages):
                if n:
                    for sem in stages[n - 1].sems:
                        sp.sem_clear(sem)
                stage.sync(sp)
                between(sp, "sp", n)

        @block.gpsimd
        def _(pool):
            for n, stage in enumerate(stages):
                stage.gpsimd(pool)
                between(pool, "pool", n)

        @block.scalar
        def _(act):
            for n, stage in enumerate(stages):
                stage.scalar(act)
                between(act, "act", n)

        @block.vector
        def _(dve):
            for n, stage in enumerate(stages):
                stage.vector(dve)
                between(dve, "dve", n)

        @block.tensor
        def _(pe):
            for n, stage in enumerate(stages):
                stage.tensor(pe)
                between(pe, "pe", n)


def laid_out(inputs):
    import numpy as _np

    T_ = lambda a, *d: _np.ascontiguousarray(_np.transpose(_np.asarray(a), d))
    keep = {n: _np.ascontiguousarray(a) for n, a in inputs.items()}
    keep["L1_ffn_router_w"] = T_(inputs["L1_ffn_router_w"], 1, 0)
    keep["L3_ffn_Wg"] = T_(inputs["L3_ffn_Wg"], 1, 0)
    keep["L3_ffn_W1"] = T_(inputs["L3_ffn_W1"], 0, 2, 1)
    keep["L3_ffn_W2"] = T_(inputs["L3_ffn_W2"], 0, 2, 1)
    for l in ("L0", "L3"):
        keep[l + "_gate_w"] = _np.ascontiguousarray(_np.concatenate(
            [_np.asarray(inputs[f"{l}_xattn_{g}gate_w"]).T for g in "if"], axis=1))
        keep[l + "_gate_b"] = _np.concatenate([_np.asarray(inputs[f"{l}_xattn_{g}gate_b"]) for g in "if"])
    keep["hopsT"] = T_(inputs["itok_SxS2_0_2016"], 1, 0)
    keep["ctxT"] = _np.ascontiguousarray(_np.asarray(inputs["ctx_1024"]).reshape(T, D).T)
    for n in [f"L1_xattn_w_{m}" for m in "qkvo"] + [f"L2_xattn_W{m}" for m in "qkvo"]:
        keep[n] = T_(inputs[n], 1, 0)
    for n in ("L1_xattn_b_q", "L1_xattn_b_k"):
        keep[n] = T_(_np.asarray(inputs[n]).reshape(2, 128), 1, 0)
    keep["L3_ffn_b1"] = T_(_np.asarray(inputs["L3_ffn_b1"]).reshape(8, 4, 128), 0, 2, 1)
    return keep


def kernel(**inputs):
    import numpy as _np
    import concourse.bacc as _bacc
    from concourse import mybir as _mybir
    from concourse.bass_utils import run_bass_kernel_spmd as _run

    nc = _bacc.Bacc("TRN2", target_bir_lowering=False, num_devices=1)
    arrays, ins = {}, {}
    for name, a in laid_out(inputs).items():
        arrays[f"in_{name}"] = a
        ins[name] = nc.dram_tensor(f"in_{name}", a.shape, _mybir.dt.from_np(a.dtype), kind="ExternalInput").ap()
    out = nc.dram_tensor("out", (8, 256, 256), F32, kind="ExternalOutput").ap()
    flamingo_stack(nc, ins, out)
    r = _run(nc, [arrays], core_ids=[0])
    return r.results[0]["out"]
```

```python
from contextlib import ExitStack, contextmanager

import concourse.bass as bass
from concourse import mybir

F32 = mybir.dt.float32
BF16 = mybir.dt.bfloat16
I32 = mybir.dt.int32
ALU = mybir.AluOpType
ACT = mybir.ActivationFunctionType
AX = mybir.AxisListType

P = 128
B, S, D = 8, 256, 256
T = B * S
NT = T // P
HALVES = S // P
KC = D // P
E = 8
LN_EPS = 1e-5
SLOT_TILES = 40
BIG = 1e30

SUBLAYERS = (0, 1, 2, 3, 4, 5, 6, 7)


def ds(start, size):
    return bass.ds(start, size)


class Chain:

    def __init__(self, eng, sem):
        self.eng, self.sem, self.base, self.n = eng, sem, 0, 0

    def start(self, base=0):
        self.base, self.n = base, 0

    def link(self, ins):
        self.n += 1
        ins.then_inc(self.sem, 1)
        self.eng.wait_ge(self.sem, self.base + self.n)


def wait_apart(eng, sem, value, passed):
    eng.wait_ge(sem, value)
    eng.sem_inc(passed, 1)


class Stage:

    def __init__(self, k):
        self.k, self.b, self.sems = k, k.b, []
        kind = type(self).__name__
        self.round = k.rounds[kind] = k.rounds.get(kind, -1) + 1

    def sem(self, name):
        s = self.k.shared_sem(f"{type(self).__name__}_{name}")
        self.sems.append(s)
        return s

    def lasting_sem(self, name):
        return self.k.shared_sem(f"{type(self).__name__}_{name}")

    def tensor(self, pe):
        pass

    def vector(self, dve):
        pass

    def scalar(self, act):
        pass

    def gpsimd(self, pool):
        pass

    def sync(self, sp):
        pass


class LayerNorm(Stage):

    GROUP = 4
    GROUPS = NT // GROUP

    def __init__(self, k, tag, weights=None):
        super().__init__(k)
        self.weights = weights
        self.stats_done = self.sem("stats_done")
        self.own = self.sem("chain")
        self.inv_ready = self.sem("inv_ready")
        self.rstd_ready = self.sem("rstd_ready")
        self.normed = self.sem("normed")
        self.transposed = self.sem("transposed")
        self.copied0 = self.sem("copied0")
        self.copied1 = self.sem("copied1")

    def sync(self, sp):
        for dst, src in self.weights or ():
            sp.dma_start(dst, src).then_inc(self.k.weights_landed, 16)

    def vector(self, dve):
        k, G = self.k, self.GROUP
        chain = Chain(dve, self.own)
        with dve.Fori(0, NT // G) as i:
            for j in range(G):
                dve.bn_stats(self.b.ln_stats[:, ds(i * G * 6 + j * 6, 6)],
                             k.x[:, ds(i * G * D + j * D, D)]).then_inc(self.stats_done, 1)
        dve.wait_ge(self.stats_done, NT)
        for t in range(NT):
            ins = dve.bn_aggr(self.b.ln_mv[:, t, :], self.b.ln_stats[:, t * 6:(t + 1) * 6])
        chain.link(ins)
        chain.link(dve.tensor_scalar(self.b.ln_inv[:], self.b.ln_mv[:, :, 1], LN_EPS, None, ALU.add))
        dve.reciprocal(self.b.ln_inv[:], self.b.ln_inv[:]).then_inc(self.inv_ready, 1)
        chain.link(dve.tensor_copy(self.b.ln_mean[:], self.b.ln_mv[:, :, 0]))
        dve.wait_ge(self.rstd_ready, 1)
        for g in range(self.GROUPS):
            if g >= len(self.b.ln_x):
                dve.wait_ge(self.transposed, g - len(self.b.ln_x) + 1)
            for j in range(G):
                t = g * G + j
                ins = dve.tensor_scalar(self.b.ln_x[g % len(self.b.ln_x)][:, j, :], k.x[:, t * D:(t + 1) * D],
                                        self.b.ln_mean[:, t:t + 1], self.b.ln_rstd[:, t:t + 1], ALU.subtract, ALU.mult)
            ins.then_inc(self.normed, 1)
            if g:
                self.lnT_out(dve, dve.tensor_copy, 1, g - 1, self.copied1)
        self.lnT_out(dve, dve.tensor_copy, 1, self.GROUPS - 1, self.copied1)

    def lnT_out(self, eng, copy_, c, g, copied):
        k, W = self.k, self.GROUP * P
        eng.wait_ge(self.transposed, g + 1)
        copy_(k.lnT[:, c * T + g * W:c * T + (g + 1) * W], k.bank[2 * (g % 2) + c][:]).then_inc(copied, 1)

    def scalar(self, act):
        k = self.k
        act.wait_ge(self.inv_ready, 1)
        act.activation(self.b.ln_rstd[:], self.b.ln_inv[:], ACT.Sqrt).then_inc(self.rstd_ready, 1)
        for g in range(self.GROUPS):
            self.lnT_out(act, act.copy, 0, g, self.copied0)

    def tensor(self, pe):
        k, G = self.k, self.GROUP
        for g in range(self.GROUPS):
            if g >= 2:
                pe.wait_ge(self.copied0, g - 1)
                pe.wait_ge(self.copied1, g - 1)
            pe.wait_ge(self.normed, g + 1)
            for c in range(KC):
                for j in range(G):
                    ins = pe.transpose(k.bank[2 * (g % 2) + c][:, j * P:(j + 1) * P],
                                       self.b.ln_x[g % len(self.b.ln_x)][:, j, c * P:(c + 1) * P], k.ident[:])
            ins.then_inc(self.transposed, 1)


class Router(Stage):

    def __init__(self, k, tag, wg, g, bias=None):
        super().__init__(k)
        self.wg_dram, self.g, self.bias_dram = wg, g, bias
        self.loaded = self.sem("loaded")
        self.logits_ready = self.sem("logits_ready")
        self.own = self.sem("chain")
        self.diff_ready = self.sem("diff_ready")
        self.exp_ready = self.sem("exp_ready")

    def sync(self, sp):
        k = self.k
        sp.dma_start(self.b.wg[:], self.wg_dram.rearrange("(c p) e -> p c e", p=P)).then_inc(self.loaded, 16)
        if self.bias_dram is not None:
            sp.dma_start(self.b.bg[:], self.bias_dram.partition_broadcast(P)).then_inc(self.loaded, 16)

    def tensor(self, pe):
        k = self.k
        pe.wait_ge(self.loaded, 16 * (1 + (self.bias_dram is not None)))
        for t in range(NT):
            for c in range(KC):
                ins = pe.matmul(k.bank[0][:, t * E:(t + 1) * E], k.lnT[:, c * T + t * P:c * T + (t + 1) * P],
                                self.b.wg[:, c, :], start=c == 0, stop=c == KC - 1)
        ins.then_inc(self.logits_ready, 1)

    def vector(self, dve):
        k = self.k
        full = [P, NT, E]
        over_e = lambda a: a.unsqueeze(2).to_broadcast(full)
        over_t = lambda a: a.unsqueeze(1).to_broadcast(full)
        chain = Chain(dve, self.own)
        logits = self.b.rt[:, 0]
        eq, key, sel1, sel2 = self.b.rt[:, 1], self.b.rt[:, 2], self.b.rt[:, 3], self.b.rt[:, 4]
        m1, m2, kmax, diff, w1, w2 = (self.b.rs[:, n] for n in range(6))
        ps = k.bank[0][:, 0:NT * E].rearrange("p (t e) -> p t e", e=E)
        dve.wait_ge(self.logits_ready, 1)
        if self.bias_dram is not None:
            chain.link(dve.tensor_tensor(logits, ps, over_t(self.b.bg[:]), ALU.add))
        else:
            chain.link(dve.tensor_copy(logits, ps))
        for m, sel, nxt in ((m1, sel1, key), (m2, sel2, None)):
            left = logits if nxt is not None else self.b.rt[:, 5]
            chain.link(dve.tensor_reduce(m, left, AX.X, ALU.max))
            chain.link(dve.tensor_tensor(eq, left, over_e(m), ALU.is_equal))
            chain.link(dve.tensor_tensor(key, eq, over_t(k.rank[:]), ALU.mult))
            chain.link(dve.tensor_reduce(kmax, key, AX.X, ALU.max))
            chain.link(dve.tensor_tensor(sel, key, over_e(kmax), ALU.is_equal))
            if nxt is not None:
                chain.link(dve.scalar_tensor_tensor(out=self.b.rt[:, 5], in0=sel, scalar=-BIG, in1=logits,
                                                    op0=ALU.mult, op1=ALU.add))
        dve.tensor_tensor(diff, m2, m1, ALU.subtract).then_inc(self.diff_ready, 1)
        dve.wait_ge(self.exp_ready, 1)
        chain.link(dve.tensor_scalar(w1, self.b.rexp[:], 1.0, None, ALU.add))
        chain.link(dve.reciprocal(w1, w1))
        chain.link(dve.tensor_scalar(w1, w1, k.tanh_g[:, self.g:self.g + 1], None, ALU.mult))
        chain.link(dve.tensor_tensor(w2, self.b.rexp[:], w1, ALU.mult))
        chain.link(dve.tensor_tensor(eq, sel1, over_e(w1), ALU.mult))
        chain.link(dve.tensor_tensor(key, sel2, over_e(w2), ALU.mult))
        chain.link(dve.tensor_tensor(self.b.gate3, eq, key, ALU.add))

    def scalar(self, act):
        k = self.k
        act.wait_ge(self.diff_ready, 1)
        act.activation(self.b.rexp[:], self.b.rs[:, 3], ACT.Exp).then_inc(self.exp_ready, 1)


class GateBias(Stage):

    def __init__(self, k, tag, bias):
        super().__init__(k)
        self.bias_dram = bias
        self.loaded = self.sem("loaded")
        self.turned = self.sem("turned")
        self.gate_ready = self.sem("gate_ready")
        self.y_ready = self.sem("y_ready")
        self.added = self.sem("added")

    def sync(self, sp):
        sp.dma_start(self.b.ebias[:], self.bias_dram).then_inc(self.loaded, 16)

    def tensor(self, pe):
        k = self.k
        for t in range(NT):
            ins = pe.transpose(k.bank[t // 4][0:E, (t % 4) * P:(t % 4 + 1) * P], self.b.gate[:, t * E:(t + 1) * E], k.ident[:])
        ins.then_inc(self.turned, 1)
        pe.wait_ge(self.gate_ready, 4)
        pe.wait_ge(self.loaded, 16)
        for t in range(NT):
            if t >= 4:
                pe.wait_ge(self.added, t - 3)
            pe.matmul(k.bank[4 + t % 4][:, 0:D], self.b.gateT[:, t * P:(t + 1) * P], self.b.ebias[:],
                      start=True, stop=True).then_inc(self.y_ready, 1)

    def vector(self, dve):
        k = self.k
        dve.wait_ge(self.turned, 1)
        for n in range(4):
            dve.tensor_copy(self.b.gateT[:, n * 4 * P:(n + 1) * 4 * P], k.bank[n][0:E, :]).then_inc(self.gate_ready, 1)
        for t in range(NT):
            dve.wait_ge(self.y_ready, t + 1)
            dve.tensor_tensor(k.x[:, t * D:(t + 1) * D], k.bank[4 + t % 4][:, 0:D], k.x[:, t * D:(t + 1) * D],
                              ALU.add).then_inc(self.added, 1)


class LinearExperts(Stage):

    RING = 8

    def __init__(self, k, tag, we):
        super().__init__(k)
        self.we = we.rearrange("e (c p) h -> e p c h", p=P)
        self.landed = [self.sem(f"landed{u}") for u in range(2)]
        self.used = self.sem("used")
        self.y_ready = self.sem("y_ready")
        self.added = self.sem("added")
        self.col = self.sem("col")
        self.up = [k.scoped(f"{tag}_up{u}", [P, KC, D], F32) for u in range(2)]
        self.gcol = [k.scoped(f"{tag}_gcol{u}", [P, NT], F32) for u in range(2)]

    def sync(self, sp):
        for u in range(2):
            sp.dma_start(self.up[u][:], self.we[u]).then_inc(self.landed[u], 16)
        with sp.Fori(1, E // 2) as i:
            for u in range(2):
                sp.wait_ge(self.used, i * 2 + (u - 1))
                sp.dma_start(self.up[u][:], self.we[ds(i * 2 + u, 1)].rearrange("e p c h -> (e p) c h")).then_inc(self.landed[u], 16)

    def tensor(self, pe):
        k = self.k

        def expert(e, round_, u, first):
            pe.wait_ge(self.landed[u], round_ * 16 + 16)
            for t in range(NT):
                if not (first and t < self.RING):
                    pe.wait_ge(self.added, e * NT + (t - self.RING + 1))
                for c in range(KC):
                    ins = pe.matmul(k.bank[t % self.RING][:, 0:D], k.lnT[:, c * T + t * P:c * T + (t + 1) * P],
                                    self.up[u][:, c, :], start=c == 0, stop=c == KC - 1)
                if t < NT - 1:
                    ins.then_inc(self.y_ready, 1)
            ins.then_inc(self.y_ready, 1)
            pe.wait_ge(self.y_ready, e * NT + NT)
            pe.sem_inc(self.used, 1)

        for u in range(2):
            expert(u, 0, u, u == 0)
        with pe.Fori(1, E // 2) as i:
            for u in range(2):
                expert(i * 2 + u, i, u, False)

    def vector(self, dve):
        k = self.k
        with dve.Fori(0, E // 2) as i:
            for u in range(2):
                e = i * 2 + u
                dve.tensor_copy(self.gcol[u][:].unsqueeze(2), self.b.gate3[:, :, ds(e, 1)]).then_inc(self.col, 1)
                dve.wait_ge(self.col, e + 1)
                for t in range(NT):
                    dve.wait_ge(self.y_ready, e * NT + (t + 1))
                    dve.scalar_tensor_tensor(out=k.x[:, t * D:(t + 1) * D], in0=k.bank[t % self.RING][:, 0:D],
                                             scalar=self.gcol[u][:, t:t + 1], in1=k.x[:, t * D:(t + 1) * D],
                                             op0=ALU.mult, op1=ALU.add).then_inc(self.added, 1)


class Dispatch(Stage):

    def __init__(self, k, tag):
        super().__init__(k)
        S_ = self.sem
        self.own, self.m_ready, self.counted = S_("chain"), S_("m_ready"), S_("counted")
        self.slots_ready, self.scattered = S_("slots_ready"), self.lasting_sem("scattered")
        sb = k.scoped
        self.m = sb(tag + "_m", [P, NT * E], BF16)
        self.tot, self.cum, self.cex = (sb(f"{tag}_{n}", [P, E, NT], F32) for n in ("tot", "cum", "cex"))
        self.slot = sb(tag + "_slot", [P, NT, E], F32)
        self.pick = sb(tag + "_pick", [P, 2, NT, E], F32)
        self.slotf = sb(tag + "_slotf", [P, 2, NT], F32)
        self.n, self.tend, self.adj, self.nt = (sb(f"{tag}_{n}", [P, E], F32) for n in ("n", "tend", "adj", "nt"))
        self.ni = sb(tag + "_ni", [P, E], I32)
        self.le = sb(tag + "_le", [1, SLOT_TILES, E], F32)
        self.ef = sb(tag + "_ef", [1, SLOT_TILES], F32)

    def tensor(self, pe):
        k = self.k
        pe.wait_ge(self.m_ready, 1)
        pe.matmul(k.bank[0][:, 0:NT * E], k.before_bf[:], self.m[:], start=True, stop=True)
        pe.matmul(k.bank[1][:, 0:NT * E], k.ones_bf[:], self.m[:], start=True, stop=True).then_inc(self.counted, 1)

    def vector(self, dve):
        k = self.k
        chain = Chain(dve, self.own)
        sel = [self.b.rt[:, 3], self.b.rt[:, 4]]
        over_t = lambda a: a.unsqueeze(1).to_broadcast([P, NT, E])
        dve.tensor_tensor(self.m[:].rearrange("p (t e) -> p t e", e=E), sel[0], sel[1], ALU.add).then_inc(self.m_ready, 1)
        dve.wait_ge(self.counted, 1)
        chain.link(dve.tensor_copy(self.tot[:], k.bank[1][:, 0:NT * E].rearrange("p (t e) -> p e t", e=E)))
        flat = lambda a: a[:].rearrange("p e t -> p (e t)")
        chain.link(dve.tensor_tensor_scan(flat(self.cum), k.ones_f[:], flat(self.tot), 0.0, ALU.mult, ALU.add))
        chain.link(dve.tensor_tensor(self.cex[:], self.cum[:], self.tot[:], ALU.subtract))
        chain.link(dve.tensor_tensor(self.n[:], self.cum[:, :, NT - 1], self.cex[:, :, 0], ALU.subtract))
        chain.link(dve.tensor_scalar(self.ni[:], self.n[:], float(P - 1), None, ALU.add))
        chain.link(dve.tensor_scalar(self.ni[:], self.ni[:], 7, None, ALU.arith_shift_right))
        chain.link(dve.tensor_copy(self.nt[:], self.ni[:]))
        chain.link(dve.tensor_tensor_scan(self.tend[:], k.ones_f[:, 0:E], self.nt[:], 0.0, ALU.mult, ALU.add))
        chain.link(dve.tensor_tensor(self.adj[:], self.tend[:], self.nt[:], ALU.subtract))
        chain.link(dve.scalar_tensor_tensor(out=self.adj[:], in0=self.adj[:], scalar=float(P), in1=self.cex[:, :, 0],
                                            op0=ALU.mult, op1=ALU.subtract))
        before = k.bank[0][:, 0:NT * E].rearrange("p (t e) -> p t e", e=E)
        chain.link(dve.tensor_tensor(self.slot[:], before, self.cex[:].rearrange("p e t -> p t e"), ALU.add))
        chain.link(dve.tensor_tensor(self.slot[:], self.slot[:], over_t(self.adj[:]), ALU.add))
        for c in range(2):
            ins = dve.tensor_tensor(self.pick[:, c], self.slot[:], sel[c], ALU.mult)
        chain.link(ins)
        chain.link(dve.tensor_reduce(self.slotf[:], self.pick[:], AX.X, ALU.add))
        dve.tensor_copy(k.slots[:], self.slotf[:]).then_inc(self.slots_ready, 1)
        full = [1, SLOT_TILES, E]
        chain.link(dve.tensor_tensor(self.le[:], self.tend[0:1, :].unsqueeze(1).to_broadcast(full),
                                     k.tile_row[:].unsqueeze(2).to_broadcast(full), ALU.is_le))
        chain.link(dve.tensor_reduce(self.ef[:], self.le[:], AX.X, ALU.add))
        dve.tensor_scalar(k.tile_expert[:], self.ef[:], float(E - 1), None, ALU.min)

    def gpsimd(self, pool):
        k = self.k
        pool.wait_ge(k.slots_zeroed, 16)
        pool.wait_ge(self.slots_ready, 1)
        for t in range(NT):
            for c in range(2):
                pool.indirect_dma_start(k.slot_x, bass.IndirectOffsetOnAxis(ap=k.slots[:, c, t:t + 1], axis=0),
                                        self.b.ln_x[t // 4][:, t % 4, :], None).then_inc(self.scattered, 16)
        pool.wait_ge(self.scattered, (self.round + 1) * 16 * 2 * NT)


class ExpertTiles(Stage):

    U = 4

    def __init__(self, k, tag, kind, UF, HF):
        super().__init__(k)
        self.kind, self.UF, self.HF = kind, UF, HF
        self.weights_due = k.weights_due
        S_ = self.sem
        self.x_landed = [S_(f"x_landed{r}") for r in range(4)]
        self.tx_done, self.xT_out, self.up_done = S_("tx_done"), S_("xT_out"), S_("up_done")
        self.silu_ready, self.h_out, self.th_done, self.hT_out = S_("silu_ready"), S_("h_out"), S_("th_done"), S_("hT_out")
        self.dn_done, self.y_out = S_("dn_done"), S_("y_out")
        self.stored = [self.lasting_sem(f"stored{u}") for u in range(2)]
        self.stored_before = self.round * 16 * SLOT_TILES // 2
        sb = k.scoped
        self.xs = [sb(f"{tag}_xs{r}", [P, D], F32) for r in range(4)]
        self.xT = [sb(f"{tag}_xT{u}", [P, KC * P], F32) for u in range(2)]
        self.h = [sb(f"{tag}_h{u}", [P, HF * P], F32) for u in range(2)]
        self.hT = [sb(f"{tag}_hT{u}", [P, HF * P], F32) for u in range(2)]
        self.s = [sb(f"{tag}_s{u}", [P, HF * P], F32) for u in range(2)] if kind == "glu" else None
        self.y = [sb(f"{tag}_y{u}", [P, D], F32) for u in range(2)]

    def quads(self, eng, body):
        body(0, True, False)
        with eng.Fori(1, SLOT_TILES // self.U - 1) as i:
            body(i, False, False)
        body(SLOT_TILES // self.U - 1, False, True)

    def steps(self, i, first, last, lags):
        for n in range(self.U + (3 if last else 0)):
            for at, lag in enumerate(lags):
                m = n - lag
                if m >= self.U or (m < 0 and first):
                    continue
                yield at, (i if m >= 0 else i - 1), m % self.U

    def sync(self, sp):
        k = self.k
        rows = k.slot_x.rearrange("(j p) d -> j p d", p=P)
        with sp.Fori(0, SLOT_TILES // self.U) as i:
            for r in range(self.U):
                sp.wait_ge(self.tx_done, i * 4 + (r + 1))
                sp.dma_start(self.xs[r][:], rows[ds(i * 4 + r, 1)].rearrange("j p d -> (j p) d")).then_inc(self.x_landed[r], 16)

    def tensor(self, pe):
        k = self.k
        pe.sem_inc(self.tx_done, 4)
        pe.sem_inc(self.up_done, 2)
        pe.sem_inc(self.th_done, 2)
        pe.sem_inc(self.dn_done, 2)
        pe.wait_ge(k.weights_landed, self.weights_due)

        def expert(i, r):
            if isinstance(i, int):
                return pe.value_load(k.tile_expert[0:1, i * 4 + r:i * 4 + r + 1], min_val=0, max_val=E - 1)
            return pe.value_load(k.tile_expert[0:1, ds(i * 4 + r, 1)], min_val=0, max_val=E - 1)

        def turn_x(i, r):
            pe.wait_ge(self.x_landed[r], i * 16 + 16)
            pe.wait_ge(self.xT_out, i * 4 + (r + 1))
            for c in range(KC):
                ins = pe.transpose(k.bank[r % 2][:, c * P:(c + 1) * P], self.xs[r][:, c * P:(c + 1) * P], k.ident[:])
            ins.then_inc(self.tx_done, 1)

        def up(i, r):
            e = expert(i, r)
            pe.wait_ge(self.xT_out, i * 4 + (r + 3))
            pe.wait_ge(self.h_out, i * 4 + (r + 1))
            F = self.UF * P
            for c in range(KC):
                ins = pe.matmul(k.bank[2 + r % 2][:, 0:F], self.xT[r % 2][:, c * P:(c + 1) * P],
                                self.b.w_up[:, ds(e * (KC * F) + c * F, F)], start=c == 0, stop=c == KC - 1)
            ins.then_inc(self.up_done, 1)

        def turn_h(i, r):
            pe.wait_ge(self.h_out, i * 4 + (r + 3))
            pe.wait_ge(self.hT_out, i * 4 + (r + 1))
            for f in range(self.HF):
                ins = pe.transpose(k.bank[4 + r % 2][:, f * P:(f + 1) * P], self.h[r % 2][:, f * P:(f + 1) * P], k.ident[:])
            ins.then_inc(self.th_done, 1)

        def down(i, r):
            e = expert(i, r)
            pe.wait_ge(self.hT_out, i * 4 + (r + 3))
            pe.wait_ge(self.y_out, i * 4 + (r + 1))
            for f in range(self.HF):
                ins = pe.matmul(k.bank[6 + r % 2][:, 0:D], self.hT[r % 2][:, f * P:(f + 1) * P],
                                self.b.w_down[:, ds(e * (self.HF * D) + f * D, D)], start=f == 0, stop=f == self.HF - 1)
            ins.then_inc(self.dn_done, 1)

        def body(i, first, last):
            for at, gi, r in self.steps(i, first, last, (0, 1, 2, 3)):
                (turn_x, up, turn_h, down)[at](gi, r)

        self.quads(pe, body)

    def scalar(self, act):
        k = self.k
        act.sem_inc(self.xT_out, 2)
        act.sem_inc(self.hT_out, 2)

        def xT(i, r):
            act.wait_ge(self.tx_done, i * 4 + (r + 5))
            act.wait_ge(self.up_done, i * 4 + (r + 1))
            act.copy(self.xT[r % 2][:], k.bank[r % 2][:, 0:KC * P]).then_inc(self.xT_out, 1)

        def silu(i, r):
            if self.kind != "glu":
                return
            act.wait_ge(self.up_done, i * 4 + (r + 3))
            act.wait_ge(self.h_out, i * 4 + (r + 1))
            act.activation(self.s[r % 2][:], k.bank[2 + r % 2][:, 0:self.HF * P], ACT.Silu).then_inc(self.silu_ready, 1)

        def hT(i, r):
            act.wait_ge(self.th_done, i * 4 + (r + 3))
            act.wait_ge(self.dn_done, i * 4 + (r + 1))
            func = {"glu": ACT.Copy, "silu": ACT.Silu, "relu": ACT.Relu}[self.kind]
            act.activation(self.hT[r % 2][:], k.bank[4 + r % 2][:, 0:self.HF * P], func).then_inc(self.hT_out, 1)

        def body(i, first, last):
            for at, gi, r in self.steps(i, first, last, (0, 1, 2)):
                (xT, silu, hT)[at](gi, r)

        self.quads(act, body)

    def vector(self, dve):
        k = self.k
        dve.sem_inc(self.h_out, 2)
        dve.sem_inc(self.y_out, 2)
        W = self.HF * P

        def h(i, r):
            ps = k.bank[2 + r % 2]
            if self.kind == "relu":
                at = ds(i * 4 + r, 1) if not isinstance(i, int) else slice(i * 4 + r, i * 4 + r + 1)
                e = dve.value_load(k.tile_expert[0:1, at], min_val=0, max_val=E - 1)
            dve.wait_ge(self.th_done, i * 4 + (r + 1))
            dve.wait_ge(self.up_done, i * 4 + (r + 3))
            if self.kind == "glu":
                dve.wait_ge(self.silu_ready, i * 4 + (r + 1))
                ins = dve.tensor_tensor(self.h[r % 2][:], self.s[r % 2][:], ps[:, W:2 * W], ALU.mult)
            elif self.kind == "relu":
                ins = dve.tensor_tensor(self.h[r % 2][:], ps[:, 0:W], self.b.b1_all[:, ds(e * W, W)], ALU.add)
            else:
                ins = dve.tensor_copy(self.h[r % 2][:], ps[:, 0:W])
            ins.then_inc(self.h_out, 1)

        def y(i, r):
            if not (isinstance(i, int) and i == 0 and r < 2):
                dve.wait_ge(self.stored[r % 2], i * 32 + (self.stored_before + 16 * (r // 2)))
            dve.wait_ge(self.dn_done, i * 4 + (r + 3))
            dve.tensor_copy(self.y[r % 2][:], k.bank[6 + r % 2][:, 0:D]).then_inc(self.y_out, 1)

        def body(i, first, last):
            for at, gi, r in self.steps(i, first, last, (1, 3)):
                (h, y)[at](gi, r)

        if self.kind == "relu":
            dve.wait_ge(k.weights_landed, self.weights_due)
        self.quads(dve, body)

    def gpsimd(self, pool):
        k = self.k
        rows = k.slot_y.rearrange("(j p) d -> j p d", p=P)
        with pool.Fori(0, SLOT_TILES // self.U) as i:
            for r in range(self.U):
                wait_apart(pool, self.y_out, i * 4 + (r + 3), k.passed)
                pool.dma_start(rows[ds(i * 4 + r, 1)].rearrange("j p d -> (j p) d"), self.y[r % 2][:]).then_inc(self.stored[r % 2], 16)
        for u in range(2):
            pool.wait_ge(self.stored[u], self.stored_before + 16 * SLOT_TILES // 2)


class Combine(Stage):

    def __init__(self, k, tag):
        super().__init__(k)
        self.gathered = [self.lasting_sem(f"gathered{n}") for n in range(NT // 2)]
        self.own = self.sem("chain")
        self.rows = [[k.scoped(f"{tag}_rows{c}{t}", [P, D], F32) for t in range(NT)] for c in range(2)]

    def gpsimd(self, pool):
        k = self.k
        for t in range(NT):
            for c in range(2):
                pool.indirect_dma_start(self.rows[c][t][:], None, k.slot_y,
                                        bass.IndirectOffsetOnAxis(ap=k.slots[:, c, t:t + 1], axis=0)
                                        ).then_inc(self.gathered[t // 2], 16)

    def vector(self, dve):
        k = self.k
        for n in range(NT // 2):
            dve.wait_ge(self.gathered[n], (self.round + 1) * 64)
            for c in range(2):
                for t in (2 * n, 2 * n + 1):
                    x = k.x[:, t * D:(t + 1) * D]
                    ins = dve.scalar_tensor_tensor(out=x, in0=self.rows[c][t][:], scalar=self.b.rs[:, 4 + c, t:t + 1], in1=x,
                                                   op0=ALU.mult, op1=ALU.add)
                    ins.then_inc(self.own, 1)
                if c == 0:
                    dve.wait_ge(self.own, n * 4 + 2)


class Attention(Stage):

    H, DH = 16, 16
    HC = P // DH
    U = H // 2

    def __init__(self, k, tag, g, causal, wq, wk, wv, wo, bo, bq=None, bk=None, bv=None):
        super().__init__(k)
        self.g, self.causal = g, causal
        self.w = (wq, wk, wv, wo)
        self.biases = (bq, bk, bv, bo)
        self.bias = bq is not None
        self.qscale = 0.25 if causal else 0.0625
        S_ = self.sem
        self.w_landed = S_("w_landed")
        self.ctx_landed = [S_(f"ctx_landed{u}") for u in range(2)]
        self.proj_ready = S_("proj_ready")
        self.k_ready, self.q_ready, self.v_ready = S_("k_ready"), S_("q_ready"), S_("v_ready")
        self.km_ready, self.v_zeroed = S_("km_ready"), S_("v_zeroed")
        self.scores_ready = S_("scores_ready")
        self.max_ready, self.exp_ready = S_("max_ready"), S_("exp_ready")
        self.rsum_ready, self.scaled, self.turned = S_("rsum_ready"), S_("scaled"), S_("turned")
        self.pt_ready = [S_(f"pt_ready{m}") for m in range(2)]
        self.pv_done = S_("pv_done")
        self.ot_ready, self.y_ready, self.added = S_("ot_ready"), S_("y_ready"), S_("added")
        sb = k.scoped
        self.wt = [sb(f"{tag}_w{n}", [P, KC, D], F32) for n in range(4)]
        self.bqk = sb(tag + "_bqk", [P, 2, KC], F32)
        self.bvb = sb(tag + "_bvb", [P, D], F32)
        self.bo = sb(tag + "_bo", [1, D], F32)
        self.cT = [sb(f"{tag}_cT{u}", [P, KC, S], F32) for u in range(2)]
        self.kT = sb(f"{tag}_kT", [P, KC * S], F32)
        self.km = [sb(f"{tag}_km{u}", [P, KC, self.HC, S], F32) for u in range(2)]
        self.qT = [sb(f"{tag}_qT{u}", [P, KC * S], F32) for u in range(2)]
        self.v = [[sb(f"{tag}_v{u}{m}", [P, HALVES, D], F32) for m in range(2)] for u in range(2)]
        self.p = [sb(f"{tag}_p{n}", [P, HALVES, 2, S], F32) for n in range(4)]
        self.pT = [sb(f"{tag}_pT{n}", [P, 2, HALVES * S], F32) for n in range(2)]
        self.nmax = [sb(f"{tag}_nmax{u}", [P, self.U * 4], F32) for u in range(2)]
        self.sum = [sb(f"{tag}_sum{u}", [P, self.U * 4], F32) for u in range(2)]
        self.oT = sb(tag + "_oT", [P, KC * S], F32)
        self.n_loads = 5 + 3 * self.bias

    def width(self, s):
        return (s + 1) * P if self.causal else S

    def blocks(self):
        for t in range(HALVES):
            first = t if self.causal else 0
            for s in range(first, HALVES):
                yield t, s, t * S + (s - first) * P

    def sync(self, sp):
        k = self.k
        for wt, w in zip(self.wt, self.w):
            sp.dma_start(wt[:], w.rearrange("(c p) f -> p c f", p=P)).then_inc(self.w_landed, 16)
        bq, bk, bv, bo = self.biases
        sp.dma_start(self.bo[:], bo.unsqueeze(0)).then_inc(self.w_landed, 16)
        if self.bias:
            sp.dma_start(self.bqk[:, 0, :], bq).then_inc(self.w_landed, 16)
            sp.dma_start(self.bqk[:, 1, :], bk).then_inc(self.w_landed, 16)
            sp.dma_start(self.bvb[:], bv.partition_broadcast(P)).then_inc(self.w_landed, 16)
        ctxT = k.ins["ctxT"].rearrange("(c p) t -> p c t", p=P)
        with sp.Fori(0, B // 2) as i:
            for u in range(2):
                sp.wait_ge(self.proj_ready, i * 6 + 3 * u + 1)
                sp.dma_start(self.cT[u][:], ctxT[:, :, ds(i * 2 * S + u * S, S)]).then_inc(self.ctx_landed[u], 16)

    def pairs(self, eng, body):
        body(0, True, False)
        with eng.Fori(1, B // 2 - 1) as i:
            body(i, False, False)
        body(B // 2 - 1, False, True)

    def lagged(self, i, n, lag, first):
        m = n - lag
        if m >= 0:
            return i, m // self.U, m % self.U
        return None if first else (i - 1, 1, self.U + m)

    def tensor(self, pe):
        k = self.k
        wq, wk, wv, wo = self.wt
        pe.sem_inc(self.proj_ready, 4)
        pe.sem_inc(self.scores_ready, 9)
        pe.sem_inc(self.turned, 4)
        pe.sem_inc(self.pv_done, 2)
        pe.sem_inc(self.y_ready, 1)
        pe.wait_ge(self.w_landed, 16 * self.n_loads)

        def proj_k(i, u):
            b = i * 2 + u
            pe.wait_ge(self.ctx_landed[u], i * 16 + 16)
            pe.wait_ge(self.added, b + 1)
            if not (isinstance(b, int) and b == 0):
                pe.wait_ge(self.v_ready, i * 4 + 2 * u)
            for f in range(KC):
                for c in range(KC):
                    ins = pe.matmul(k.bank[7][:, f * S:(f + 1) * S], wk[:, c, f * P:(f + 1) * P],
                                    self.cT[u][:, c, :], start=c == 0, stop=c == KC - 1)
            ins.then_inc(self.proj_ready, 1)

        def proj_q(i, u):
            pe.wait_ge(self.k_ready, i * 4 + (2 * u + 2))
            for f in range(KC):
                for c in range(KC):
                    ins = pe.matmul(k.bank[7][:, f * S:(f + 1) * S], wq[:, c, f * P:(f + 1) * P],
                                    k.lnT[:, ds(i * 2 * S + (c * T + u * S), S)], start=c == 0, stop=c == KC - 1)
            ins.then_inc(self.proj_ready, 1)

        def proj_v(i, u):
            pe.wait_ge(self.q_ready, i * 4 + (2 * u + 2))
            for t in range(HALVES):
                for c in range(KC):
                    ins = pe.matmul(k.bank[7][:, t * D:(t + 1) * D], self.cT[u][:, c, t * P:(t + 1) * P],
                                    wv[:, c, :], start=c == 0, stop=c == KC - 1)
            ins.then_inc(self.proj_ready, 1)

        def scores(i, u, r):
            n = (i * 2 + u) * self.U
            if r == 0:
                pe.wait_ge(self.q_ready, i * 4 + (2 * u + 2))
                pe.wait_ge(self.km_ready, i * 4 + (2 * u + 3))
            pe.wait_ge(self.exp_ready, n + (r + 1))
            c, hc = divmod(2 * r, self.HC)
            for s in range(HALVES):
                w = self.width(s)
                bank = k.bank[2 * (r % 2) + s][:].rearrange("p (m t) -> p m t", m=2)
                ins = pe.matmul(bank[:, :, 0:w], self.qT[u][:, c * S + s * P:c * S + (s + 1) * P],
                                self.km[u][:, c, hc:hc + 2, 0:w], start=True, stop=not self.causal)
                if self.causal:
                    ins = pe.matmul(bank[:, :, s * P:(s + 1) * P], k.ident_bf[:],
                                    k.causal_bf[:].unsqueeze(1).to_broadcast([P, 2, P]), start=False, stop=True)
                ins.then_inc(self.scores_ready, 1) if s == HALVES - 1 else None

        def turn(i, u, r):
            n = (i * 2 + u) * self.U
            pe.wait_ge(self.scaled, n + (r + 1))
            for m in range(2):
                pe.wait_ge(self.pt_ready[m], n + (r + 1))
                for t, s, at in self.blocks():
                    ins = pe.transpose(k.bank[4 + m][:, at:at + P], self.p[r % 4][:, s, m, t * P:(t + 1) * P], k.ident[:])
            ins.then_inc(self.turned, 1)

        def pv(i, u, r):
            n = (i * 2 + u) * self.U
            if r == 0:
                pe.wait_ge(self.v_ready, i * 4 + (2 * u + 2))
                pe.wait_ge(self.ot_ready, i * 2 + (u + 1))
            c, strip = divmod(r, 4)
            for m in range(2):
                pe.wait_ge(self.pt_ready[m], n + (r + 2))
                for t in range(HALVES):
                    w = S - t * P if self.causal else S
                    ins = pe.matmul(k.bank[6][32 * strip:32 * strip + 32, (c + 1) * S - w:(c + 1) * S],
                                    self.v[u][m][:, t, 32 * r:32 * r + 32], self.pT[r % 2][:, m, t * S:t * S + w],
                                    start=m == 0 and t == 0, stop=m == 1 and t == HALVES - 1)
            ins.then_inc(self.pv_done, 1)

        def out(i, u, last):
            pe.wait_ge(self.ot_ready, i * 2 + (u + 2))
            if last:
                pe.wait_ge(self.added, B - 1 + 3)
            else:
                pe.wait_ge(self.v_ready, i * 4 + (2 * u + 6))
            for s in range(HALVES):
                pe.matmul(k.bank[7][:, s * D:(s + 1) * D], k.ones_row, self.bo[:], start=True, stop=False)
                for c in range(KC):
                    ins = pe.matmul(k.bank[7][:, s * D:(s + 1) * D], self.oT[:, c * S + s * P:c * S + (s + 1) * P],
                                    wo[:, c, :], start=False, stop=c == KC - 1)
            ins.then_inc(self.y_ready, 1)

        def out6():
            pe.wait_ge(self.ot_ready, B)
            pe.wait_ge(self.v_ready, 2 * B)
            for s in range(HALVES):
                pe.matmul(k.bank[7][:, s * D:(s + 1) * D], k.ones_row, self.bo[:], start=True, stop=False)
                for c in range(KC):
                    ins = pe.matmul(k.bank[7][:, s * D:(s + 1) * D], self.oT[:, c * S + s * P:c * S + (s + 1) * P],
                                    wo[:, c, :], start=False, stop=c == KC - 1)
            ins.then_inc(self.y_ready, 1)

        def body(i, first, last):
            if first:
                proj_k(0, 0)
                proj_q(0, 0)
                proj_v(0, 0)
            for n in range(2 * self.U + (3 if last else 0)):
                u, r = divmod(n, self.U)
                if u < 2:
                    scores(i, u, r)
                for step, lag in ((turn, 2), (pv, 3)):
                    unit = self.lagged(i, n, lag, first)
                    if unit and unit[1] < 2:
                        step(*unit)
                if u == 2:
                    continue
                nxt = (i, 1) if u == 0 else (i + 1, 0)
                prev = (i, 0) if u else (i - 1, 1)
                if r in (1, 2, 3) and not (last and u == 1):
                    (proj_k, proj_q, proj_v)[r - 1](*nxt)
                if r == 4 and not (first and u == 0):
                    if last and u == 1:
                        out6()
                    else:
                        out(*prev, False)
            if last:
                out(i, 1, True)

        self.pairs(pe, body)

    def scalar(self, act):
        k = self.k
        act.sem_inc(self.exp_ready, 2)
        act.sem_inc(self.pt_ready[0], 1)
        act.sem_inc(self.ot_ready, 1)
        if self.bias:
            act.wait_ge(self.w_landed, 16 * self.n_loads)

        def k_out(i, u):
            act.wait_ge(self.proj_ready, i * 6 + (3 * u + 5))
            act.wait_ge(self.km_ready, i * 4 + (2 * u + 1))
            for c in range(KC):
                src, dst = k.bank[7][:, c * S:(c + 1) * S], self.kT[:, c * S:(c + 1) * S]
                if self.bias:
                    ins = act.activation(dst, src, ACT.Identity, bias=self.bqk[:, 1, c:c + 1])
                else:
                    ins = act.copy(dst, src)
                ins.then_inc(self.k_ready, 1)

        def exps(i, u, r):
            n = (i * 2 + u) * self.U
            act.wait_ge(self.max_ready, n + (r + 1))
            act.wait_ge(self.turned, n + (r + 1))
            for s in range(HALVES):
                w = self.width(s)
                for m in range(2):
                    col = r * 4 + s * 2 + m
                    ins = act.activation(self.p[r % 4][:, s, m, 0:w], k.bank[2 * (r % 2) + s][:, m * S:m * S + w], ACT.Exp,
                                         bias=self.nmax[u][:, col:col + 1], accum_out=self.sum[u][:, col:col + 1])
            ins.then_inc(self.exp_ready, 1)

        def o_out(i, u):
            act.wait_ge(self.pv_done, (i * 2 + u) * self.U + (self.U + 2))
            act.wait_ge(self.y_ready, i * 2 + (u + 1))
            act.copy(self.oT[:], k.bank[6][:]).then_inc(self.ot_ready, 1)

        def body(i, first, last):
            if first:
                k_out(0, 0)
            for n in range(2 * self.U + (3 if last else 0)):
                u, r = divmod(n, self.U)
                if u < 2:
                    exps(i, u, r)
                unit = self.lagged(i, n, 2, first)
                if unit and unit[1] < 2:
                    self.pt_out(act, act.copy, 0, *unit)
                if u == 2:
                    continue
                if r == 1 and not (last and u == 1):
                    k_out(*((i, 1) if u == 0 else (i + 1, 0)))
                if r == 3 and not (first and u == 0):
                    o_out(*((i, 0) if u else (i - 1, 1)))
            if last:
                o_out(i, 1)

        self.pairs(act, body)

    def pt_out(self, eng, copy, m, i, u, r):
        n = (i * 2 + u) * self.U
        w = S + P if self.causal else 2 * S
        eng.wait_ge(self.turned, n + (r + 5))
        eng.wait_ge(self.pv_done, n + (r + 1))
        copy(self.pT[r % 2][:, m, 0:w], self.k.bank[4 + m][:, 0:w]).then_inc(self.pt_ready[m], 1)

    def vector(self, dve):
        k = self.k
        dve.sem_inc(self.pt_ready[1], 1)
        dve.sem_inc(self.added, 3)
        dve.wait_ge(self.v_zeroed, 4)
        if self.bias:
            dve.wait_ge(self.w_landed, 16 * self.n_loads)

        def q_out(i, u):
            dve.wait_ge(self.proj_ready, i * 6 + (3 * u + 6))
            for c in range(KC):
                src, dst = k.bank[7][:, c * S:(c + 1) * S], self.qT[u][:, c * S:(c + 1) * S]
                if self.bias:
                    ins = dve.tensor_scalar(dst, src, self.bqk[:, 0, c:c + 1], self.qscale, ALU.add, ALU.mult)
                else:
                    ins = dve.tensor_scalar(dst, src, self.qscale, None, ALU.mult)
                ins.then_inc(self.q_ready, 1)

        def v_out(i, u):
            dve.wait_ge(self.proj_ready, i * 6 + (3 * u + 7))
            view = lambda a, m: a.rearrange("p (s h e d) -> p s h e d", s=HALVES, e=2, d=self.DH)[:, :, :, m, :]
            for m in range(2):
                dst = view(self.v[u][m][:].rearrange("p s d -> p (s d)"), m)
                if self.bias:
                    bias = self.bvb[:].rearrange("p (h e d) -> p h e d", e=2, d=self.DH)[:, :, m, :]
                    ins = [dve.tensor_tensor(dst[:, s], view(k.bank[7][:], m)[:, s], bias, ALU.add)
                           for s in range(HALVES)][-1]
                else:
                    ins = dve.tensor_copy(dst, view(k.bank[7][:], m))
                ins.then_inc(self.v_ready, 1)

        def maxes(i, u, r):
            n = (i * 2 + u) * self.U
            dve.wait_ge(self.scores_ready, n + (r + 10))
            for s in range(HALVES):
                col = r * 4 + s * 2
                ins = dve.tensor_reduce(self.nmax[u][:, col:col + 2],
                                        k.bank[2 * (r % 2) + s][:].rearrange("p (m t) -> p m t", m=2)[:, :, 0:self.width(s)],
                                        AX.X, ALU.max, negate=True)
            ins.then_inc(self.max_ready, 1)

        def recips(i, u, r):
            n = (i * 2 + u) * self.U
            dve.wait_ge(self.exp_ready, n + (r + 3))
            sums = self.sum[u][:, r * 4:r * 4 + 4]
            dve.reciprocal(sums, sums).then_inc(self.rsum_ready, 1)

        def add(i, u):
            dve.wait_ge(self.y_ready, i * 2 + (u + 2))
            dyn = i * 4 * D + u * 2 * D
            xb = k.x[:, ds(dyn, 2 * D)]
            dve.scalar_tensor_tensor(out=xb, in0=k.bank[7][:], scalar=k.tanh_g[:, self.g:self.g + 1], in1=xb,
                                     op0=ALU.mult, op1=ALU.add).then_inc(self.added, 1)

        def body(i, first, last):
            if first:
                q_out(0, 0)
                v_out(0, 0)
            for n in range(2 * self.U + (3 if last else 0)):
                u, r = divmod(n, self.U)
                if u < 2:
                    maxes(i, u, r)
                unit = self.lagged(i, n, 1, first)
                if unit and unit[1] < 2:
                    recips(*unit)
                unit = self.lagged(i, n, 2, first)
                if unit and unit[1] < 2:
                    self.pt_out(dve, dve.tensor_copy, 1, *unit)
                if u == 2:
                    continue
                nxt = (i, 1) if u == 0 else (i + 1, 0)
                if r == 2 and not (last and u == 1):
                    q_out(*nxt)
                if r == 3 and not (last and u == 1):
                    v_out(*nxt)
                if r == 5 and not (first and u == 0):
                    add(*((i, 0) if u else (i - 1, 1)))
            if last:
                add(i, 1)

        self.pairs(dve, body)

    def gpsimd(self, pool):
        k = self.k
        for u in range(2):
            for m in range(2):
                pool.memset(self.v[u][m][:], 0.0).then_inc(self.v_zeroed, 1)
        pool.sem_inc(self.km_ready, 1)

        def mask_k(i, u):
            pool.wait_ge(self.k_ready, i * 4 + (2 * u + 2))
            pool.wait_ge(self.scores_ready, i * 2 * self.U + (u * self.U + 1))
            full = [P, self.HC, S]
            for c in range(KC):
                pool.tensor_tensor(self.km[u][:, c], self.kT[:, c * S:(c + 1) * S].unsqueeze(1).to_broadcast(full),
                                   k.head16[:].unsqueeze(2).to_broadcast(full), ALU.mult).then_inc(self.km_ready, 1)

        def scale(i, u, r):
            n = (i * 2 + u) * self.U
            pool.wait_ge(self.rsum_ready, n + (r + 1))
            for s in range(HALVES):
                w = self.width(s)
                p = self.p[r % 4][:, s, :, 0:w]
                ins = pool.tensor_tensor(p, p, self.sum[u][:, r * 4 + s * 2:r * 4 + s * 2 + 2].unsqueeze(2)
                                         .to_broadcast([P, 2, w]), ALU.mult)
            ins.then_inc(self.scaled, 1)

        def body(i, first, last):
            if first:
                mask_k(0, 0)
            for n in range(2 * self.U + (3 if last else 0)):
                u, r = divmod(n, self.U)
                unit = self.lagged(i, n, 1, first)
                if unit and unit[1] < 2:
                    scale(*unit)
                if u < 2 and r == 1 and not (last and u == 1):
                    mask_k(*((i, 1) if u == 0 else (i + 1, 0)))

        self.pairs(pool, body)


class MlstmGates(Stage):

    def __init__(self, k, tag, NH, w, bias, shifted, cols, negm):
        super().__init__(k)
        self.NH, self.R, self.shifted = NH, B * NH, shifted
        self.w, self.bias, self.cols, self.negm = w, bias, cols, negm
        S_ = self.sem
        self.landed, self.logits_ready, self.own = S_("landed"), S_("logits_ready"), S_("chain")
        self.abs_ready, self.exp_ready, self.ln_ready = S_("abs_ready"), S_("exp_ready"), S_("ln_ready")
        self.g_ready, self.rows_turned = S_("g_ready"), S_("rows_turned")
        self.negm_ready, self.m_ready, self.en_ready = S_("negm_ready"), S_("m_ready"), S_("en_ready")
        self.cols_turned, self.negm_stored = S_("cols_turned"), S_("negm_stored")
        sb, R = k.scoped, self.R
        self.ctxT = sb(tag + "_ctxT", [P, KC * T], F32)
        self.wg = sb(tag + "_wg", [P, 3 * KC, 2 * NH], F32)
        self.bg = sb(tag + "_bg", [P, 2 * NH], F32)
        self.g = [sb(f"{tag}_g{n}", [P, HALVES * R], F32) for n in range(2)]
        self.t = sb(tag + "_t", [P, HALVES * R], F32)
        self.rows = sb(tag + "_rows", [R, 2 * S], F32)
        self.ones = sb(tag + "_ones", [R, S], F32)
        self.cs, self.a, self.M, self.m, self.nm, self.en = (sb(f"{tag}_{n}", [R, S], F32)
                                                             for n in ("cs", "a", "M", "m", "nm", "en"))

    def sync(self, sp):
        k = self.k
        sp.dma_start(self.wg[:], self.w.rearrange("(c p) g -> p c g", p=P)).then_inc(self.landed, 16)
        sp.dma_start(self.bg[:], self.bias.partition_broadcast(P)).then_inc(self.landed, 16)
        sp.dma_start(self.ctxT[:].rearrange("p (c t) -> p c t", c=KC),
                     k.ins["ctxT"].rearrange("(c p) t -> p c t", p=P)).then_inc(self.landed, 16)
        sp.wait_ge(self.negm_ready, 1)
        sp.dma_start(self.negm, self.nm[:]).then_inc(self.negm_stored, 16)
        sp.wait_ge(self.negm_stored, 16)

    def tensor(self, pe):
        k, R, G = self.k, self.R, 2 * self.NH
        pe.wait_ge(self.landed, 48)
        for t in range(NT):
            for n in range(3 * KC):
                src = k.lnT if n < KC else self.ctxT
                c = n % KC
                ins = pe.matmul(k.bank[0][:, t * G:(t + 1) * G], src[:, c * T + t * P:c * T + (t + 1) * P],
                                self.wg[:, n, :], start=n == 0, stop=n == 3 * KC - 1)
        ins.then_inc(self.logits_ready, 1)
        pe.wait_ge(self.g_ready, 2)
        for kind in range(2):
            for half in range(HALVES):
                n = kind * HALVES + half
                ins = pe.transpose(k.bank[1][0:R, n * P:(n + 1) * P], self.g[kind][:, half * R:(half + 1) * R], k.ident[:])
        ins.then_inc(self.rows_turned, 1)
        pe.wait_ge(self.negm_ready, 1)
        pe.wait_ge(self.en_ready, 1)
        for n, rows in enumerate((self.a, self.en)):
            for half in range(HALVES):
                at = (n * HALVES + half) * R
                ins = pe.transpose(k.bank[2][:, at:at + R], rows[:, half * P:(half + 1) * P], k.ident[0:R, 0:R])
        ins.then_inc(self.cols_turned, 1)

    def vector(self, dve):
        k, R, NH = self.k, self.R, self.NH
        chain = Chain(dve, self.own)
        dve.memset(self.ones[:], 1.0)
        dve.wait_ge(self.logits_ready, 1)
        ps = k.bank[0][:, 0:NT * 2 * NH].rearrange("p (b s k h) -> p s b k h", s=HALVES, k=2, h=NH)
        for kind in range(2):
            for half in range(HALVES):
                bias = self.bg[:, kind * NH:(kind + 1) * NH].unsqueeze(1).to_broadcast([P, B, NH])
                ins = dve.tensor_tensor(self.g[kind][:, half * R:(half + 1) * R].rearrange("p (b h) -> p b h", h=NH),
                                        ps[:, half, :, kind, :], bias, ALU.add)
                chain.link(ins)
        fg = self.g[1]
        dve.sem_inc(self.g_ready, 1)
        dve.wait_ge(self.ln_ready, 1)
        dve.scalar_tensor_tensor(out=fg[:], in0=fg[:], scalar=0.0, in1=self.t[:], op0=ALU.min,
                                 op1=ALU.subtract).then_inc(self.g_ready, 1)
        dve.wait_ge(self.rows_turned, 1)
        chain.link(dve.tensor_copy(self.rows[:], k.bank[1][0:R, :]))
        ig, lf = self.rows[:, 0:S], self.rows[:, S:2 * S]
        chain.link(dve.tensor_tensor_scan(self.cs[:], self.ones[:], lf, 0.0, ALU.mult, ALU.add))
        if self.shifted:
            dve.tensor_copy(self.a[:, 0:1], ig[:, 0:1])
            chain.link(dve.tensor_tensor(self.a[:, 1:S], ig[:, 1:S], self.cs[:, 0:S - 1], ALU.subtract))
        else:
            chain.link(dve.tensor_tensor(self.a[:], ig, self.cs[:], ALU.subtract))
        chain.link(dve.tensor_tensor_scan(self.M[:], self.ones[:], self.a[:], -3e38, ALU.mult, ALU.max))
        dve.tensor_tensor(self.m[:], self.cs[:], self.M[:], ALU.add).then_inc(self.m_ready, 1)
        dve.tensor_scalar(self.nm[:], self.M[:], -1.0, None, ALU.mult).then_inc(self.negm_ready, 1)
        dve.wait_ge(self.cols_turned, 1)
        dve.tensor_copy(self.cols[:], k.bank[2][:, 0:2 * HALVES * R])

    def scalar(self, act):
        act.wait_ge(self.g_ready, 1)
        act.activation(self.t[:], self.g[1][:], ACT.Abs).then_inc(self.abs_ready, 1)
        act.wait_ge(self.abs_ready, 1)
        act.activation(self.t[:], self.t[:], ACT.Exp, scale=-1.0).then_inc(self.exp_ready, 1)
        act.wait_ge(self.exp_ready, 1)
        act.activation(self.t[:], self.t[:], ACT.Ln, bias=1.0).then_inc(self.ln_ready, 1)
        act.wait_ge(self.m_ready, 1)
        act.activation(self.en[:], self.m[:], ACT.Exp, scale=-1.0).then_inc(self.en_ready, 1)


class Hops(Stage):

    VI = 8
    VB = 2 * VI

    def __init__(self, k, tag, kh, rpe, hopsT):
        super().__init__(k)
        self.kh, self.rpe = kh, rpe
        self.hopsT = hopsT.rearrange("(m p) v -> p m v", p=P)
        S_ = self.sem
        self.idx_landed = [S_(f"idx_landed{u}") for u in range(2)]
        self.gathered = [[S_(f"gathered{mb}{u}") for u in range(2)] for mb in range(2)]
        self.issued = S_("issued")
        self.turned = S_("turned")
        self.peT_ready = [S_(f"peT_ready{u}") for u in range(2)]
        self.q_ready = S_("q_ready")
        self.kmm_done = S_("kmm_done")
        self.kh_out = [S_(f"kh_out{u}") for u in range(2)]
        sb = k.scoped
        self.idx = [sb(f"{tag}_idx{u}", [P, 2, self.VI], I32) for u in range(2)]
        self.pe_rows = [[sb(f"{tag}_pe{u}{j}", [P, 2, D], F32) for j in range(self.VI)] for u in range(2)]
        self.peT = [sb(f"{tag}_peT{u}", [P, 4 * P], F32) for u in range(4)]
        self.q = [sb(f"{tag}_q{u}", [P, KC, self.VI, 32], F32) for u in range(2)]

    def phases(self, eng):
        for phase in range(2):
            with eng.Fori(0, P // self.VB) as i:
                yield phase, i, i * self.VB + phase * P

    def sync(self, sp):
        for phase, i, v0 in self.phases(sp):
            for u in range(2):
                sp.wait_ge(self.issued, i * 2 + (1 + u + phase * 16))
                sp.dma_start(self.idx[u][:], self.hopsT[:, :, ds(v0 + u * self.VI, self.VI)]).then_inc(self.idx_landed[u], 16)

    def gpsimd(self, pool):
        pool.sem_inc(self.issued, 2)
        for phase, i, v0 in self.phases(pool):
            for u in range(2):
                pool.wait_ge(self.idx_landed[u], i * 16 + (16 + phase * 128))
                wait_apart(pool, self.turned, v0 + (u * self.VI + 8), self.k.passed)
                for j in range(self.VI):
                    for mb in range(phase + 1):
                        pool.indirect_dma_start(self.pe_rows[u][j][:, mb, :], None, self.rpe,
                                                bass.IndirectOffsetOnAxis(ap=self.idx[u][:, mb, j:j + 1], axis=0)
                                                ).then_inc(self.gathered[phase][u], 16)
                pool.wait_ge(self.gathered[phase][u], i * (128 * (phase + 1)) + 128 * (phase + 1))
                pool.sem_inc(self.issued, 1)

    def tensor(self, pe):
        k = self.k
        pe.sem_inc(self.turned, 16)
        pe.sem_inc(self.kmm_done, 16)

        def turn(phase, i, v0, n):
            u, j = divmod(n, self.VI)
            if j == 0:
                pe.wait_ge(self.gathered[phase][u], i * (128 * (phase + 1)) + 128 * (phase + 1))
            pe.wait_ge(self.peT_ready[n % 2], i * self.VI + (phase * 64 + n // 2 + 1))
            for mb in range(phase + 1):
                for c in range(KC):
                    ins = pe.transpose(k.bank[n % 4][:, (mb * KC + c) * P:(mb * KC + c + 1) * P],
                                       self.pe_rows[u][j][:, mb, c * P:(c + 1) * P], k.ident[:])
            ins.then_inc(self.turned, 1)

        def mult(phase, i, v0, n):
            u, j = divmod(n, self.VI)
            pe.wait_ge(self.peT_ready[n % 2], i * self.VI + (phase * 64 + n // 2 + 3))
            if j == 0:
                pe.wait_ge(self.q_ready, i * 4 + (phase * 32 + 2 * u + 2))
            g = n // 4
            if n % 4 == 0:
                pe.wait_ge(self.kh_out[g % 2], i * 2 + (phase * 16 + g // 2 + 1))
            for mb in range(phase + 1):
                for c in range(KC):
                    at = mb * 256 + (n % 4) * 64 + c * 32
                    ins = pe.matmul(k.bank[4 + g][:, at:at + 32], self.peT[n % 4][:, (mb * KC + c) * P:(mb * KC + c + 1) * P],
                                    self.q[u][:, c, j, :], start=True, stop=True)
            ins.then_inc(self.kmm_done, 1)

        for phase, i, v0 in self.phases(pe):
            for n in range(self.VB + 2):
                if n < self.VB:
                    turn(phase, i, v0, n)
                if n >= 2:
                    mult(phase, i, v0, n - 2)

    def peT_out(self, eng, copy, phase, i, v0, n):
        w = (phase + 1) * KC * P
        eng.wait_ge(self.turned, v0 + (n + 17))
        eng.wait_ge(self.kmm_done, v0 + (n + 13))
        copy(self.peT[n % 4][:, 0:w], self.k.bank[n % 4][:, 0:w]).then_inc(self.peT_ready[n % 2], 1)

    def kh_to_sbuf(self, eng, copy, phase, i, v0, g):
        k = self.k
        eng.wait_ge(self.kmm_done, v0 + (g * 4 + 4 + 16))
        for mb in range(phase + 1):
            at = v0 * 64 + (g * 256 - mb * P * 64)
            ins = copy(self.kh[mb][:, ds(at, 256)], k.bank[4 + g][:, mb * 256:(mb + 1) * 256])
        ins.then_inc(self.kh_out[g % 2], 1)

    def scalar(self, act):
        act.sem_inc(self.peT_ready[0], 2)
        act.sem_inc(self.kh_out[0], 1)
        for phase, i, v0 in self.phases(act):
            for n in range(self.VB + 4):
                if n < self.VB and n % 2 == 0:
                    self.peT_out(act, act.copy, phase, i, v0, n)
                if n >= 7 and (n - 7) % 8 == 0:
                    self.kh_to_sbuf(act, act.copy, phase, i, v0, (n - 7) // 4)

    def vector(self, dve):
        k = self.k
        dve.sem_inc(self.peT_ready[1], 2)
        dve.sem_inc(self.kh_out[1], 1)

        def spread(phase, i, v0, u):
            dve.wait_ge(self.kmm_done, v0 + (u * self.VI + 8))
            full = [P, self.VI, B, 4]
            for c in range(KC):
                src = k.lnT[:].rearrange("p (c b s) -> p c s b", c=KC, b=B)[:, c, ds(v0 + u * self.VI, self.VI), :]
                dve.tensor_tensor(self.q[u][:, c].rearrange("p v (b r) -> p v b r", r=4),
                                  src.unsqueeze(3).to_broadcast(full),
                                  k.strip[:].unsqueeze(1).unsqueeze(1).to_broadcast(full), ALU.mult).then_inc(self.q_ready, 1)

        for phase, i, v0 in self.phases(dve):
            for n in range(self.VB + 4):
                if n in (0, self.VI):
                    spread(phase, i, v0, n // self.VI)
                if n < self.VB and n % 2 == 1:
                    self.peT_out(dve, dve.tensor_copy, phase, i, v0, n)
                if n >= 7 and (n - 7) % 8 == 4:
                    self.kh_to_sbuf(dve, dve.tensor_copy, phase, i, v0, (n - 7) // 4)


class Mlstm(Stage):

    def __init__(self, k, tag, NH, eps, cols, negm, var, kh=None):
        super().__init__(k)
        self.NH, self.R, self.DH, self.NS = NH, B * NH, D // NH, NH // 2
        self.eps, self.cols, self.negm, self.var, self.kh = eps, cols, negm, var, kh
        self.scale = float(self.DH) ** -0.5
        S_ = self.sem
        self.landed = [S_(f"landed{u}") for u in range(2)]
        self.q_ready, self.arg1_ready, self.arg_ready = S_("q_ready"), S_("arg1_ready"), S_("arg_ready")
        self.d_ready, self.masked = S_("d_ready"), S_("masked")
        self.qk_ready, self.qk_read, self.ct_ready = S_("qk_ready"), S_("qk_read"), S_("ct_ready")
        self.hm_done, self.h_ready, self.h_read = S_("hm_done"), S_("h_ready"), S_("h_read")
        self.own = S_("chain")
        self.cent_ready, self.cent_kept, self.sq_ready, self.var_done = S_("cent_ready"), S_("cent_kept"), S_("sq_ready"), S_("var_done")
        sb, DH = k.scoped, self.DH
        self.cT = [sb(f"{tag}_cT{u}", [P, KC, S], F32) for u in range(2)]
        self.qT = [sb(f"{tag}_qT{u}", [P, KC, S], F32) for u in range(2)]
        self.v = [sb(f"{tag}_v{u}", [P, HALVES, NH, DH + 1], F32) for u in range(2)]
        self.d0 = [sb(f"{tag}_d0{u}", [P, NH, S], F32) for u in range(2)]
        self.d1 = [sb(f"{tag}_d1{u}", [P, NH, P], F32) for u in range(2)]
        self.ct = [sb(f"{tag}_ct{u}", [P, 2 * S + 2 * P], F32) for u in range(2)]
        self.tmp = [sb(f"{tag}_tmp{u}", [P, 2 * S + 2 * P], F32) for u in range(2)] if kh else None
        self.den = sb(tag + "_den", [P, HALVES, NH], F32)
        self.mu = sb(tag + "_mu", [P, HALVES * NH], F32)
        self.h1 = sb(tag + "_h1", [P, HALVES * NH, DH], F32)
        self.sq = sb(tag + "_sq", [P, HALVES * NH, DH], F32)

    def sync(self, sp):
        k, NH = self.k, self.NH
        ctxT = k.ins["ctxT"].rearrange("(c p) t -> p c t", p=P)
        ctx = k.ins["ctx_1024"].rearrange("b (s p) (h d) -> p b s h d", p=P, h=NH)
        negm = self.negm.rearrange("r s -> (r s)")
        with sp.Fori(0, B // 2) as i:
            for u in range(2):
                b = i * 2 + u
                sp.wait_ge(self.h_ready, b + 1)
                sp.dma_start(self.d0[u][:].rearrange("p h s -> p (h s)"),
                             negm[ds(i * 2 * NH * S + u * NH * S, NH * S)].partition_broadcast(P)).then_inc(self.landed[u], 16)
                sp.dma_start(self.cT[u][:], ctxT[:, :, ds(i * 2 * S + u * S, S)]).then_inc(self.landed[u], 16)
                for s in range(HALVES):
                    sp.dma_start(self.v[u][:, s, :, 0:self.DH],
                                 ctx[:, ds(b, 1), s].rearrange("p o h d -> p (o h) d")).then_inc(self.landed[u], 16)

    def tensor(self, pe):
        k, DH, NS, NH = self.k, self.DH, self.NS, self.NH
        pe.sem_inc(self.h_ready, 2)
        pe.sem_inc(self.hm_done, 2)

        def qk(i, u, r):
            n = (i * 2 + u) * NS
            pair = (u * NS + r) % 2
            if r == 0:
                pe.wait_ge(self.landed[u], i * 64 + 64)
                pe.wait_ge(self.q_ready, i * 2 + (u + 1))
            pe.wait_ge(self.qk_read, n + (r + 1))
            at = slice(r * DH, (r + 1) * DH)
            for c in range(KC):
                pe.matmul(k.bank[2 * pair][:, c * S:(c + 1) * S], self.cT[u][at, c, 0:P], self.qT[u][at, c, :],
                          start=True, stop=True)
            for c in range(KC):
                ins = pe.matmul(k.bank[2 * pair + 1][:, c * P:(c + 1) * P], self.cT[u][at, c, P:S],
                                self.qT[u][at, c, P:S], start=True, stop=True)
            ins.then_inc(self.qk_ready, 1)

        def hm(i, u, r):
            n = (i * 2 + u) * NS
            ct = self.ct[(u * NS + r) % 2]
            if r == 0:
                pe.wait_ge(self.h_read, i * 2 + (u + 1))
            pe.wait_ge(self.ct_ready, n + (r + 1))
            for c in range(KC):
                h = c * NS + r
                cols = slice(h * (DH + 1), (h + 1) * (DH + 1))
                pe.matmul(k.bank[4 + 2 * u][:, cols], ct[:, c * S:c * S + P], self.v[u][:, 0, h, :], start=True, stop=True)
                pe.matmul(k.bank[5 + 2 * u][:, cols], ct[:, c * S + P:(c + 1) * S], self.v[u][:, 0, h, :], start=True, stop=False)
                ins = pe.matmul(k.bank[5 + 2 * u][:, cols], ct[:, 2 * S + c * P:2 * S + (c + 1) * P], self.v[u][:, 1, h, :],
                                start=False, stop=True)
            ins.then_inc(self.hm_done, 1)
            if r == NS - 1:
                pe.wait_ge(self.hm_done, n + (NS + 2))
                pe.sem_inc(self.h_ready, 1)

        steps = [(u, r) for u in range(2) for r in range(NS)]
        with pe.Fori(0, B // 2) as i:
            for n in range(len(steps) + 1):
                if n < len(steps):
                    qk(i, *steps[n])
                if n >= 1:
                    hm(i, *steps[n - 1])

    def scalar(self, act):
        k = self.k
        act.sem_inc(self.cent_kept, 1)
        lnT = k.lnT[:].rearrange("p (c t) -> p c t", c=KC)

        def q_in(i, u):
            wait_apart(act, self.h_ready, i * 2 + (u + 1), k.passed)
            act.copy(self.qT[u][:], lnT[:, :, ds(i * 2 * S + u * S, S)]).then_inc(self.q_ready, 1)

        def decay(i, u):
            act.wait_ge(self.arg1_ready, i * 2 + (u + 1))
            act.activation(self.d1[u][:], self.d1[u][:], ACT.Exp).then_inc(self.d_ready, 1)
            act.wait_ge(self.arg_ready, i * 2 + (u + 1))
            act.activation(self.d0[u][:], self.d0[u][:], ACT.Exp).then_inc(self.d_ready, 1)

        def keep(i, u):
            b = i * 2 + u
            act.wait_ge(self.cent_ready, b + 1)
            act.activation(self.sq[:], self.h1[:], ACT.Square).then_inc(self.sq_ready, 1)
            wait_apart(act, self.q_ready, b + 1, k.passed)
            act.copy(lnT[:, :, ds(i * 2 * S + u * S, S)],
                     self.h1[:].rearrange("p (s h) d -> p s (h d)", s=HALVES)).then_inc(self.cent_kept, 1)

        with act.Fori(0, B // 2) as i:
            q_in(i, 0)
            decay(i, 0)
            q_in(i, 1)
            decay(i, 1)
            keep(i, 0)
            keep(i, 1)

    def views(self, u, r, buf):
        NS = self.NS
        for t, (a, w) in enumerate(((0, S), (2 * S, P))):
            d = (self.d0 if t == 0 else self.d1)[u][:].rearrange("p (c r) s -> p c r s", r=NS)[:, :, r, :]
            yield t, w, buf[:, a:a + 2 * w].rearrange("p (c s) -> p c s", c=KC), d

    def vector(self, dve):
        k, DH, NS, NH, R = self.k, self.DH, self.NS, self.NH, self.R
        LINKS = 7
        chain = Chain(dve, self.own)
        dve.sem_inc(self.qk_read, 2)
        dve.sem_inc(self.h_read, 2)
        for u in range(2):
            ins = dve.memset(self.v[u][:, :, :, DH:DH + 1], 1.0)
        dve.sem_inc(self.var_done, 1)

        def args(i, u):
            b = i * 2 + u
            dve.wait_ge(self.landed[u], i * 64 + 64)
            for t in (1, 0):
                for h in range(NH):
                    dst = self.d1[u][:, h, :] if t else self.d0[u][:, h, :]
                    src = self.d0[u][:, h, P:S] if t else self.d0[u][:, h, :]
                    ins = dve.tensor_scalar(dst, src, self.cols[:, ds(i * 2 * NH + (t * R + u * NH + h), 1)], 0.0,
                                            ALU.add, ALU.min)
                ins.then_inc(self.arg1_ready if t else self.arg_ready, 1)
                if t:
                    dve.wait_ge(self.arg1_ready, b + 1)

        def ct(i, u, r):
            n = (i * 2 + u) * NS
            pair = (u * NS + r) % 2
            if r == 0 and not self.kh:
                dve.wait_ge(self.masked, i * 4 + (2 * u + 2))
            dve.wait_ge(self.qk_ready, n + (r + 1))
            dve.wait_ge(self.hm_done, n + (r + 1))
            buf = self.tmp[pair] if self.kh else self.ct[pair]
            for t, w, dst, d in self.views(u, r, buf):
                src = k.bank[2 * pair + t][:, 0:2 * w].rearrange("p (c s) -> p c s", c=KC)
                if self.kh:
                    hop = self.kh[t][:].rearrange("p (v c m) -> p c v m", c=KC, m=4 * B)
                    hop = hop[:, :, :, ds(i * 8 + (u * 4 + r), 1)].rearrange("p c v o -> p c (v o)")
                    ins = dve.scalar_tensor_tensor(out=dst, in0=src, scalar=self.scale, in1=hop, op0=ALU.mult, op1=ALU.add)
                else:
                    ins = dve.scalar_tensor_tensor(out=dst, in0=src, scalar=self.scale, in1=d, op0=ALU.mult, op1=ALU.mult)
            ins.then_inc(self.qk_read, 1)
            if not self.kh:
                dve.wait_ge(self.qk_read, n + (r + 3))
                dve.sem_inc(self.ct_ready, 1)

        def finish(i, u):
            b = i * 2 + u
            chain.start(i * 2 * LINKS + u * LINKS)
            dve.wait_ge(self.h_ready, b + 3)
            h_ps = k.ps[:, (4 + 2 * u) * 512:(6 + 2 * u) * 512].rearrange("p (s w) -> p s w", s=HALVES)
            h_ps = h_ps[:, :, 0:NH * (DH + 1)].rearrange("p s (h e) -> p s h e", e=DH + 1)
            en = self.cols[:, 2 * R:4 * R].rearrange("p (s r) -> p s r", s=HALVES)[:, :, ds(i * 2 * NH + u * NH, NH)]
            chain.link(dve.tensor_tensor(self.den[:], h_ps[:, :, :, DH], en, ALU.max))
            chain.link(dve.scalar_tensor_tensor(out=self.den[:], in0=h_ps[:, :, :, DH], scalar=-1.0, in1=self.den[:],
                                                op0=ALU.mult, op1=ALU.max))
            chain.link(dve.tensor_scalar(self.den[:], self.den[:], self.eps, None, ALU.add))
            chain.link(dve.reciprocal(self.den[:], self.den[:]))
            dve.wait_ge(self.cent_kept, b + 1)
            h1 = self.h1[:].rearrange("p (s h) d -> p s h d", s=HALVES)
            dve.tensor_tensor(h1, h_ps[:, :, :, 0:DH], self.den[:].unsqueeze(3).to_broadcast([P, HALVES, NH, DH]),
                              ALU.mult).then_inc(self.h_read, 1)
            dve.wait_ge(self.h_read, b + 3)
            chain.link(dve.tensor_reduce(self.mu[:], self.h1[:], AX.X, ALU.add))
            chain.link(dve.tensor_scalar(self.mu[:], self.mu[:], 1.0 / DH, None, ALU.mult))
            dve.tensor_tensor(self.h1[:], self.h1[:], self.mu[:].unsqueeze(2).to_broadcast([P, HALVES * NH, DH]),
                              ALU.subtract).then_inc(self.cent_ready, 1)
            dve.wait_ge(self.sq_ready, b + 1)
            chain.link(dve.tensor_reduce(self.var[:].rearrange("p (s r) -> p s r", s=HALVES)[:, :, ds(i * 2 * NH + u * NH, NH)],
                              self.sq[:].rearrange("p (s h) d -> p s h d", s=HALVES), AX.X, ALU.add))

        with dve.Fori(0, B // 2) as i:
            args(i, 0)
            args(i, 1)
            for r in range(NS):
                ct(i, 0, r)
            for r in range(NS):
                ct(i, 1, r)
            finish(i, 0)
            finish(i, 1)

    def gpsimd(self, pool):
        k, NS, NH = self.k, self.NS, self.NH

        def mask(i, u):
            cm = k.causal01[:].unsqueeze(1).to_broadcast([P, NH, P])
            for t, d in ((1, self.d1[u][:]), (0, self.d0[u][:, :, 0:P])):
                pool.wait_ge(self.d_ready, i * 4 + (2 * u + 2 - t))
                pool.tensor_tensor(d, d, cm, ALU.mult).then_inc(self.masked, 1)

        def ct(i, u, r):
            n = (i * 2 + u) * NS
            pair = (u * NS + r) % 2
            if r == 0:
                pool.wait_ge(self.masked, i * 4 + (2 * u + 2))
            pool.wait_ge(self.qk_read, n + (r + 3))
            pool.wait_ge(self.hm_done, n + (r + 1))
            for (t, w, dst, d), (_, _, src, _) in zip(self.views(u, r, self.ct[pair]), self.views(u, r, self.tmp[pair])):
                ins = pool.tensor_tensor(dst, src, d, ALU.mult)
            ins.then_inc(self.ct_ready, 1)

        with pool.Fori(0, B // 2) as i:
            mask(i, 0)
            if not self.kh:
                mask(i, 1)
            else:
                for r in range(NS):
                    ct(i, 0, r)
                mask(i, 1)
                for r in range(NS):
                    ct(i, 1, r)


class MlstmOut(Stage):

    def __init__(self, k, tag, NH, g, var, w, b=None):
        super().__init__(k)
        self.NH, self.R, self.DH, self.g, self.var, self.w_dram, self.b_dram = NH, B * NH, D // NH, g, var, w, b
        S_ = self.sem
        self.landed, self.own, self.inv_ready, self.rstd_ready = S_("landed"), S_("chain"), S_("inv_ready"), S_("rstd_ready")
        self.wrow = k.scoped(tag + "_wrow", [P, D], F32)
        self.brow = k.scoped(tag + "_brow", [P, D], F32)

    def sync(self, sp):
        sp.dma_start(self.wrow[:], self.w_dram.partition_broadcast(P)).then_inc(self.landed, 16)
        if self.b_dram is not None:
            sp.dma_start(self.brow[:], self.b_dram.partition_broadcast(P)).then_inc(self.landed, 16)

    def scalar(self, act):
        act.wait_ge(self.inv_ready, 1)
        act.activation(self.var[:], self.var[:], ACT.Sqrt).then_inc(self.rstd_ready, 1)

    def vector(self, dve):
        k, R, DH = self.k, self.R, self.DH
        chain = Chain(dve, self.own)
        tg = k.tanh_g[:, self.g:self.g + 1]
        chain.link(dve.tensor_scalar(self.var[:], self.var[:], 1.0 / DH, LN_EPS, ALU.mult, ALU.add))
        dve.reciprocal(self.var[:], self.var[:]).then_inc(self.inv_ready, 1)
        dve.wait_ge(self.landed, 16 * (1 + (self.b_dram is not None)))
        chain.link(dve.tensor_scalar(self.wrow[:], self.wrow[:], 1.0, tg, ALU.add, ALU.mult))
        if self.b_dram is not None:
            chain.link(dve.tensor_scalar(self.brow[:], self.brow[:], tg, None, ALU.mult))
        dve.wait_ge(self.rstd_ready, 1)
        for half in range(HALVES):
            h = k.lnT[:, half * T:half * T + B * D]
            chain.link(dve.tensor_tensor(h.rearrange("p (r d) -> p r d", d=DH), h.rearrange("p (r d) -> p r d", d=DH),
                                         self.var[:, half * R:(half + 1) * R].unsqueeze(2).to_broadcast([P, R, DH]), ALU.mult))
            h3 = h.rearrange("p (b d) -> p b d", d=D)
            row = lambda a: a[:].unsqueeze(1).to_broadcast([P, B, D])
            chain.link(dve.tensor_tensor(h3, h3, row(self.wrow), ALU.mult))
            x = k.x[:].rearrange("p (b s d) -> p s b d", s=HALVES, d=D)[:, half]
            chain.link(dve.tensor_tensor(x, h3, x, ALU.add))
            if self.b_dram is not None:
                chain.link(dve.tensor_tensor(x, x, row(self.brow), ALU.add))


class Buffers:
    pass


class Kernel:
    def __init__(self, nc, ctx, ins, out):
        self.nc, self.ctx, self.ins, self.out = nc, ctx, ins, out
        self.stage_sems, self.rounds = {}, {}
        self.b = Buffers()
        sb, F = self.sb, F32
        self.x = sb("x", [P, NT * D], F)
        self.lnT = sb("lnT", [P, KC * T], F)
        self.ident = sb("ident", [P, P], F)
        self.rank = sb("rank", [P, E], F)
        self.graw = sb("graw", [P, 8], F)
        self.tanh_g = sb("tanh_g", [P, 8], F)
        self.ps = ctx.enter_context(nc.psum_tensor("ps", [P, 8 * 512], F))
        self.bank = [self.ps[:, n * 512:(n + 1) * 512] for n in range(8)]
        self.ident_bf = sb("ident_bf", [P, P], BF16)
        self.causal_bf = sb("causal_bf", [P, P], BF16)
        self.causal01 = sb("causal01", [P, P], F)
        self.ones_f = sb("ones_f", [P, P], F)
        self.ones_row = self.ones_f[0:1, :]
        self.ones_bf = sb("ones_bf", [P, P], BF16)
        self.before_bf = sb("before_bf", [P, P], BF16)
        self.tile_rowi = sb("tile_rowi", [1, SLOT_TILES], I32)
        self.tile_row = sb("tile_row", [1, SLOT_TILES], F)
        self.tile_expert = sb("tile_expert", [1, SLOT_TILES], I32)
        self.slots = sb("slots", [P, 2, NT], mybir.dt.uint32)
        self.zeros = sb("zeros", [P, D], F)
        self.slot_x = nc.dram_tensor("slot_x", (SLOT_TILES * P, D), F, kind="Internal").ap()
        self.slot_y = nc.dram_tensor("slot_y", (SLOT_TILES * P, D), F, kind="Internal").ap()
        self.slots_zeroed = self.sem("slots_zeroed")
        self.weights_landed = self.sem("weights_landed")
        self.weights_due = 0
        self.prow = sb("prow", [P, 1], I32)
        self.pbits = sb("pbits", [P, 2], I32)
        self.pbitsf = sb("pbitsf", [P, 2], F)
        self.head16 = sb("head16", [P, 8], F)
        self.strip = sb("strip", [P, 4], F)

        self.setup_loaded = self.sem("setup_loaded")
        self.setup_dve = self.sem("setup_dve")
        self.setup_pool = self.sem("setup_pool")
        self.setup_tanh = self.sem("setup_tanh")
        self.passed = self.sem("passed")
        self.stored = self.sem("stored")
        self.over = {e: self.sem(e + "_over") for e in ("pe", "act", "dve", "pool", "sp")}

    def sb(self, name, shape, dt):
        return self.ctx.enter_context(self.nc.sbuf_tensor(name, shape, dt))

    def ln_buffers(self, tag, rows=2):
        self.b.ln_stats = self.scoped(tag + "_ln_stats", [P, NT * 6], F32)
        self.b.ln_mv = self.scoped(tag + "_ln_mv", [P, NT, 2], F32)
        self.b.ln_mean = self.scoped(tag + "_ln_mean", [P, NT], F32)
        self.b.ln_inv = self.scoped(tag + "_ln_inv", [P, NT], F32)
        self.b.ln_rstd = self.scoped(tag + "_ln_rstd", [P, NT], F32)
        self.b.ln_x = [self.scoped(tag + f"_ln_x{u}", [P, 4, D], F32) for u in range(rows)]

    def router_buffers(self, tag):
        self.b.wg = self.scoped(tag + "_wg", [P, KC, E], F32)
        self.b.bg = self.scoped(tag + "_bg", [P, E], F32)
        self.b.rt = self.scoped(tag + "_rt", [P, 6, NT, E], F32)
        self.b.rs = self.scoped(tag + "_rs", [P, 6, NT], F32)
        self.b.rexp = self.scoped(tag + "_rexp", [P, NT], F32)
        self.b.gate = self.scoped(tag + "_gate", [P, NT * E], F32)
        self.b.gate3 = self.b.gate[:].rearrange("p (t e) -> p t e", e=E)

    def bias_buffers(self, tag):
        self.b.gateT = self.scoped(tag + "_gateT", [E, T], F32)
        self.b.ebias = self.scoped(tag + "_ebias", [E, D], F32)

    def expert_weights(self, tag, up, down, b1=None):
        up = up.rearrange("e (c p) f -> e p c f", p=P)
        down = down.rearrange("e (c p) h -> e p c h", p=P)
        self.b.w_up = self.scoped(tag + "_w_up", [P, E * KC * up.shape[3]], F32)
        self.b.w_down = self.scoped(tag + "_w_down", [P, E * down.shape[2] * D], F32)
        by_expert = lambda w, like: w[:].rearrange("p (e c f) -> p e c f", e=E, c=like.shape[2])
        loads = [(by_expert(self.b.w_up, up)[:, e], up[e]) for e in range(E)]
        loads += [(by_expert(self.b.w_down, down)[:, e], down[e]) for e in range(E)]
        if b1 is not None:
            self.b.b1_all = self.scoped(tag + "_b1_all", [P, E * up.shape[3]], F32)
            loads.append((self.b.b1_all[:], b1.rearrange("e f -> (e f)").partition_broadcast(P)))
        self.weights_due += 16 * len(loads)
        return loads

    def scoped(self, name, shape, dt):
        return self.scope.enter_context(self.nc.sbuf_tensor(name, shape, dt))

    def shared_sem(self, name):
        if name not in self.stage_sems:
            self.stage_sems[name] = self.sem(name)
        return self.stage_sems[name]

    def sem(self, name):
        return self.ctx.enter_context(self.nc.semaphore(name))


class Setup(Stage):

    def sync(self, sp):
        k = self.k
        x = k.ins["x"].rearrange("b s d -> (b s) d").rearrange("(t p) d -> p t d", p=P)
        sp.dma_start(k.x[:].rearrange("p (t d) -> p t d", d=D), x).then_inc(k.setup_loaded, 16)
        sp.dma_start(k.graw[:, 0:4], k.ins["g_xattn"].partition_broadcast(P)).then_inc(k.setup_loaded, 16)
        sp.dma_start(k.graw[:, 4:8], k.ins["g_ffn"].partition_broadcast(P)).then_inc(k.setup_loaded, 16)
        sp.wait_ge(k.setup_pool, 13 + E)
        sp.dma_start(k.slot_x.rearrange("(j p) d -> p j d", p=P),
                     k.zeros[:].unsqueeze(1).to_broadcast([P, SLOT_TILES, D])).then_inc(k.slots_zeroed, 16)
        sp.wait_ge(k.setup_loaded, 48)

    def gpsimd(self, pool):
        k = self.k
        pool.memset(k.ident[:], 0.0).then_inc(k.setup_pool, 1)
        pool.wait_ge(k.setup_pool, 1)
        pool.affine_select(out=k.ident[:], in_=k.ident[:], compare_op=ALU.not_equal, fill=1.0, base=0,
                           pattern=[[-1, P]], channel_multiplier=1).then_inc(k.setup_pool, 1)
        for e in range(E):
            pool.memset(k.rank[:, e:e + 1], float(E - e)).then_inc(k.setup_pool, 1)
        pool.memset(k.causal_bf[:], 0.0).then_inc(k.setup_pool, 1)
        pool.memset(k.ones_f[:], 1.0).then_inc(k.setup_pool, 1)
        pool.memset(k.ones_bf[:], 1.0).then_inc(k.setup_pool, 1)
        pool.memset(k.before_bf[:], 1.0).then_inc(k.setup_pool, 1)
        pool.memset(k.zeros[:], 0.0).then_inc(k.setup_pool, 1)
        pool.iota(k.tile_rowi[:], pattern=[[1, SLOT_TILES]], base=0, channel_multiplier=0).then_inc(k.setup_pool, 1)
        pool.memset(k.causal01[:], 1.0).then_inc(k.setup_pool, 1)
        pool.iota(k.prow[:], pattern=[[0, 1]], base=0, channel_multiplier=1).then_inc(k.setup_pool, 1)
        pool.wait_ge(k.setup_pool, 10 + E)
        pool.affine_select(out=k.causal_bf[:], in_=k.causal_bf[:], compare_op=ALU.is_ge, fill=-BIG, base=0,
                           pattern=[[-1, P]], channel_multiplier=1).then_inc(k.setup_pool, 1)
        pool.affine_select(out=k.causal01[:], in_=k.causal01[:], compare_op=ALU.is_ge, fill=0.0, base=0,
                           pattern=[[1, P]], channel_multiplier=-1).then_inc(k.setup_pool, 1)
        pool.affine_select(out=k.before_bf[:], in_=k.before_bf[:], compare_op=ALU.is_ge, fill=0.0, base=-1,
                           pattern=[[1, P]], channel_multiplier=-1).then_inc(k.setup_pool, 1)

    def vector(self, dve):
        k = self.k
        chain = Chain(dve, k.setup_dve)
        dve.wait_ge(k.setup_pool, 13 + E)
        chain.link(dve.tensor_copy(k.ident_bf[:], k.ident[:]))
        chain.link(dve.tensor_copy(k.tile_row[:], k.tile_rowi[:]))
        chain.link(dve.tensor_scalar(k.pbits[:, 0:1], k.prow[:], 112, None, ALU.bitwise_and))
        chain.link(dve.tensor_scalar(k.pbits[:, 1:2], k.prow[:], 96, None, ALU.bitwise_and))
        chain.link(dve.tensor_copy(k.pbitsf[:], k.pbits[:]))
        for h in range(8):
            dve.tensor_scalar(k.head16[:, h:h + 1], k.pbitsf[:, 0:1], 16.0 * h, None, ALU.is_equal)
        for r in range(4):
            dve.tensor_scalar(k.strip[:, r:r + 1], k.pbitsf[:, 1:2], 32.0 * r, None, ALU.is_equal)

    def scalar(self, act):
        k = self.k
        act.wait_ge(k.setup_loaded, 48)
        act.activation(k.tanh_g[:], k.graw[:], ACT.Tanh).then_inc(k.setup_tanh, 1)


class Store(Stage):
    def sync(self, sp):
        k = self.k
        out = k.out.rearrange("b s d -> (b s) d").rearrange("(t p) d -> p t d", p=P)
        sp.dma_start(out, k.x[:].rearrange("p (t d) -> p t d", d=D)).then_inc(k.stored, 16)
        sp.wait_ge(k.stored, 16)


def make_stages(k):
    I = k.ins
    stages = [Setup(k)]

    @contextmanager
    def scope():
        with ExitStack() as k.scope:
            yield

    def layer_norm(tag):
        with scope():
            k.ln_buffers(tag)
            stages.append(LayerNorm(k, tag))

    def mlstm(tag, layer, NH, eps, g, shifted, w, b=None, rpe=None, hopsT=None):
        R = B * NH
        negm = k.nc.dram_tensor(tag + "_negm", (R, S), F32, kind="Internal").ap()
        with ExitStack() as held:
            sb = lambda n, shape: held.enter_context(k.nc.sbuf_tensor(f"{tag}_{n}", shape, F32))
            cols, var = sb("cols", [P, 4 * R]), sb("var", [P, HALVES * R])
            kh = [sb("kh0", [P, S * 64]), sb("kh1", [P, P * 64])] if rpe is not None else None
            with scope():
                stages.append(MlstmGates(k, tag + "_mg", NH, I[layer + "_gate_w"], I[layer + "_gate_b"], shifted, cols, negm))
            if kh:
                with scope():
                    stages.append(Hops(k, tag + "_hp", kh, rpe, hopsT))
            with scope():
                stages.append(Mlstm(k, tag + "_ml", NH, eps, cols, negm, var, kh))
            with scope():
                stages.append(MlstmOut(k, tag + "_mo", NH, g, var, w, b))

    def moe(tag, n, wg, bg=None, bias=None, dense=None, kind=None, up=None, down=None, b1=None):
        with scope():
            k.ln_buffers(tag + "_ln", rows=2 if kind is None else 4)
            k.router_buffers(tag)
            if bias is not None:
                k.bias_buffers(tag)
            loads = None if kind is None else k.expert_weights(tag, up, down, b1)
            stages.append(LayerNorm(k, tag + "_ln", loads))
            stages.append(Router(k, tag + "_rt", wg, 4 + n, bg))
            if bias is not None:
                stages.append(GateBias(k, tag + "_gb", bias))
            if dense is not None:
                stages.append(LinearExperts(k, tag + "_ex", dense))
            else:
                stages.append(Dispatch(k, tag + "_di"))
                stages.append(ExpertTiles(k, tag + "_et", kind, up.shape[2] // P, down.shape[1] // P))
                stages.append(Combine(k, tag + "_co"))

    for n in SUBLAYERS:
        tag = f"s{n}"
        k.b = Buffers()
        if n % 2 == 0:
            layer_norm(tag + "_ln")
        if n == 0:
            mlstm(tag, "L0", 4, 1e-8, 0, True, I["L0_xattn_out_w"])
        if n == 1:
            moe(tag, 0, I["L0_ffn_Wg"], bias=I["L0_ffn_be"], dense=I["L0_ffn_We"])
        if n == 2:
            with scope():
                stages.append(Attention(k, tag + "_at", 1, True, *(I["L1_xattn_w_" + m] for m in "qkvo"),
                                        *(I["L1_xattn_b_" + m] for m in "oqkv")))
        if n == 3:
            moe(tag, 1, I["L1_ffn_router_w"], kind="glu", up=I["L1_ffn_up_proj"], down=I["L1_ffn_down_proj"])
        if n == 4:
            with scope():
                stages.append(Attention(k, tag + "_at", 2, False, *(I["L2_xattn_W" + m] for m in "qkvo"),
                                        I["L2_xattn_bo"]))
        if n == 5:
            moe(tag, 2, I["L2_ffn_router_w"], kind="silu", up=I["L2_ffn_w1"], down=I["L2_ffn_w2"])
        if n == 6:
            mlstm(tag, "L3", 8, 1e-6, 3, False, I["L3_xattn_ln_w"], I["L3_xattn_ln_b"],
                  I["L3_xattn_rpe"], I["hopsT"])
        if n == 7:
            moe(tag, 3, I["L3_ffn_Wg"], bg=I["L3_ffn_bg"], bias=I["L3_ffn_b2"], kind="relu",
                up=I["L3_ffn_W1"], down=I["L3_ffn_W2"], b1=I["L3_ffn_b1"])
    stages.append(Store(k))
    return stages


def flamingo_stack(nc, ins, out):
    with ExitStack() as ctx:
        k = Kernel(nc, ctx, ins, out)
        stages = make_stages(k)
        block = ctx.enter_context(nc.Block())

        def between(eng, name, n):
            eng.drain().then_inc(k.over[name], 1)
            for other, over in k.over.items():
                eng.wait_ge(over, n + 1)

        @block.sync
        def _(sp):
            for n, stage in enumerate(stages):
                if n:
                    for sem in stages[n - 1].sems:
                        sp.sem_clear(sem)
                stage.sync(sp)
                between(sp, "sp", n)

        @block.gpsimd
        def _(pool):
            for n, stage in enumerate(stages):
                stage.gpsimd(pool)
                between(pool, "pool", n)

        @block.scalar
        def _(act):
            for n, stage in enumerate(stages):
                stage.scalar(act)
                between(act, "act", n)

        @block.vector
        def _(dve):
            for n, stage in enumerate(stages):
                stage.vector(dve)
                between(dve, "dve", n)

        @block.tensor
        def _(pe):
            for n, stage in enumerate(stages):
                stage.tensor(pe)
                between(pe, "pe", n)


def laid_out(inputs):
    import numpy as _np

    T_ = lambda a, *d: _np.ascontiguousarray(_np.transpose(_np.asarray(a), d))
    keep = {n: _np.ascontiguousarray(a) for n, a in inputs.items()}
    keep["L1_ffn_router_w"] = T_(inputs["L1_ffn_router_w"], 1, 0)
    keep["L3_ffn_Wg"] = T_(inputs["L3_ffn_Wg"], 1, 0)
    keep["L3_ffn_W1"] = T_(inputs["L3_ffn_W1"], 0, 2, 1)
    keep["L3_ffn_W2"] = T_(inputs["L3_ffn_W2"], 0, 2, 1)
    for l in ("L0", "L3"):
        keep[l + "_gate_w"] = _np.ascontiguousarray(_np.concatenate(
            [_np.asarray(inputs[f"{l}_xattn_{g}gate_w"]).T for g in "if"], axis=1))
        keep[l + "_gate_b"] = _np.concatenate([_np.asarray(inputs[f"{l}_xattn_{g}gate_b"]) for g in "if"])
    keep["hopsT"] = T_(inputs["itok_SxS2_0_2016"], 1, 0)
    keep["ctxT"] = _np.ascontiguousarray(_np.asarray(inputs["ctx_1024"]).reshape(T, D).T)
    for n in [f"L1_xattn_w_{m}" for m in "qkvo"] + [f"L2_xattn_W{m}" for m in "qkvo"]:
        keep[n] = T_(inputs[n], 1, 0)
    for n in ("L1_xattn_b_q", "L1_xattn_b_k"):
        keep[n] = T_(_np.asarray(inputs[n]).reshape(2, 128), 1, 0)
    return keep


def kernel(**inputs):
    import numpy as _np
    import concourse.bacc as _bacc
    from concourse import mybir as _mybir
    from concourse.bass_utils import run_bass_kernel_spmd as _run

    nc = _bacc.Bacc("TRN2", target_bir_lowering=False, num_devices=1)
    arrays, ins = {}, {}
    for name, a in laid_out(inputs).items():
        arrays[f"in_{name}"] = a
        ins[name] = nc.dram_tensor(f"in_{name}", a.shape, _mybir.dt.from_np(a.dtype), kind="ExternalInput").ap()
    out = nc.dram_tensor("out", (8, 256, 256), F32, kind="ExternalOutput").ap()
    flamingo_stack(nc, ins, out)
    r = _run(nc, [arrays], core_ids=[0])
    return r.results[0]["out"]
```

```python
from contextlib import ExitStack, contextmanager

import concourse.bass as bass
from concourse import mybir

F32 = mybir.dt.float32
BF16 = mybir.dt.bfloat16
I32 = mybir.dt.int32
ALU = mybir.AluOpType
ACT = mybir.ActivationFunctionType
AX = mybir.AxisListType

P = 128
B, S, D = 8, 256, 256
T = B * S
NT = T // P
HALVES = S // P
KC = D // P
E = 8
LN_EPS = 1e-5
SLOT_TILES = 40
BIG = 1e30

SUBLAYERS = (0, 1, 2, 3, 4, 5, 6, 7)


def ds(start, size):
    return bass.ds(start, size)


class Chain:

    def __init__(self, eng, sem):
        self.eng, self.sem, self.base, self.n = eng, sem, 0, 0

    def start(self, base=0):
        self.base, self.n = base, 0

    def link(self, ins):
        self.n += 1
        ins.then_inc(self.sem, 1)
        self.eng.wait_ge(self.sem, self.base + self.n)


def wait_apart(eng, sem, value, passed):
    eng.wait_ge(sem, value)
    eng.sem_inc(passed, 1)


class Stage:

    def __init__(self, k):
        self.k, self.b, self.sems = k, k.b, []
        kind = type(self).__name__
        self.round = k.rounds[kind] = k.rounds.get(kind, -1) + 1

    def sem(self, name):
        s = self.k.shared_sem(f"{type(self).__name__}_{name}")
        self.sems.append(s)
        return s

    def lasting_sem(self, name):
        return self.k.shared_sem(f"{type(self).__name__}_{name}")

    def tensor(self, pe):
        pass

    def vector(self, dve):
        pass

    def scalar(self, act):
        pass

    def gpsimd(self, pool):
        pass

    def sync(self, sp):
        pass


class LayerNorm(Stage):

    GROUP = 4
    GROUPS = NT // GROUP
    AHEAD = 16

    def __init__(self, k, tag, weights=None, beside=None):
        super().__init__(k)
        self.weights = weights
        self.beside = beside
        self.stats_done = self.sem("stats_done")
        self.own = self.sem("chain")
        self.inv_ready = self.sem("inv_ready")
        self.rstd_ready = self.sem("rstd_ready")
        self.normed = self.sem("normed")
        self.transposed = self.sem("transposed")
        self.copied0 = self.sem("copied0")
        self.copied1 = self.sem("copied1")

    def sync(self, sp):
        for dst, src in self.weights or ():
            sp.dma_start(dst, src).then_inc(self.k.weights_landed, 16)
        if self.beside:
            self.beside.ahead_sync(sp)

    def gpsimd(self, pool):
        if self.beside:
            self.beside.ahead_gpsimd(pool, 0, self.AHEAD)

    def vector(self, dve):
        k, G = self.k, self.GROUP
        chain = Chain(dve, self.own)
        with dve.Fori(0, NT // G) as i:
            for j in range(G):
                dve.bn_stats(self.b.ln_stats[:, ds(i * G * 6 + j * 6, 6)],
                             k.x[:, ds(i * G * D + j * D, D)]).then_inc(self.stats_done, 1)
        dve.wait_ge(self.stats_done, NT)
        for t in range(NT):
            ins = dve.bn_aggr(self.b.ln_mv[:, t, :], self.b.ln_stats[:, t * 6:(t + 1) * 6])
        chain.link(ins)
        chain.link(dve.tensor_scalar(self.b.ln_inv[:], self.b.ln_mv[:, :, 1], LN_EPS, None, ALU.add))
        dve.reciprocal(self.b.ln_inv[:], self.b.ln_inv[:]).then_inc(self.inv_ready, 1)
        chain.link(dve.tensor_copy(self.b.ln_mean[:], self.b.ln_mv[:, :, 0]))
        dve.wait_ge(self.rstd_ready, 1)
        for g in range(self.GROUPS):
            if g >= len(self.b.ln_x):
                dve.wait_ge(self.transposed, g - len(self.b.ln_x) + 1)
            for j in range(G):
                t = g * G + j
                ins = dve.tensor_scalar(self.b.ln_x[g % len(self.b.ln_x)][:, j, :], k.x[:, t * D:(t + 1) * D],
                                        self.b.ln_mean[:, t:t + 1], self.b.ln_rstd[:, t:t + 1], ALU.subtract, ALU.mult)
            ins.then_inc(self.normed, 1)
            if g:
                self.lnT_out(dve, dve.tensor_copy, 1, g - 1, self.copied1)
        self.lnT_out(dve, dve.tensor_copy, 1, self.GROUPS - 1, self.copied1)

    def lnT_out(self, eng, copy_, c, g, copied):
        k, W = self.k, self.GROUP * P
        eng.wait_ge(self.transposed, g + 1)
        copy_(k.lnT[:, c * T + g * W:c * T + (g + 1) * W], k.bank[2 * (g % 2) + c][:]).then_inc(copied, 1)

    def scalar(self, act):
        k = self.k
        act.wait_ge(self.inv_ready, 1)
        act.activation(self.b.ln_rstd[:], self.b.ln_inv[:], ACT.Sqrt).then_inc(self.rstd_ready, 1)
        for g in range(self.GROUPS):
            self.lnT_out(act, act.copy, 0, g, self.copied0)

    def tensor(self, pe):
        k, G = self.k, self.GROUP
        for g in range(self.GROUPS):
            if g >= 2:
                pe.wait_ge(self.copied0, g - 1)
                pe.wait_ge(self.copied1, g - 1)
            pe.wait_ge(self.normed, g + 1)
            for c in range(KC):
                for j in range(G):
                    ins = pe.transpose(k.bank[2 * (g % 2) + c][:, j * P:(j + 1) * P],
                                       self.b.ln_x[g % len(self.b.ln_x)][:, j, c * P:(c + 1) * P], k.ident[:])
            ins.then_inc(self.transposed, 1)


class Router(Stage):

    def __init__(self, k, tag, wg, g, bias=None):
        super().__init__(k)
        self.wg_dram, self.g, self.bias_dram = wg, g, bias
        self.loaded = self.sem("loaded")
        self.logits_ready = self.sem("logits_ready")
        self.own = self.sem("chain")
        self.diff_ready = self.sem("diff_ready")
        self.exp_ready = self.sem("exp_ready")

    def sync(self, sp):
        k = self.k
        sp.dma_start(self.b.wg[:], self.wg_dram.rearrange("(c p) e -> p c e", p=P)).then_inc(self.loaded, 16)
        if self.bias_dram is not None:
            sp.dma_start(self.b.bg[:], self.bias_dram.partition_broadcast(P)).then_inc(self.loaded, 16)

    def tensor(self, pe):
        k = self.k
        pe.wait_ge(self.loaded, 16 * (1 + (self.bias_dram is not None)))
        for t in range(NT):
            for c in range(KC):
                ins = pe.matmul(k.bank[0][:, t * E:(t + 1) * E], k.lnT[:, c * T + t * P:c * T + (t + 1) * P],
                                self.b.wg[:, c, :], start=c == 0, stop=c == KC - 1)
        ins.then_inc(self.logits_ready, 1)

    def vector(self, dve):
        k = self.k
        full = [P, NT, E]
        over_e = lambda a: a.unsqueeze(2).to_broadcast(full)
        over_t = lambda a: a.unsqueeze(1).to_broadcast(full)
        chain = Chain(dve, self.own)
        logits = self.b.rt[:, 0]
        eq, key, sel1, sel2 = self.b.rt[:, 1], self.b.rt[:, 2], self.b.rt[:, 3], self.b.rt[:, 4]
        m1, m2, kmax, diff, w1, w2 = (self.b.rs[:, n] for n in range(6))
        ps = k.bank[0][:, 0:NT * E].rearrange("p (t e) -> p t e", e=E)
        dve.wait_ge(self.logits_ready, 1)
        if self.bias_dram is not None:
            chain.link(dve.tensor_tensor(logits, ps, over_t(self.b.bg[:]), ALU.add))
        else:
            chain.link(dve.tensor_copy(logits, ps))
        for m, sel, nxt in ((m1, sel1, key), (m2, sel2, None)):
            left = logits if nxt is not None else self.b.rt[:, 5]
            chain.link(dve.tensor_reduce(m, left, AX.X, ALU.max))
            chain.link(dve.tensor_tensor(eq, left, over_e(m), ALU.is_equal))
            chain.link(dve.tensor_tensor(key, eq, over_t(k.rank[:]), ALU.mult))
            chain.link(dve.tensor_reduce(kmax, key, AX.X, ALU.max))
            chain.link(dve.tensor_tensor(sel, key, over_e(kmax), ALU.is_equal))
            if nxt is not None:
                chain.link(dve.scalar_tensor_tensor(out=self.b.rt[:, 5], in0=sel, scalar=-BIG, in1=logits,
                                                    op0=ALU.mult, op1=ALU.add))
        dve.tensor_tensor(diff, m2, m1, ALU.subtract).then_inc(self.diff_ready, 1)
        dve.wait_ge(self.exp_ready, 1)
        chain.link(dve.tensor_scalar(w1, self.b.rexp[:], 1.0, None, ALU.add))
        chain.link(dve.reciprocal(w1, w1))
        chain.link(dve.tensor_scalar(w1, w1, k.tanh_g[:, self.g:self.g + 1], None, ALU.mult))
        chain.link(dve.tensor_tensor(w2, self.b.rexp[:], w1, ALU.mult))
        chain.link(dve.tensor_tensor(eq, sel1, over_e(w1), ALU.mult))
        chain.link(dve.tensor_tensor(key, sel2, over_e(w2), ALU.mult))
        chain.link(dve.tensor_tensor(self.b.gate3, eq, key, ALU.add))

    def scalar(self, act):
        k = self.k
        act.wait_ge(self.diff_ready, 1)
        act.activation(self.b.rexp[:], self.b.rs[:, 3], ACT.Exp).then_inc(self.exp_ready, 1)


class GateBias(Stage):

    def __init__(self, k, tag, bias):
        super().__init__(k)
        self.bias_dram = bias
        self.loaded = self.sem("loaded")
        self.turned = self.sem("turned")
        self.gate_ready = self.sem("gate_ready")
        self.y_ready = self.sem("y_ready")
        self.added = self.sem("added")

    def sync(self, sp):
        sp.dma_start(self.b.ebias[:], self.bias_dram).then_inc(self.loaded, 16)

    def tensor(self, pe):
        k = self.k
        for t in range(NT):
            ins = pe.transpose(k.bank[t // 4][0:E, (t % 4) * P:(t % 4 + 1) * P], self.b.gate[:, t * E:(t + 1) * E], k.ident[:])
        ins.then_inc(self.turned, 1)
        pe.wait_ge(self.gate_ready, 4)
        pe.wait_ge(self.loaded, 16)
        for t in range(NT):
            if t >= 4:
                pe.wait_ge(self.added, t - 3)
            pe.matmul(k.bank[4 + t % 4][:, 0:D], self.b.gateT[:, t * P:(t + 1) * P], self.b.ebias[:],
                      start=True, stop=True).then_inc(self.y_ready, 1)

    def vector(self, dve):
        k = self.k
        dve.wait_ge(self.turned, 1)
        for n in range(4):
            dve.tensor_copy(self.b.gateT[:, n * 4 * P:(n + 1) * 4 * P], k.bank[n][0:E, :]).then_inc(self.gate_ready, 1)
        for t in range(NT):
            dve.wait_ge(self.y_ready, t + 1)
            dve.tensor_tensor(k.x[:, t * D:(t + 1) * D], k.bank[4 + t % 4][:, 0:D], k.x[:, t * D:(t + 1) * D],
                              ALU.add).then_inc(self.added, 1)


class LinearExperts(Stage):

    RING = 8

    def __init__(self, k, tag, we):
        super().__init__(k)
        self.we = we.rearrange("e (c p) h -> e p c h", p=P)
        self.landed = [self.sem(f"landed{u}") for u in range(2)]
        self.used = self.sem("used")
        self.y_ready = self.sem("y_ready")
        self.added = self.sem("added")
        self.col = self.sem("col")
        self.up = [k.scoped(f"{tag}_up{u}", [P, KC, D], F32) for u in range(2)]
        self.gcol = [k.scoped(f"{tag}_gcol{u}", [P, NT], F32) for u in range(2)]

    def sync(self, sp):
        for u in range(2):
            sp.dma_start(self.up[u][:], self.we[u]).then_inc(self.landed[u], 16)
        with sp.Fori(1, E // 2) as i:
            for u in range(2):
                sp.wait_ge(self.used, i * 2 + (u - 1))
                sp.dma_start(self.up[u][:], self.we[ds(i * 2 + u, 1)].rearrange("e p c h -> (e p) c h")).then_inc(self.landed[u], 16)

    def tensor(self, pe):
        k = self.k

        def expert(e, round_, u, first):
            pe.wait_ge(self.landed[u], round_ * 16 + 16)
            for t in range(NT):
                if not (first and t < self.RING):
                    pe.wait_ge(self.added, e * NT + (t - self.RING + 1))
                for c in range(KC):
                    ins = pe.matmul(k.bank[t % self.RING][:, 0:D], k.lnT[:, c * T + t * P:c * T + (t + 1) * P],
                                    self.up[u][:, c, :], start=c == 0, stop=c == KC - 1)
                if t < NT - 1:
                    ins.then_inc(self.y_ready, 1)
            ins.then_inc(self.y_ready, 1)
            pe.wait_ge(self.y_ready, e * NT + NT)
            pe.sem_inc(self.used, 1)

        for u in range(2):
            expert(u, 0, u, u == 0)
        with pe.Fori(1, E // 2) as i:
            for u in range(2):
                expert(i * 2 + u, i, u, False)

    def vector(self, dve):
        k = self.k
        with dve.Fori(0, E // 2) as i:
            for u in range(2):
                e = i * 2 + u
                dve.tensor_copy(self.gcol[u][:].unsqueeze(2), self.b.gate3[:, :, ds(e, 1)]).then_inc(self.col, 1)
                dve.wait_ge(self.col, e + 1)
                for t in range(NT):
                    dve.wait_ge(self.y_ready, e * NT + (t + 1))
                    dve.scalar_tensor_tensor(out=k.x[:, t * D:(t + 1) * D], in0=k.bank[t % self.RING][:, 0:D],
                                             scalar=self.gcol[u][:, t:t + 1], in1=k.x[:, t * D:(t + 1) * D],
                                             op0=ALU.mult, op1=ALU.add).then_inc(self.added, 1)


class Dispatch(Stage):

    def __init__(self, k, tag):
        super().__init__(k)
        S_ = self.sem
        self.own, self.m_ready, self.counted = S_("chain"), S_("m_ready"), S_("counted")
        self.slots_ready, self.scattered = S_("slots_ready"), self.lasting_sem("scattered")
        sb = k.scoped
        self.m = sb(tag + "_m", [P, NT * E], BF16)
        self.tot, self.cum, self.cex = (sb(f"{tag}_{n}", [P, E, NT], F32) for n in ("tot", "cum", "cex"))
        self.slot = sb(tag + "_slot", [P, NT, E], F32)
        self.pick = sb(tag + "_pick", [P, 2, NT, E], F32)
        self.slotf = sb(tag + "_slotf", [P, 2, NT], F32)
        self.n, self.tend, self.adj, self.nt = (sb(f"{tag}_{n}", [P, E], F32) for n in ("n", "tend", "adj", "nt"))
        self.ni = sb(tag + "_ni", [P, E], I32)
        self.le = sb(tag + "_le", [1, SLOT_TILES, E], F32)
        self.ef = sb(tag + "_ef", [1, SLOT_TILES], F32)

    def tensor(self, pe):
        k = self.k
        pe.wait_ge(self.m_ready, 1)
        pe.matmul(k.bank[0][:, 0:NT * E], k.before_bf[:], self.m[:], start=True, stop=True)
        pe.matmul(k.bank[1][:, 0:NT * E], k.ones_bf[:], self.m[:], start=True, stop=True).then_inc(self.counted, 1)

    def vector(self, dve):
        k = self.k
        chain = Chain(dve, self.own)
        sel = [self.b.rt[:, 3], self.b.rt[:, 4]]
        over_t = lambda a: a.unsqueeze(1).to_broadcast([P, NT, E])
        dve.tensor_tensor(self.m[:].rearrange("p (t e) -> p t e", e=E), sel[0], sel[1], ALU.add).then_inc(self.m_ready, 1)
        dve.wait_ge(self.counted, 1)
        chain.link(dve.tensor_copy(self.tot[:], k.bank[1][:, 0:NT * E].rearrange("p (t e) -> p e t", e=E)))
        flat = lambda a: a[:].rearrange("p e t -> p (e t)")
        chain.link(dve.tensor_tensor_scan(flat(self.cum), k.ones_f[:], flat(self.tot), 0.0, ALU.mult, ALU.add))
        chain.link(dve.tensor_tensor(self.cex[:], self.cum[:], self.tot[:], ALU.subtract))
        chain.link(dve.tensor_tensor(self.n[:], self.cum[:, :, NT - 1], self.cex[:, :, 0], ALU.subtract))
        chain.link(dve.tensor_scalar(self.ni[:], self.n[:], float(P - 1), None, ALU.add))
        chain.link(dve.tensor_scalar(self.ni[:], self.ni[:], 7, None, ALU.arith_shift_right))
        chain.link(dve.tensor_copy(self.nt[:], self.ni[:]))
        chain.link(dve.tensor_tensor_scan(self.tend[:], k.ones_f[:, 0:E], self.nt[:], 0.0, ALU.mult, ALU.add))
        chain.link(dve.tensor_tensor(self.adj[:], self.tend[:], self.nt[:], ALU.subtract))
        chain.link(dve.scalar_tensor_tensor(out=self.adj[:], in0=self.adj[:], scalar=float(P), in1=self.cex[:, :, 0],
                                            op0=ALU.mult, op1=ALU.subtract))
        before = k.bank[0][:, 0:NT * E].rearrange("p (t e) -> p t e", e=E)
        chain.link(dve.tensor_tensor(self.slot[:], before, self.cex[:].rearrange("p e t -> p t e"), ALU.add))
        chain.link(dve.tensor_tensor(self.slot[:], self.slot[:], over_t(self.adj[:]), ALU.add))
        for c in range(2):
            ins = dve.tensor_tensor(self.pick[:, c], self.slot[:], sel[c], ALU.mult)
        chain.link(ins)
        chain.link(dve.tensor_reduce(self.slotf[:], self.pick[:], AX.X, ALU.add))
        dve.tensor_copy(k.slots[:], self.slotf[:]).then_inc(self.slots_ready, 1)
        full = [1, SLOT_TILES, E]
        chain.link(dve.tensor_tensor(self.le[:], self.tend[0:1, :].unsqueeze(1).to_broadcast(full),
                                     k.tile_row[:].unsqueeze(2).to_broadcast(full), ALU.is_le))
        chain.link(dve.tensor_reduce(self.ef[:], self.le[:], AX.X, ALU.add))
        dve.tensor_scalar(k.tile_expert[:], self.ef[:], float(E - 1), None, ALU.min)

    def gpsimd(self, pool):
        k = self.k
        pool.wait_ge(k.slots_zeroed, 16)
        pool.wait_ge(self.slots_ready, 1)
        for t in range(NT):
            for c in range(2):
                pool.indirect_dma_start(k.slot_x, bass.IndirectOffsetOnAxis(ap=k.slots[:, c, t:t + 1], axis=0),
                                        self.b.ln_x[t // 4][:, t % 4, :], None).then_inc(self.scattered, 16)
        pool.wait_ge(self.scattered, (self.round + 1) * 16 * 2 * NT)


class ExpertTiles(Stage):

    U = 4

    def __init__(self, k, tag, kind, UF, HF):
        super().__init__(k)
        self.kind, self.UF, self.HF = kind, UF, HF
        self.weights_due = k.weights_due
        S_ = self.sem
        self.x_landed = [S_(f"x_landed{r}") for r in range(4)]
        self.tx_done, self.xT_out, self.up_done = S_("tx_done"), S_("xT_out"), S_("up_done")
        self.silu_ready, self.h_out, self.th_done, self.hT_out = S_("silu_ready"), S_("h_out"), S_("th_done"), S_("hT_out")
        self.dn_done, self.y_out = S_("dn_done"), S_("y_out")
        self.stored = [self.lasting_sem(f"stored{u}") for u in range(2)]
        self.stored_before = self.round * 16 * SLOT_TILES // 2
        sb = k.scoped
        self.xs = [sb(f"{tag}_xs{r}", [P, D], F32) for r in range(4)]
        self.xT = [sb(f"{tag}_xT{u}", [P, KC * P], F32) for u in range(2)]
        self.h = [sb(f"{tag}_h{u}", [P, HF * P], F32) for u in range(2)]
        self.hT = [sb(f"{tag}_hT{u}", [P, HF * P], F32) for u in range(2)]
        self.s = [sb(f"{tag}_s{u}", [P, HF * P], F32) for u in range(2)] if kind == "glu" else None
        self.y = [sb(f"{tag}_y{u}", [P, D], F32) for u in range(2)]

    def quads(self, eng, body):
        body(0, True, False)
        with eng.Fori(1, SLOT_TILES // self.U - 1) as i:
            body(i, False, False)
        body(SLOT_TILES // self.U - 1, False, True)

    def steps(self, i, first, last, lags):
        for n in range(self.U + (3 if last else 0)):
            for at, lag in enumerate(lags):
                m = n - lag
                if m >= self.U or (m < 0 and first):
                    continue
                yield at, (i if m >= 0 else i - 1), m % self.U

    def sync(self, sp):
        k = self.k
        rows = k.slot_x.rearrange("(j p) d -> j p d", p=P)
        with sp.Fori(0, SLOT_TILES // self.U) as i:
            for r in range(self.U):
                sp.wait_ge(self.tx_done, i * 4 + (r + 1))
                sp.dma_start(self.xs[r][:], rows[ds(i * 4 + r, 1)].rearrange("j p d -> (j p) d")).then_inc(self.x_landed[r], 16)

    def tensor(self, pe):
        k = self.k
        pe.sem_inc(self.tx_done, 4)
        pe.sem_inc(self.up_done, 2)
        pe.sem_inc(self.th_done, 2)
        pe.sem_inc(self.dn_done, 2)
        pe.wait_ge(k.weights_landed, self.weights_due)

        def expert(i, r):
            if isinstance(i, int):
                return pe.value_load(k.tile_expert[0:1, i * 4 + r:i * 4 + r + 1], min_val=0, max_val=E - 1)
            return pe.value_load(k.tile_expert[0:1, ds(i * 4 + r, 1)], min_val=0, max_val=E - 1)

        def turn_x(i, r):
            pe.wait_ge(self.x_landed[r], i * 16 + 16)
            pe.wait_ge(self.xT_out, i * 4 + (r + 1))
            for c in range(KC):
                ins = pe.transpose(k.bank[r % 2][:, c * P:(c + 1) * P], self.xs[r][:, c * P:(c + 1) * P], k.ident[:])
            ins.then_inc(self.tx_done, 1)

        def up(i, r):
            e = expert(i, r)
            pe.wait_ge(self.xT_out, i * 4 + (r + 3))
            pe.wait_ge(self.h_out, i * 4 + (r + 1))
            F = self.UF * P
            for c in range(KC):
                ins = pe.matmul(k.bank[2 + r % 2][:, 0:F], self.xT[r % 2][:, c * P:(c + 1) * P],
                                self.b.w_up[:, ds(e * (KC * F) + c * F, F)], start=c == 0, stop=c == KC - 1)
            ins.then_inc(self.up_done, 1)

        def turn_h(i, r):
            pe.wait_ge(self.h_out, i * 4 + (r + 3))
            pe.wait_ge(self.hT_out, i * 4 + (r + 1))
            for f in range(self.HF):
                ins = pe.transpose(k.bank[4 + r % 2][:, f * P:(f + 1) * P], self.h[r % 2][:, f * P:(f + 1) * P], k.ident[:])
            ins.then_inc(self.th_done, 1)

        def down(i, r):
            e = expert(i, r)
            pe.wait_ge(self.hT_out, i * 4 + (r + 3))
            pe.wait_ge(self.y_out, i * 4 + (r + 1))
            for f in range(self.HF):
                ins = pe.matmul(k.bank[6 + r % 2][:, 0:D], self.hT[r % 2][:, f * P:(f + 1) * P],
                                self.b.w_down[:, ds(e * (self.HF * D) + f * D, D)], start=f == 0, stop=f == self.HF - 1)
            ins.then_inc(self.dn_done, 1)

        def body(i, first, last):
            for at, gi, r in self.steps(i, first, last, (0, 1, 2, 3)):
                (turn_x, up, turn_h, down)[at](gi, r)

        self.quads(pe, body)

    def scalar(self, act):
        k = self.k
        act.sem_inc(self.xT_out, 2)
        act.sem_inc(self.hT_out, 2)

        def xT(i, r):
            act.wait_ge(self.tx_done, i * 4 + (r + 5))
            act.wait_ge(self.up_done, i * 4 + (r + 1))
            act.copy(self.xT[r % 2][:], k.bank[r % 2][:, 0:KC * P]).then_inc(self.xT_out, 1)

        def silu(i, r):
            if self.kind != "glu":
                return
            act.wait_ge(self.up_done, i * 4 + (r + 3))
            act.wait_ge(self.h_out, i * 4 + (r + 1))
            act.activation(self.s[r % 2][:], k.bank[2 + r % 2][:, 0:self.HF * P], ACT.Silu).then_inc(self.silu_ready, 1)

        def hT(i, r):
            act.wait_ge(self.th_done, i * 4 + (r + 3))
            act.wait_ge(self.dn_done, i * 4 + (r + 1))
            func = {"glu": ACT.Copy, "silu": ACT.Silu, "relu": ACT.Relu}[self.kind]
            act.activation(self.hT[r % 2][:], k.bank[4 + r % 2][:, 0:self.HF * P], func).then_inc(self.hT_out, 1)

        def body(i, first, last):
            for at, gi, r in self.steps(i, first, last, (0, 1, 2)):
                (xT, silu, hT)[at](gi, r)

        self.quads(act, body)

    def vector(self, dve):
        k = self.k
        dve.sem_inc(self.h_out, 2)
        dve.sem_inc(self.y_out, 2)
        W = self.HF * P

        def h(i, r):
            ps = k.bank[2 + r % 2]
            if self.kind == "relu":
                at = ds(i * 4 + r, 1) if not isinstance(i, int) else slice(i * 4 + r, i * 4 + r + 1)
                e = dve.value_load(k.tile_expert[0:1, at], min_val=0, max_val=E - 1)
            dve.wait_ge(self.th_done, i * 4 + (r + 1))
            dve.wait_ge(self.up_done, i * 4 + (r + 3))
            if self.kind == "glu":
                dve.wait_ge(self.silu_ready, i * 4 + (r + 1))
                ins = dve.tensor_tensor(self.h[r % 2][:], self.s[r % 2][:], ps[:, W:2 * W], ALU.mult)
            elif self.kind == "relu":
                ins = dve.tensor_tensor(self.h[r % 2][:], ps[:, 0:W], self.b.b1_all[:, ds(e * W, W)], ALU.add)
            else:
                ins = dve.tensor_copy(self.h[r % 2][:], ps[:, 0:W])
            ins.then_inc(self.h_out, 1)

        def y(i, r):
            if not (isinstance(i, int) and i == 0 and r < 2):
                dve.wait_ge(self.stored[r % 2], i * 32 + (self.stored_before + 16 * (r // 2)))
            dve.wait_ge(self.dn_done, i * 4 + (r + 3))
            dve.tensor_copy(self.y[r % 2][:], k.bank[6 + r % 2][:, 0:D]).then_inc(self.y_out, 1)

        def body(i, first, last):
            for at, gi, r in self.steps(i, first, last, (1, 3)):
                (h, y)[at](gi, r)

        if self.kind == "relu":
            dve.wait_ge(k.weights_landed, self.weights_due)
        self.quads(dve, body)

    def gpsimd(self, pool):
        k = self.k
        rows = k.slot_y.rearrange("(j p) d -> j p d", p=P)
        with pool.Fori(0, SLOT_TILES // self.U) as i:
            for r in range(self.U):
                wait_apart(pool, self.y_out, i * 4 + (r + 3), k.passed)
                pool.dma_start(rows[ds(i * 4 + r, 1)].rearrange("j p d -> (j p) d"), self.y[r % 2][:]).then_inc(self.stored[r % 2], 16)
        for u in range(2):
            pool.wait_ge(self.stored[u], self.stored_before + 16 * SLOT_TILES // 2)


class Combine(Stage):

    def __init__(self, k, tag):
        super().__init__(k)
        self.gathered = [self.lasting_sem(f"gathered{n}") for n in range(NT // 2)]
        self.own = self.sem("chain")
        self.rows = [[k.scoped(f"{tag}_rows{c}{t}", [P, D], F32) for t in range(NT)] for c in range(2)]

    def gpsimd(self, pool):
        k = self.k
        for t in range(NT):
            for c in range(2):
                pool.indirect_dma_start(self.rows[c][t][:], None, k.slot_y,
                                        bass.IndirectOffsetOnAxis(ap=k.slots[:, c, t:t + 1], axis=0)
                                        ).then_inc(self.gathered[t // 2], 16)

    def vector(self, dve):
        k = self.k
        for n in range(NT // 2):
            dve.wait_ge(self.gathered[n], (self.round + 1) * 64)
            for c in range(2):
                for t in (2 * n, 2 * n + 1):
                    x = k.x[:, t * D:(t + 1) * D]
                    ins = dve.scalar_tensor_tensor(out=x, in0=self.rows[c][t][:], scalar=self.b.rs[:, 4 + c, t:t + 1], in1=x,
                                                   op0=ALU.mult, op1=ALU.add)
                    ins.then_inc(self.own, 1)
                if c == 0:
                    dve.wait_ge(self.own, n * 4 + 2)


class Attention(Stage):

    H, DH = 16, 16
    HC = P // DH
    U = H // 2

    def __init__(self, k, tag, g, causal, wq, wk, wv, wo, bo, bq=None, bk=None, bv=None):
        super().__init__(k)
        self.g, self.causal = g, causal
        self.w = (wq, wk, wv, wo)
        self.biases = (bq, bk, bv, bo)
        self.bias = bq is not None
        self.qscale = 0.25 if causal else 0.0625
        S_ = self.sem
        self.w_landed = S_("w_landed")
        self.ctx_landed = [S_(f"ctx_landed{u}") for u in range(2)]
        self.proj_ready = S_("proj_ready")
        self.k_ready, self.q_ready, self.v_ready = S_("k_ready"), S_("q_ready"), S_("v_ready")
        self.km_ready, self.v_zeroed = S_("km_ready"), S_("v_zeroed")
        self.scores_ready = S_("scores_ready")
        self.max_ready, self.exp_ready = S_("max_ready"), S_("exp_ready")
        self.rsum_ready, self.scaled, self.turned = S_("rsum_ready"), S_("scaled"), S_("turned")
        self.pt_ready = [S_(f"pt_ready{m}") for m in range(2)]
        self.pv_done = S_("pv_done")
        self.ot_ready, self.y_ready, self.added = S_("ot_ready"), S_("y_ready"), S_("added")
        sb = k.scoped
        self.wt = [sb(f"{tag}_w{n}", [P, KC, D], F32) for n in range(4)]
        self.bqk = sb(tag + "_bqk", [P, 2, KC], F32)
        self.bvb = sb(tag + "_bvb", [P, D], F32)
        self.bo = sb(tag + "_bo", [1, D], F32)
        self.cT = [sb(f"{tag}_cT{u}", [P, KC, S], F32) for u in range(2)]
        self.kT = sb(f"{tag}_kT", [P, KC * S], F32)
        self.km = [sb(f"{tag}_km{u}", [P, KC, self.HC, S], F32) for u in range(2)]
        self.qT = [sb(f"{tag}_qT{u}", [P, KC * S], F32) for u in range(2)]
        self.v = [[sb(f"{tag}_v{u}{m}", [P, HALVES, D], F32) for m in range(2)] for u in range(2)]
        self.p = [sb(f"{tag}_p{n}", [P, HALVES, 2, S], F32) for n in range(4)]
        self.pT = [sb(f"{tag}_pT{n}", [P, 2, HALVES * S], F32) for n in range(2)]
        self.nmax = [sb(f"{tag}_nmax{u}", [P, self.U * 4], F32) for u in range(2)]
        self.sum = [sb(f"{tag}_sum{u}", [P, self.U * 4], F32) for u in range(2)]
        self.oT = sb(tag + "_oT", [P, KC * S], F32)
        self.n_loads = 5 + 3 * self.bias

    def width(self, s):
        return (s + 1) * P if self.causal else S

    def blocks(self):
        for t in range(HALVES):
            first = t if self.causal else 0
            for s in range(first, HALVES):
                yield t, s, t * S + (s - first) * P

    def sync(self, sp):
        k = self.k
        for wt, w in zip(self.wt, self.w):
            sp.dma_start(wt[:], w.rearrange("(c p) f -> p c f", p=P)).then_inc(self.w_landed, 16)
        bq, bk, bv, bo = self.biases
        sp.dma_start(self.bo[:], bo.unsqueeze(0)).then_inc(self.w_landed, 16)
        if self.bias:
            sp.dma_start(self.bqk[:, 0, :], bq).then_inc(self.w_landed, 16)
            sp.dma_start(self.bqk[:, 1, :], bk).then_inc(self.w_landed, 16)
            sp.dma_start(self.bvb[:], bv.partition_broadcast(P)).then_inc(self.w_landed, 16)
        ctxT = k.ins["ctxT"].rearrange("(c p) t -> p c t", p=P)
        with sp.Fori(0, B // 2) as i:
            for u in range(2):
                sp.wait_ge(self.proj_ready, i * 6 + 3 * u + 1)
                sp.dma_start(self.cT[u][:], ctxT[:, :, ds(i * 2 * S + u * S, S)]).then_inc(self.ctx_landed[u], 16)

    def pairs(self, eng, body):
        body(0, True, False)
        with eng.Fori(1, B // 2 - 1) as i:
            body(i, False, False)
        body(B // 2 - 1, False, True)

    def lagged(self, i, n, lag, first):
        m = n - lag
        if m >= 0:
            return i, m // self.U, m % self.U
        return None if first else (i - 1, 1, self.U + m)

    def tensor(self, pe):
        k = self.k
        wq, wk, wv, wo = self.wt
        pe.sem_inc(self.proj_ready, 4)
        pe.sem_inc(self.scores_ready, 9)
        pe.sem_inc(self.turned, 4)
        pe.sem_inc(self.pv_done, 2)
        pe.sem_inc(self.y_ready, 1)
        pe.wait_ge(self.w_landed, 16 * self.n_loads)

        def proj_k(i, u):
            b = i * 2 + u
            pe.wait_ge(self.ctx_landed[u], i * 16 + 16)
            pe.wait_ge(self.added, b + 1)
            if not (isinstance(b, int) and b == 0):
                pe.wait_ge(self.v_ready, i * 4 + 2 * u)
            for f in range(KC):
                for c in range(KC):
                    ins = pe.matmul(k.bank[7][:, f * S:(f + 1) * S], wk[:, c, f * P:(f + 1) * P],
                                    self.cT[u][:, c, :], start=c == 0, stop=c == KC - 1)
            ins.then_inc(self.proj_ready, 1)

        def proj_q(i, u):
            pe.wait_ge(self.k_ready, i * 4 + (2 * u + 2))
            for f in range(KC):
                for c in range(KC):
                    ins = pe.matmul(k.bank[7][:, f * S:(f + 1) * S], wq[:, c, f * P:(f + 1) * P],
                                    k.lnT[:, ds(i * 2 * S + (c * T + u * S), S)], start=c == 0, stop=c == KC - 1)
            ins.then_inc(self.proj_ready, 1)

        def proj_v(i, u):
            pe.wait_ge(self.q_ready, i * 4 + (2 * u + 2))
            for t in range(HALVES):
                for c in range(KC):
                    ins = pe.matmul(k.bank[7][:, t * D:(t + 1) * D], self.cT[u][:, c, t * P:(t + 1) * P],
                                    wv[:, c, :], start=c == 0, stop=c == KC - 1)
            ins.then_inc(self.proj_ready, 1)

        def scores(i, u, r):
            n = (i * 2 + u) * self.U
            if r == 0:
                pe.wait_ge(self.q_ready, i * 4 + (2 * u + 2))
                pe.wait_ge(self.km_ready, i * 4 + (2 * u + 3))
            pe.wait_ge(self.exp_ready, n + (r + 1))
            c, hc = divmod(2 * r, self.HC)
            for s in range(HALVES):
                w = self.width(s)
                bank = k.bank[2 * (r % 2) + s][:].rearrange("p (m t) -> p m t", m=2)
                ins = pe.matmul(bank[:, :, 0:w], self.qT[u][:, c * S + s * P:c * S + (s + 1) * P],
                                self.km[u][:, c, hc:hc + 2, 0:w], start=True, stop=not self.causal)
                if self.causal:
                    ins = pe.matmul(bank[:, :, s * P:(s + 1) * P], k.ident_bf[:],
                                    k.causal_bf[:].unsqueeze(1).to_broadcast([P, 2, P]), start=False, stop=True)
                ins.then_inc(self.scores_ready, 1) if s == HALVES - 1 else None

        def turn(i, u, r):
            n = (i * 2 + u) * self.U
            pe.wait_ge(self.scaled, n + (r + 1))
            for m in range(2):
                pe.wait_ge(self.pt_ready[m], n + (r + 1))
                for t, s, at in self.blocks():
                    ins = pe.transpose(k.bank[4 + m][:, at:at + P], self.p[r % 4][:, s, m, t * P:(t + 1) * P], k.ident[:])
            ins.then_inc(self.turned, 1)

        def pv(i, u, r):
            n = (i * 2 + u) * self.U
            if r == 0:
                pe.wait_ge(self.v_ready, i * 4 + (2 * u + 2))
                pe.wait_ge(self.ot_ready, i * 2 + (u + 1))
            c, strip = divmod(r, 4)
            for m in range(2):
                pe.wait_ge(self.pt_ready[m], n + (r + 2))
                for t in range(HALVES):
                    w = S - t * P if self.causal else S
                    ins = pe.matmul(k.bank[6][32 * strip:32 * strip + 32, (c + 1) * S - w:(c + 1) * S],
                                    self.v[u][m][:, t, 32 * r:32 * r + 32], self.pT[r % 2][:, m, t * S:t * S + w],
                                    start=m == 0 and t == 0, stop=m == 1 and t == HALVES - 1)
            ins.then_inc(self.pv_done, 1)

        def out(i, u, last):
            pe.wait_ge(self.ot_ready, i * 2 + (u + 2))
            if last:
                pe.wait_ge(self.added, B - 1 + 3)
            else:
                pe.wait_ge(self.v_ready, i * 4 + (2 * u + 6))
            for s in range(HALVES):
                pe.matmul(k.bank[7][:, s * D:(s + 1) * D], k.ones_row, self.bo[:], start=True, stop=False)
                for c in range(KC):
                    ins = pe.matmul(k.bank[7][:, s * D:(s + 1) * D], self.oT[:, c * S + s * P:c * S + (s + 1) * P],
                                    wo[:, c, :], start=False, stop=c == KC - 1)
            ins.then_inc(self.y_ready, 1)

        def out6():
            pe.wait_ge(self.ot_ready, B)
            pe.wait_ge(self.v_ready, 2 * B)
            for s in range(HALVES):
                pe.matmul(k.bank[7][:, s * D:(s + 1) * D], k.ones_row, self.bo[:], start=True, stop=False)
                for c in range(KC):
                    ins = pe.matmul(k.bank[7][:, s * D:(s + 1) * D], self.oT[:, c * S + s * P:c * S + (s + 1) * P],
                                    wo[:, c, :], start=False, stop=c == KC - 1)
            ins.then_inc(self.y_ready, 1)

        def body(i, first, last):
            if first:
                proj_k(0, 0)
                proj_q(0, 0)
                proj_v(0, 0)
            for n in range(2 * self.U + (3 if last else 0)):
                u, r = divmod(n, self.U)
                if u < 2:
                    scores(i, u, r)
                for step, lag in ((turn, 2), (pv, 3)):
                    unit = self.lagged(i, n, lag, first)
                    if unit and unit[1] < 2:
                        step(*unit)
                if u == 2:
                    continue
                nxt = (i, 1) if u == 0 else (i + 1, 0)
                prev = (i, 0) if u else (i - 1, 1)
                if r in (1, 2, 3) and not (last and u == 1):
                    (proj_k, proj_q, proj_v)[r - 1](*nxt)
                if r == 4 and not (first and u == 0):
                    if last and u == 1:
                        out6()
                    else:
                        out(*prev, False)
            if last:
                out(i, 1, True)

        self.pairs(pe, body)

    def scalar(self, act):
        k = self.k
        act.sem_inc(self.exp_ready, 2)
        act.sem_inc(self.pt_ready[0], 1)
        act.sem_inc(self.ot_ready, 1)
        if self.bias:
            act.wait_ge(self.w_landed, 16 * self.n_loads)

        def k_out(i, u):
            act.wait_ge(self.proj_ready, i * 6 + (3 * u + 5))
            act.wait_ge(self.km_ready, i * 4 + (2 * u + 1))
            for c in range(KC):
                src, dst = k.bank[7][:, c * S:(c + 1) * S], self.kT[:, c * S:(c + 1) * S]
                if self.bias:
                    ins = act.activation(dst, src, ACT.Identity, bias=self.bqk[:, 1, c:c + 1])
                else:
                    ins = act.copy(dst, src)
                ins.then_inc(self.k_ready, 1)

        def exps(i, u, r):
            n = (i * 2 + u) * self.U
            act.wait_ge(self.max_ready, n + (r + 1))
            act.wait_ge(self.turned, n + (r + 1))
            for s in range(HALVES):
                w = self.width(s)
                for m in range(2):
                    col = r * 4 + s * 2 + m
                    ins = act.activation(self.p[r % 4][:, s, m, 0:w], k.bank[2 * (r % 2) + s][:, m * S:m * S + w], ACT.Exp,
                                         bias=self.nmax[u][:, col:col + 1], accum_out=self.sum[u][:, col:col + 1])
            ins.then_inc(self.exp_ready, 1)

        def o_out(i, u):
            act.wait_ge(self.pv_done, (i * 2 + u) * self.U + (self.U + 2))
            act.wait_ge(self.y_ready, i * 2 + (u + 1))
            act.copy(self.oT[:], k.bank[6][:]).then_inc(self.ot_ready, 1)

        def body(i, first, last):
            if first:
                k_out(0, 0)
            for n in range(2 * self.U + (3 if last else 0)):
                u, r = divmod(n, self.U)
                if u < 2:
                    exps(i, u, r)
                unit = self.lagged(i, n, 2, first)
                if unit and unit[1] < 2:
                    self.pt_out(act, act.copy, 0, *unit)
                if u == 2:
                    continue
                if r == 1 and not (last and u == 1):
                    k_out(*((i, 1) if u == 0 else (i + 1, 0)))
                if r == 3 and not (first and u == 0):
                    o_out(*((i, 0) if u else (i - 1, 1)))
            if last:
                o_out(i, 1)

        self.pairs(act, body)

    def pt_out(self, eng, copy, m, i, u, r):
        n = (i * 2 + u) * self.U
        w = S + P if self.causal else 2 * S
        eng.wait_ge(self.turned, n + (r + 5))
        eng.wait_ge(self.pv_done, n + (r + 1))
        copy(self.pT[r % 2][:, m, 0:w], self.k.bank[4 + m][:, 0:w]).then_inc(self.pt_ready[m], 1)

    def vector(self, dve):
        k = self.k
        dve.sem_inc(self.pt_ready[1], 1)
        dve.sem_inc(self.added, 3)
        dve.wait_ge(self.v_zeroed, 4)
        if self.bias:
            dve.wait_ge(self.w_landed, 16 * self.n_loads)

        def q_out(i, u):
            dve.wait_ge(self.proj_ready, i * 6 + (3 * u + 6))
            for c in range(KC):
                src, dst = k.bank[7][:, c * S:(c + 1) * S], self.qT[u][:, c * S:(c + 1) * S]
                if self.bias:
                    ins = dve.tensor_scalar(dst, src, self.bqk[:, 0, c:c + 1], self.qscale, ALU.add, ALU.mult)
                else:
                    ins = dve.tensor_scalar(dst, src, self.qscale, None, ALU.mult)
                ins.then_inc(self.q_ready, 1)

        def v_out(i, u):
            dve.wait_ge(self.proj_ready, i * 6 + (3 * u + 7))
            view = lambda a, m: a.rearrange("p (s h e d) -> p s h e d", s=HALVES, e=2, d=self.DH)[:, :, :, m, :]
            for m in range(2):
                dst = view(self.v[u][m][:].rearrange("p s d -> p (s d)"), m)
                if self.bias:
                    bias = self.bvb[:].rearrange("p (h e d) -> p h e d", e=2, d=self.DH)[:, :, m, :]
                    ins = [dve.tensor_tensor(dst[:, s], view(k.bank[7][:], m)[:, s], bias, ALU.add)
                           for s in range(HALVES)][-1]
                else:
                    ins = dve.tensor_copy(dst, view(k.bank[7][:], m))
                ins.then_inc(self.v_ready, 1)

        def maxes(i, u, r):
            n = (i * 2 + u) * self.U
            dve.wait_ge(self.scores_ready, n + (r + 10))
            for s in range(HALVES):
                col = r * 4 + s * 2
                ins = dve.tensor_reduce(self.nmax[u][:, col:col + 2],
                                        k.bank[2 * (r % 2) + s][:].rearrange("p (m t) -> p m t", m=2)[:, :, 0:self.width(s)],
                                        AX.X, ALU.max, negate=True)
            ins.then_inc(self.max_ready, 1)

        def recips(i, u, r):
            n = (i * 2 + u) * self.U
            dve.wait_ge(self.exp_ready, n + (r + 3))
            sums = self.sum[u][:, r * 4:r * 4 + 4]
            dve.reciprocal(sums, sums).then_inc(self.rsum_ready, 1)

        def add(i, u):
            dve.wait_ge(self.y_ready, i * 2 + (u + 2))
            dyn = i * 4 * D + u * 2 * D
            xb = k.x[:, ds(dyn, 2 * D)]
            dve.scalar_tensor_tensor(out=xb, in0=k.bank[7][:], scalar=k.tanh_g[:, self.g:self.g + 1], in1=xb,
                                     op0=ALU.mult, op1=ALU.add).then_inc(self.added, 1)

        def body(i, first, last):
            if first:
                q_out(0, 0)
                v_out(0, 0)
            for n in range(2 * self.U + (3 if last else 0)):
                u, r = divmod(n, self.U)
                if u < 2:
                    maxes(i, u, r)
                unit = self.lagged(i, n, 1, first)
                if unit and unit[1] < 2:
                    recips(*unit)
                unit = self.lagged(i, n, 2, first)
                if unit and unit[1] < 2:
                    self.pt_out(dve, dve.tensor_copy, 1, *unit)
                if u == 2:
                    continue
                nxt = (i, 1) if u == 0 else (i + 1, 0)
                if r == 2 and not (last and u == 1):
                    q_out(*nxt)
                if r == 3 and not (last and u == 1):
                    v_out(*nxt)
                if r == 5 and not (first and u == 0):
                    add(*((i, 0) if u else (i - 1, 1)))
            if last:
                add(i, 1)

        self.pairs(dve, body)

    def gpsimd(self, pool):
        k = self.k
        for u in range(2):
            for m in range(2):
                pool.memset(self.v[u][m][:], 0.0).then_inc(self.v_zeroed, 1)
        pool.sem_inc(self.km_ready, 1)

        def mask_k(i, u):
            pool.wait_ge(self.k_ready, i * 4 + (2 * u + 2))
            pool.wait_ge(self.scores_ready, i * 2 * self.U + (u * self.U + 1))
            full = [P, self.HC, S]
            for c in range(KC):
                pool.tensor_tensor(self.km[u][:, c], self.kT[:, c * S:(c + 1) * S].unsqueeze(1).to_broadcast(full),
                                   k.head16[:].unsqueeze(2).to_broadcast(full), ALU.mult).then_inc(self.km_ready, 1)

        def scale(i, u, r):
            n = (i * 2 + u) * self.U
            pool.wait_ge(self.rsum_ready, n + (r + 1))
            for s in range(HALVES):
                w = self.width(s)
                p = self.p[r % 4][:, s, :, 0:w]
                ins = pool.tensor_tensor(p, p, self.sum[u][:, r * 4 + s * 2:r * 4 + s * 2 + 2].unsqueeze(2)
                                         .to_broadcast([P, 2, w]), ALU.mult)
            ins.then_inc(self.scaled, 1)

        def body(i, first, last):
            if first:
                mask_k(0, 0)
            for n in range(2 * self.U + (3 if last else 0)):
                u, r = divmod(n, self.U)
                unit = self.lagged(i, n, 1, first)
                if unit and unit[1] < 2:
                    scale(*unit)
                if u < 2 and r == 1 and not (last and u == 1):
                    mask_k(*((i, 1) if u == 0 else (i + 1, 0)))

        self.pairs(pool, body)


class MlstmGates(Stage):

    def __init__(self, k, tag, NH, w, bias, shifted, cols, negm, beside=None):
        super().__init__(k)
        self.beside = beside
        self.NH, self.R, self.shifted = NH, B * NH, shifted
        self.w, self.bias, self.cols, self.negm = w, bias, cols, negm
        S_ = self.sem
        self.landed, self.logits_ready, self.own = S_("landed"), S_("logits_ready"), S_("chain")
        self.abs_ready, self.exp_ready, self.ln_ready = S_("abs_ready"), S_("exp_ready"), S_("ln_ready")
        self.g_ready, self.rows_turned = S_("g_ready"), S_("rows_turned")
        self.negm_ready, self.m_ready, self.en_ready = S_("negm_ready"), S_("m_ready"), S_("en_ready")
        self.cols_turned, self.negm_stored = S_("cols_turned"), S_("negm_stored")
        sb, R = k.scoped, self.R
        self.ctxT = sb(tag + "_ctxT", [P, KC * T], F32)
        self.wg = sb(tag + "_wg", [P, 3 * KC, 2 * NH], F32)
        self.bg = sb(tag + "_bg", [P, 2 * NH], F32)
        self.g = [sb(f"{tag}_g{n}", [P, HALVES * R], F32) for n in range(2)]
        self.t = sb(tag + "_t", [P, HALVES * R], F32)
        self.rows = sb(tag + "_rows", [R, 2 * S], F32)
        self.ones = sb(tag + "_ones", [R, S], F32)
        self.cs, self.a, self.M, self.m, self.nm, self.en = (sb(f"{tag}_{n}", [R, S], F32)
                                                             for n in ("cs", "a", "M", "m", "nm", "en"))

    def sync(self, sp):
        k = self.k
        sp.dma_start(self.wg[:], self.w.rearrange("(c p) g -> p c g", p=P)).then_inc(self.landed, 16)
        sp.dma_start(self.bg[:], self.bias.partition_broadcast(P)).then_inc(self.landed, 16)
        sp.dma_start(self.ctxT[:].rearrange("p (c t) -> p c t", c=KC),
                     k.ins["ctxT"].rearrange("(c p) t -> p c t", p=P)).then_inc(self.landed, 16)
        sp.wait_ge(self.negm_ready, 1)
        sp.dma_start(self.negm, self.nm[:]).then_inc(self.negm_stored, 16)
        sp.wait_ge(self.negm_stored, 16)

    def gpsimd(self, pool):
        if self.beside:
            self.beside.ahead_gpsimd(pool, LayerNorm.AHEAD, self.beside.body_units(0) + self.beside.body_units(1))

    def tensor(self, pe):
        k, R, G = self.k, self.R, 2 * self.NH
        pe.wait_ge(self.landed, 48)
        for t in range(NT):
            for n in range(3 * KC):
                src = k.lnT if n < KC else self.ctxT
                c = n % KC
                ins = pe.matmul(k.bank[0][:, t * G:(t + 1) * G], src[:, c * T + t * P:c * T + (t + 1) * P],
                                self.wg[:, n, :], start=n == 0, stop=n == 3 * KC - 1)
        ins.then_inc(self.logits_ready, 1)
        pe.wait_ge(self.g_ready, 2)
        for kind in range(2):
            for half in range(HALVES):
                n = kind * HALVES + half
                ins = pe.transpose(k.bank[1][0:R, n * P:(n + 1) * P], self.g[kind][:, half * R:(half + 1) * R], k.ident[:])
        ins.then_inc(self.rows_turned, 1)
        pe.wait_ge(self.negm_ready, 1)
        pe.wait_ge(self.en_ready, 1)
        for n, rows in enumerate((self.a, self.en)):
            for half in range(HALVES):
                at = (n * HALVES + half) * R
                ins = pe.transpose(k.bank[2][:, at:at + R], rows[:, half * P:(half + 1) * P], k.ident[0:R, 0:R])
        ins.then_inc(self.cols_turned, 1)

    def vector(self, dve):
        k, R, NH = self.k, self.R, self.NH
        chain = Chain(dve, self.own)
        dve.memset(self.ones[:], 1.0)
        dve.wait_ge(self.logits_ready, 1)
        ps = k.bank[0][:, 0:NT * 2 * NH].rearrange("p (b s k h) -> p s b k h", s=HALVES, k=2, h=NH)
        for kind in range(2):
            for half in range(HALVES):
                bias = self.bg[:, kind * NH:(kind + 1) * NH].unsqueeze(1).to_broadcast([P, B, NH])
                ins = dve.tensor_tensor(self.g[kind][:, half * R:(half + 1) * R].rearrange("p (b h) -> p b h", h=NH),
                                        ps[:, half, :, kind, :], bias, ALU.add)
                chain.link(ins)
        fg = self.g[1]
        dve.sem_inc(self.g_ready, 1)
        dve.wait_ge(self.ln_ready, 1)
        dve.scalar_tensor_tensor(out=fg[:], in0=fg[:], scalar=0.0, in1=self.t[:], op0=ALU.min,
                                 op1=ALU.subtract).then_inc(self.g_ready, 1)
        dve.wait_ge(self.rows_turned, 1)
        chain.link(dve.tensor_copy(self.rows[:], k.bank[1][0:R, :]))
        ig, lf = self.rows[:, 0:S], self.rows[:, S:2 * S]
        chain.link(dve.tensor_tensor_scan(self.cs[:], self.ones[:], lf, 0.0, ALU.mult, ALU.add))
        if self.shifted:
            dve.tensor_copy(self.a[:, 0:1], ig[:, 0:1])
            chain.link(dve.tensor_tensor(self.a[:, 1:S], ig[:, 1:S], self.cs[:, 0:S - 1], ALU.subtract))
        else:
            chain.link(dve.tensor_tensor(self.a[:], ig, self.cs[:], ALU.subtract))
        chain.link(dve.tensor_tensor_scan(self.M[:], self.ones[:], self.a[:], -3e38, ALU.mult, ALU.max))
        dve.tensor_tensor(self.m[:], self.cs[:], self.M[:], ALU.add).then_inc(self.m_ready, 1)
        dve.tensor_scalar(self.nm[:], self.M[:], -1.0, None, ALU.mult).then_inc(self.negm_ready, 1)
        dve.wait_ge(self.cols_turned, 1)
        dve.tensor_copy(self.cols[:], k.bank[2][:, 0:2 * HALVES * R])

    def scalar(self, act):
        act.wait_ge(self.g_ready, 1)
        act.activation(self.t[:], self.g[1][:], ACT.Abs).then_inc(self.abs_ready, 1)
        act.wait_ge(self.abs_ready, 1)
        act.activation(self.t[:], self.t[:], ACT.Exp, scale=-1.0).then_inc(self.exp_ready, 1)
        act.wait_ge(self.exp_ready, 1)
        act.activation(self.t[:], self.t[:], ACT.Ln, bias=1.0).then_inc(self.ln_ready, 1)
        act.wait_ge(self.m_ready, 1)
        act.activation(self.en[:], self.m[:], ACT.Exp, scale=-1.0).then_inc(self.en_ready, 1)


class Hops(Stage):

    STEPS = 16
    SB = (8, 2)
    TRIANGLE = (((0, 3, 0),), ((0, 3, 1),), ((0, 2, 0), (96, 0, 0)), ((0, 2, 1), (96, 0, 1)), ((0, 1, 0), (64, 1, 1)))
    FULL = tuple(((0, q, e),) for q in range(4) for e in range(2))
    UNITS = (5, 13)
    PAIRS = (3, 7)
    W = 64
    PT = 4

    def __init__(self, k, tag, kh_all, rpe, hop_units):
        super().__init__(k)
        self.kh_all, self.kh = kh_all, kh_split(kh_all)
        self.rpe, self.hop_units = rpe, hop_units
        S_, L_ = self.sem, self.lasting_sem
        self.idx_landed, self.idx_copied = L_("idx_landed"), S_("idx_copied")
        self.gathered = [[L_(f"gathered{phase}{h}") for h in range(2)] for phase in range(2)]
        self.turned, self.zeroed = S_("turned"), S_("zeroed")
        self.peT_ready = [S_(f"peT_ready{u}") for u in range(2)]
        self.q_ready, self.kmm_done = S_("q_ready"), S_("kmm_done")
        self.kh_out = [S_(f"kh_out{mb}") for mb in range(2)]
        self.idx = k.held(f"{tag}_idx", [P, self.STEPS * sum(self.UNITS)], I32)
        rows = k.held(f"{tag}_rows", [P, self.SB[1] * self.UNITS[1] * D], F32)
        self.rows = (kh_all[:, P * self.W:P * self.W + self.SB[0] * self.UNITS[0] * D], rows[:])

    def buffers(self, tag):
        sb = self.k.scoped
        self.now = [sb(f"{tag}_now{h}", [P, self.UNITS[1]], I32) for h in range(2)]
        self.peT = [sb(f"{tag}_peT{u}", [P, 4 * P], F32) for u in range(self.PT)]
        self.q = [sb(f"{tag}_q{h}", [P, KC, 4, 2, 32], F32) for h in range(2)]

    def gather(self, pool, phase, n, index):
        pool.indirect_dma_start(self.rows[phase][:, n * D:(n + 1) * D], None, self.rpe,
                                bass.IndirectOffsetOnAxis(ap=index, axis=0)
                                ).then_inc(self.gathered[phase][n // (self.SB[phase] * self.UNITS[phase] // 2)], 16)

    def body_units(self, phase):
        return self.SB[phase] * self.UNITS[phase]

    def pair_of(self, phase, n):
        step, u = divmod(n, self.UNITS[phase])
        return step * self.PAIRS[phase] + u // 2

    def ahead_sync(self, sp):
        sp.dma_start(self.idx[:], self.hop_units).then_inc(self.idx_landed, 16)

    def ahead_gpsimd(self, pool, first, last):
        if first == 0:
            pool.wait_ge(self.idx_landed, 16)
        for n in range(first, last):
            phase = n >= self.body_units(0)
            at = n + phase * (self.STEPS * self.UNITS[0] - self.body_units(0))
            self.gather(pool, phase, n - phase * self.body_units(0), self.idx[:, at:at + 1])

    def gpsimd(self, pool):
        last = -1
        for n in range(self.body_units(0)):
            pair = self.pair_of(0, n)
            if pair != last:
                pool.wait_ge(self.turned, pair + 1)
            last = pair
            at = self.body_units(0) + n
            self.gather(pool, 0, n, self.idx[:, at:at + 1])
        U = self.UNITS[1]
        with pool.Fori(1, self.STEPS // self.SB[1]) as i:
            for n in range(self.body_units(1)):
                h, u = divmod(n, U)
                if u % 2 == 0:
                    wait_apart(pool, self.turned, i * 14 + (48 - 14 + self.pair_of(1, n) + 1), self.k.passed)
                if u == 0:
                    pool.tensor_copy(self.now[h][:], self.idx[:, ds(i * 2 * U + (self.STEPS * self.UNITS[0] + h * U), U)]
                                     ).then_inc(self.idx_copied, 1)
                    wait_apart(pool, self.idx_copied, i * 2 + (h - 1), self.k.passed)
                self.gather(pool, 1, n, self.now[h][:, u:u + 1])

    def phases(self, eng):
        for phase in range(2):
            with eng.Fori(0, self.STEPS // self.SB[phase]) as i:
                yield phase, i

    def pairs_done(self, phase, i, p):
        return i * (24, 14)[phase] + ((0, 48)[phase] + p + 1)

    def before(self, phase, p):
        if phase == 0 or p >= self.PT:
            return p - self.PT
        return p - 2 if p < 2 else p - 6

    def tensor(self, pe):
        k = self.k
        pe.sem_inc(self.kmm_done, 4)
        pe.wait_ge(self.zeroed, 1)

        def ready(phase, i, p, credit=2):
            return i * (12, 7)[phase] + ((0, 24)[phase] + p // 2 + 1 + credit)

        def turn(phase, i, p):
            step, pair = divmod(p, self.PAIRS[phase])
            if p % (self.SB[phase] * self.PAIRS[phase] // 2) == 0:
                sem = self.gathered[phase][2 * step // self.SB[phase]]
                landed = 16 * self.body_units(phase) // 2
                pe.wait_ge(sem, i * landed + landed)
            pe.wait_ge(self.peT_ready[p % 2], ready(phase, i, self.before(phase, p)))
            single = pair == self.PAIRS[phase] - 1
            for u in range(1 if single else 2):
                n = step * self.UNITS[phase] + 2 * pair + u
                for c in range(KC):
                    at = n * D + c * P
                    ins = pe.transpose(k.bank[p % 4][:, (u * KC + c) * P:(u * KC + c + 1) * P],
                                       self.rows[phase][:, at:at + P], k.ident[:])
            ins.then_inc(self.turned, 1)

        def mult(phase, i, p):
            step, pair = divmod(p, self.PAIRS[phase])
            pe.wait_ge(self.peT_ready[p % 2], ready(phase, i, p))
            if pair == 0:
                SB = self.SB[phase]
                pe.wait_ge(self.q_ready, i * (4 * SB) + (64 * phase + 4 * step + 4))
                pe.wait_ge(self.kh_out[0], i * SB + (16 * phase + step + 1))
                if phase:
                    pe.wait_ge(self.kh_out[1], i * SB + (step + 1))
            units = self.TRIANGLE + self.FULL
            for u, unit in enumerate(units[2 * pair:min(2 * pair + 2, self.UNITS[phase])]):
                mb = phase if 2 * pair + u < len(self.TRIANGLE) else 0
                for first, quarter, e in unit:
                    rows = 32 * (quarter + 1) if 2 * pair + u < len(self.TRIANGLE) else P
                    for c in range(KC):
                        at = (u * KC + c) * P + first
                        to = (quarter * 2 + e) * self.W + c * 32
                        ins = pe.matmul(k.bank[4 + 2 * (step % 2) + mb][0:rows, to:to + 32],
                                        self.peT[p % self.PT][:, at:at + rows],
                                        self.q[step % 2][:, c, quarter, e, :], start=True, stop=True)
            ins.then_inc(self.kmm_done, 1)

        for phase, i in self.phases(pe):
            pairs = self.SB[phase] * self.PAIRS[phase]
            for p in range(pairs + 2):
                if p < pairs:
                    turn(phase, i, p)
                if p >= 2:
                    mult(phase, i, p - 2)

    def out_of_psum(self, eng, copy, mine):
        for phase, i in self.phases(eng):
            SB, PAIRS = self.SB[phase], self.PAIRS[phase]
            for p in range(SB * PAIRS):
                step, pair = divmod(p, PAIRS)
                if mine and pair == 0:
                    self.spread(eng, phase, i, step)
                if p % 2 == mine:
                    self.peT_out(eng, copy, phase, i, p, step, pair)
                if step and pair == 2 and mine <= phase:
                    self.kh_to_sbuf(eng, copy, mine, phase, i, step - 1)
            if mine <= phase:
                self.kh_to_sbuf(eng, copy, mine, phase, i, SB - 1)

    def peT_out(self, eng, copy, phase, i, p, step, pair):
        w = (1 if pair == self.PAIRS[phase] - 1 else 2) * KC * P
        eng.wait_ge(self.turned, self.pairs_done(phase, i, p))
        eng.wait_ge(self.kmm_done, self.pairs_done(phase, i, self.before(phase, p)) + 4)
        copy(self.peT[p % self.PT][:, 0:w], self.k.bank[p % 4][:, 0:w]).then_inc(self.peT_ready[p % 2], 1)

    def kh_to_sbuf(self, eng, copy, mb, phase, i, step):
        eng.wait_ge(self.kmm_done, self.pairs_done(phase, i, (step + 1) * self.PAIRS[phase] - 1) + 4)
        first = P * self.W if phase and mb == 0 else 0
        kh = self.kh[mb][:, first:first + P * self.W].rearrange("p (q w) -> p q w", q=4)
        bank = self.k.bank[4 + 2 * (step % 2) + (mb if phase else 0)]
        copy(kh[:, :, ds(i * (2 * self.SB[phase] * self.W) + step * 2 * self.W, 2 * self.W)],
             bank[:].rearrange("p (q w) -> p q w", q=4)).then_inc(self.kh_out[mb], 1)

    def spread(self, dve, phase, i, step):
        k = self.k
        dve.wait_ge(self.kmm_done, i * 24 + (3 * step + 1) if phase == 0 else i * 14 + (52 if step else 49))
        lnT = k.lnT[:].rearrange("p (c b h q s) -> p c h s q b", c=KC, b=B, h=HALVES, q=4)
        full = [P, 4, B, 4]
        for c in range(KC):
            for e in range(2):
                src = lnT[:, c, phase, ds(i * (2 * self.SB[phase]) + (2 * step + e), 1)].rearrange("p o q b -> p (o q) b")
                dve.tensor_tensor(self.q[step % 2][:, c, :, e, :].rearrange("p q (b r) -> p q b r", r=4),
                                  src.unsqueeze(3).to_broadcast(full),
                                  k.strip[:].unsqueeze(1).unsqueeze(1).to_broadcast(full), ALU.mult).then_inc(self.q_ready, 1)

    def scalar(self, act):
        act.sem_inc(self.peT_ready[0], 2)
        act.sem_inc(self.kh_out[0], 2)
        self.out_of_psum(act, act.copy, 0)

    def vector(self, dve):
        dve.memset(self.k.ps[:, 4 * 512:8 * 512], 0.0).then_inc(self.zeroed, 1)
        dve.sem_inc(self.peT_ready[1], 2)
        dve.sem_inc(self.kh_out[1], 2)
        self.out_of_psum(dve, dve.tensor_copy, 1)


def kh_split(kh_all):
    return [kh_all[:, 0:S * 64], kh_all[:, S * 64:(S + P) * 64]]


class Mlstm(Stage):

    def __init__(self, k, tag, NH, eps, cols, negm, var, kh=None):
        super().__init__(k)
        self.NH, self.R, self.DH, self.NS = NH, B * NH, D // NH, NH // 2
        self.eps, self.cols, self.negm, self.var, self.kh = eps, cols, negm, var, kh
        self.scale = float(self.DH) ** -0.5
        S_ = self.sem
        self.landed = [S_(f"landed{u}") for u in range(2)]
        self.m_landed = S_("m_landed")
        self.q_ready, self.arg1_ready, self.arg_ready = S_("q_ready"), S_("arg1_ready"), S_("arg_ready")
        self.d_ready, self.masked = S_("d_ready"), S_("masked")
        self.qk_ready, self.qk_read, self.ct_ready = S_("qk_ready"), S_("qk_read"), S_("ct_ready")
        self.hm_done, self.h_ready, self.h_read = S_("hm_done"), S_("h_ready"), S_("h_read")
        self.own = S_("chain")
        self.cent_ready, self.cent_kept, self.sq_ready, self.var_done = S_("cent_ready"), S_("cent_kept"), S_("sq_ready"), S_("var_done")
        sb, DH = k.scoped, self.DH
        self.cT = [sb(f"{tag}_cT{u}", [P, KC, S], F32) for u in range(2)]
        self.qm = [sb(f"{tag}_qm{u}", [P, self.NS, KC, S], F32) for u in range(2)]
        self.heads = k.strip if self.NS == 4 else k.halves
        self.v = [sb(f"{tag}_v{u}", [P, HALVES, NH, DH + 1], F32) for u in range(2)]
        self.nm = sb(f"{tag}_nm", [P, NH, S], F32)
        self.d0 = [sb(f"{tag}_d0{u}", [P, NH, S], F32) for u in range(2)]
        self.d1 = [sb(f"{tag}_d1{u}", [P, NH, P], F32) for u in range(2)]
        self.ct = [sb(f"{tag}_ct{u}", [P, 2 * S + 2 * P], F32) for u in range(2)]
        self.tmp = [sb(f"{tag}_tmp{u}", [P, 2 * S + 2 * P], F32) for u in range(2)] if kh else None
        self.den = sb(tag + "_den", [P, HALVES, NH], F32)
        self.mu = sb(tag + "_mu", [P, HALVES * NH], F32)
        self.h1 = sb(tag + "_h1", [P, HALVES * NH, DH], F32)
        self.sq = sb(tag + "_sq", [P, HALVES * NH, DH], F32)

    def sync(self, sp):
        k, NH = self.k, self.NH
        ctxT = k.ins["ctxT"].rearrange("(c p) t -> p c t", p=P)
        ctx = k.ins["ctx_1024"].rearrange("b (s p) (h d) -> p b s h d", p=P, h=NH)
        negm = self.negm.rearrange("r s -> (r s)")
        with sp.Fori(0, B // 2) as i:
            for u in range(2):
                b = i * 2 + u
                sp.wait_ge(self.arg_ready, b + 1)
                sp.dma_start(self.nm[:].rearrange("p h s -> p (h s)"),
                             negm[ds(i * 2 * NH * S + u * NH * S, NH * S)].partition_broadcast(P)).then_inc(self.m_landed, 16)
                sp.wait_ge(self.h_ready, b + 1)
                sp.dma_start(self.cT[u][:], ctxT[:, :, ds(i * 2 * S + u * S, S)]).then_inc(self.landed[u], 16)
                for s in range(HALVES):
                    sp.dma_start(self.v[u][:, s, :, 0:self.DH],
                                 ctx[:, ds(b, 1), s].rearrange("p o h d -> p (o h) d")).then_inc(self.landed[u], 16)

    def tensor(self, pe):
        k, DH, NS, NH = self.k, self.DH, self.NS, self.NH
        pe.sem_inc(self.h_ready, 2)
        pe.sem_inc(self.hm_done, 2)

        def qk(i, u, r):
            n = (i * 2 + u) * NS
            pair = (u * NS + r) % 2
            if r == 0:
                pe.wait_ge(self.landed[u], i * 48 + 48)
                pe.wait_ge(self.q_ready, i * 2 + (u + 1))
            pe.wait_ge(self.qk_read, n + (r + 1))
            for c in range(KC):
                pe.matmul(k.bank[2 * pair][:, c * S:(c + 1) * S], self.cT[u][:, c, 0:P], self.qm[u][:, r, c, :],
                          start=True, stop=True)
            for c in range(KC):
                ins = pe.matmul(k.bank[2 * pair + 1][:, c * P:(c + 1) * P], self.cT[u][:, c, P:S],
                                self.qm[u][:, r, c, P:S], start=True, stop=True)
            ins.then_inc(self.qk_ready, 1)

        def hm(i, u, r):
            n = (i * 2 + u) * NS
            ct = self.ct[(u * NS + r) % 2]
            if r == 0:
                pe.wait_ge(self.h_read, i * 2 + (u + 1))
            pe.wait_ge(self.ct_ready, n + (r + 1))
            for c in range(KC):
                h = c * NS + r
                cols = slice(h * (DH + 1), (h + 1) * (DH + 1))
                pe.matmul(k.bank[4 + 2 * u][:, cols], ct[:, c * S:c * S + P], self.v[u][:, 0, h, :], start=True, stop=True)
                pe.matmul(k.bank[5 + 2 * u][:, cols], ct[:, c * S + P:(c + 1) * S], self.v[u][:, 0, h, :], start=True, stop=False)
                ins = pe.matmul(k.bank[5 + 2 * u][:, cols], ct[:, 2 * S + c * P:2 * S + (c + 1) * P], self.v[u][:, 1, h, :],
                                start=False, stop=True)
            ins.then_inc(self.hm_done, 1)
            if r == NS - 1:
                pe.wait_ge(self.hm_done, n + (NS + 2))
                pe.sem_inc(self.h_ready, 1)

        def body(i, first, last):
            for u in range(2):
                for r in range(NS):
                    qk(i, u, r)
                    if r:
                        hm(i, u, r - 1)
                    elif not (first and u == 0):
                        hm(i + u - 1, 1 - u, NS - 1)
            if last:
                hm(i, 1, NS - 1)

        self.batch_pairs(pe, body)

    def scalar(self, act):
        k = self.k
        act.sem_inc(self.cent_kept, 1)
        lnT = k.lnT[:].rearrange("p (c t) -> p c t", c=KC)

        def q_in(i, u):
            wait_apart(act, self.h_ready, i * 2 + (u + 1), k.passed)
            for r in range(self.NS):
                ins = act.activation(self.qm[u][:, r], lnT[:, :, ds(i * 2 * S + u * S, S)], ACT.Identity,
                                     scale=self.heads[:, r:r + 1])
            ins.then_inc(self.q_ready, 1)

        def decay(i, u):
            act.wait_ge(self.arg1_ready, i * 2 + (u + 1))
            act.activation(self.d1[u][:], self.d1[u][:], ACT.Exp).then_inc(self.d_ready, 1)
            act.wait_ge(self.arg_ready, i * 2 + (u + 2))
            act.activation(self.d0[u][:], self.d0[u][:], ACT.Exp).then_inc(self.d_ready, 1)

        def keep(i, u):
            b = i * 2 + u
            act.wait_ge(self.cent_ready, b + 1)
            act.activation(self.sq[:], self.h1[:], ACT.Square).then_inc(self.sq_ready, 1)
            wait_apart(act, self.q_ready, b + 1, k.passed)
            act.copy(lnT[:, :, ds(i * 2 * S + u * S, S)],
                     self.h1[:].rearrange("p (s h) d -> p s (h d)", s=HALVES)).then_inc(self.cent_kept, 1)

        q_in(0, 0)
        decay(0, 0)

        def body(i, first, last):
            for u in range(2):
                if not (last and u == 1):
                    q_in(i + u, 1 - u)
                if not (first and u == 0):
                    keep(i + u - 1, 1 - u)
                if not (last and u == 1):
                    decay(i + u, 1 - u)
            if last:
                keep(i, 1)

        self.batch_pairs(act, body)

    def batch_pairs(self, eng, body):
        body(0, True, False)
        with eng.Fori(1, B // 2 - 1) as i:
            body(i, False, False)
        body(B // 2 - 1, False, True)

    def views(self, u, r, buf):
        NS = self.NS
        for t, (a, w) in enumerate(((0, S), (2 * S, P))):
            d = (self.d0 if t == 0 else self.d1)[u][:].rearrange("p (c r) s -> p c r s", r=NS)[:, :, r, :]
            yield t, w, buf[:, a:a + 2 * w].rearrange("p (c s) -> p c s", c=KC), d

    def vector(self, dve):
        k, DH, NS, NH, R = self.k, self.DH, self.NS, self.NH, self.R
        LINKS = 7
        chain = Chain(dve, self.own)
        dve.sem_inc(self.qk_read, 2)
        dve.sem_inc(self.h_read, 2)
        dve.sem_inc(self.arg_ready, 1)
        for u in range(2):
            ins = dve.memset(self.v[u][:, :, :, DH:DH + 1], 1.0)
        dve.sem_inc(self.var_done, 1)

        def args(i, u, t):
            b = i * 2 + u
            if t:
                dve.wait_ge(self.m_landed, b * 16 + 16)
                dve.wait_ge(self.h_ready, b + 1)
            for h in range(NH):
                dst = self.d1[u][:, h, :] if t else self.d0[u][:, h, :]
                src = self.nm[:, h, P:S] if t else self.nm[:, h, :]
                ins = dve.tensor_scalar(dst, src, self.cols[:, ds(i * 2 * NH + (t * R + u * NH + h), 1)], 0.0,
                                        ALU.add, ALU.min)
            ins.then_inc(self.arg1_ready if t else self.arg_ready, 1)

        def ct(i, u, r):
            n = (i * 2 + u) * NS
            pair = (u * NS + r) % 2
            if r == 0 and not self.kh:
                dve.wait_ge(self.masked, i * 4 + (2 * u + 2))
            dve.wait_ge(self.qk_ready, n + (r + 1))
            dve.wait_ge(self.hm_done, n + (r + 1))
            buf = self.tmp[pair] if self.kh else self.ct[pair]
            for t, w, dst, d in self.views(u, r, buf):
                src = k.bank[2 * pair + t][:, 0:2 * w].rearrange("p (c s) -> p c s", c=KC)
                if self.kh:
                    hop = self.kh[t].rearrange("p (v c m) -> p c v m", c=KC, m=4 * B)
                    hop = hop[:, :, :, ds(i * 8 + (u * 4 + r), 1)].rearrange("p c v o -> p c (v o)")
                    ins = dve.scalar_tensor_tensor(out=dst, in0=src, scalar=self.scale, in1=hop, op0=ALU.mult, op1=ALU.add)
                else:
                    ins = dve.scalar_tensor_tensor(out=dst, in0=src, scalar=self.scale, in1=d, op0=ALU.mult, op1=ALU.mult)
            ins.then_inc(self.qk_read, 1)
            if not self.kh:
                dve.wait_ge(self.qk_read, n + (r + 3))
                dve.sem_inc(self.ct_ready, 1)

        def divide(i, u):
            b = i * 2 + u
            chain.start(i * 2 * LINKS + u * LINKS)
            dve.wait_ge(self.h_ready, b + 3)
            h_ps = k.ps[:, (4 + 2 * u) * 512:(6 + 2 * u) * 512].rearrange("p (s w) -> p s w", s=HALVES)
            h_ps = h_ps[:, :, 0:NH * (DH + 1)].rearrange("p s (h e) -> p s h e", e=DH + 1)
            en = self.cols[:, 2 * R:4 * R].rearrange("p (s r) -> p s r", s=HALVES)[:, :, ds(i * 2 * NH + u * NH, NH)]
            chain.link(dve.tensor_tensor(self.den[:], h_ps[:, :, :, DH], en, ALU.max))
            chain.link(dve.scalar_tensor_tensor(out=self.den[:], in0=h_ps[:, :, :, DH], scalar=-1.0, in1=self.den[:],
                                                op0=ALU.mult, op1=ALU.max))
            chain.link(dve.tensor_scalar(self.den[:], self.den[:], self.eps, None, ALU.add))
            chain.link(dve.reciprocal(self.den[:], self.den[:]))
            dve.wait_ge(self.cent_kept, b + 1)
            h1 = self.h1[:].rearrange("p (s h) d -> p s h d", s=HALVES)
            dve.tensor_tensor(h1, h_ps[:, :, :, 0:DH], self.den[:].unsqueeze(3).to_broadcast([P, HALVES, NH, DH]),
                              ALU.mult).then_inc(self.h_read, 1)

        def centre(i, u):
            dve.wait_ge(self.h_read, i * 2 + u + 3)
            chain.link(dve.tensor_reduce(self.mu[:], self.h1[:], AX.X, ALU.add))
            chain.link(dve.tensor_scalar(self.mu[:], self.mu[:], 1.0 / DH, None, ALU.mult))
            dve.tensor_tensor(self.h1[:], self.h1[:], self.mu[:].unsqueeze(2).to_broadcast([P, HALVES * NH, DH]),
                              ALU.subtract).then_inc(self.cent_ready, 1)

        def variance(i, u):
            dve.wait_ge(self.sq_ready, i * 2 + u + 1)
            chain.link(dve.tensor_reduce(self.var[:].rearrange("p (s r) -> p s r", s=HALVES)[:, :, ds(i * 2 * NH + u * NH, NH)],
                              self.sq[:].rearrange("p (s h) d -> p s h d", s=HALVES), AX.X, ALU.add))

        args(0, 0, 1)
        args(0, 0, 0)

        def body(i, first, last):
            for u in range(2):
                for r in range(NS):
                    ct(i, u, r)
                    before, after = not (first and u == 0), not (last and u == 1)
                    if r == 0 and before:
                        divide(i + u - 1, 1 - u)
                    if r == NS // 2 - 1:
                        if before:
                            centre(i + u - 1, 1 - u)
                        if after:
                            args(i + u, 1 - u, 1)
                            args(i + u, 1 - u, 0)
                    if r == NS - 2 and before:
                        variance(i + u - 1, 1 - u)
            if last:
                for step in (divide, centre, variance):
                    step(i, 1)

        self.batch_pairs(dve, body)

    def gpsimd(self, pool):
        k, NS, NH = self.k, self.NS, self.NH

        def mask(i, u, t):
            cm = k.causal01[:].unsqueeze(1).to_broadcast([P, NH, P])
            d = self.d1[u][:] if t else self.d0[u][:, :, 0:P]
            pool.wait_ge(self.d_ready, i * 4 + (2 * u + 2 - t))
            pool.tensor_tensor(d, d, cm, ALU.mult).then_inc(self.masked, 1)

        def ct(i, u, r):
            n = (i * 2 + u) * NS
            pair = (u * NS + r) % 2
            if r == 0:
                pool.wait_ge(self.masked, i * 4 + (2 * u + 2))
            pool.wait_ge(self.qk_read, n + (r + 3))
            pool.wait_ge(self.hm_done, n + (r + 1))
            for (t, w, dst, d), (_, _, src, _) in zip(self.views(u, r, self.ct[pair]), self.views(u, r, self.tmp[pair])):
                ins = pool.tensor_tensor(dst, src, d, ALU.mult)
            ins.then_inc(self.ct_ready, 1)

        mask(0, 0, 1)
        mask(0, 0, 0)

        def body(i, first, last):
            for u in range(2):
                for r in range(NS):
                    if self.kh:
                        ct(i, u, r)
                    if not (last and u == 1):
                        if r == NS // 2 - 1:
                            mask(i + u, 1 - u, 1)
                        if r == NS // 2:
                            mask(i + u, 1 - u, 0)

        self.batch_pairs(pool, body)


class MlstmOut(Stage):

    def __init__(self, k, tag, NH, g, var, w, b=None):
        super().__init__(k)
        self.NH, self.R, self.DH, self.g, self.var, self.w_dram, self.b_dram = NH, B * NH, D // NH, g, var, w, b
        S_ = self.sem
        self.landed, self.own, self.inv_ready, self.rstd_ready = S_("landed"), S_("chain"), S_("inv_ready"), S_("rstd_ready")
        self.wrow = k.scoped(tag + "_wrow", [P, D], F32)
        self.brow = k.scoped(tag + "_brow", [P, D], F32)

    def sync(self, sp):
        sp.dma_start(self.wrow[:], self.w_dram.partition_broadcast(P)).then_inc(self.landed, 16)
        if self.b_dram is not None:
            sp.dma_start(self.brow[:], self.b_dram.partition_broadcast(P)).then_inc(self.landed, 16)

    def scalar(self, act):
        act.wait_ge(self.inv_ready, 1)
        act.activation(self.var[:], self.var[:], ACT.Sqrt).then_inc(self.rstd_ready, 1)

    def vector(self, dve):
        k, R, DH = self.k, self.R, self.DH
        chain = Chain(dve, self.own)
        tg = k.tanh_g[:, self.g:self.g + 1]
        chain.link(dve.tensor_scalar(self.var[:], self.var[:], 1.0 / DH, LN_EPS, ALU.mult, ALU.add))
        dve.reciprocal(self.var[:], self.var[:]).then_inc(self.inv_ready, 1)
        dve.wait_ge(self.landed, 16 * (1 + (self.b_dram is not None)))
        chain.link(dve.tensor_scalar(self.wrow[:], self.wrow[:], 1.0, tg, ALU.add, ALU.mult))
        if self.b_dram is not None:
            chain.link(dve.tensor_scalar(self.brow[:], self.brow[:], tg, None, ALU.mult))
        dve.wait_ge(self.rstd_ready, 1)
        for half in range(HALVES):
            h = k.lnT[:, half * T:half * T + B * D]
            chain.link(dve.tensor_tensor(h.rearrange("p (r d) -> p r d", d=DH), h.rearrange("p (r d) -> p r d", d=DH),
                                         self.var[:, half * R:(half + 1) * R].unsqueeze(2).to_broadcast([P, R, DH]), ALU.mult))
            h3 = h.rearrange("p (b d) -> p b d", d=D)
            row = lambda a: a[:].unsqueeze(1).to_broadcast([P, B, D])
            chain.link(dve.tensor_tensor(h3, h3, row(self.wrow), ALU.mult))
            x = k.x[:].rearrange("p (b s d) -> p s b d", s=HALVES, d=D)[:, half]
            chain.link(dve.tensor_tensor(x, h3, x, ALU.add))
            if self.b_dram is not None:
                chain.link(dve.tensor_tensor(x, x, row(self.brow), ALU.add))


class Buffers:
    pass


class Kernel:
    def __init__(self, nc, ctx, ins, out):
        self.nc, self.ctx, self.ins, self.out = nc, ctx, ins, out
        self.stage_sems, self.rounds = {}, {}
        self.b = Buffers()
        sb, F = self.sb, F32
        self.x = sb("x", [P, NT * D], F)
        self.lnT = sb("lnT", [P, KC * T], F)
        self.ident = sb("ident", [P, P], F)
        self.rank = sb("rank", [P, E], F)
        self.graw = sb("graw", [P, 8], F)
        self.tanh_g = sb("tanh_g", [P, 8], F)
        self.ps = ctx.enter_context(nc.psum_tensor("ps", [P, 8 * 512], F))
        self.bank = [self.ps[:, n * 512:(n + 1) * 512] for n in range(8)]
        self.ident_bf = sb("ident_bf", [P, P], BF16)
        self.causal_bf = sb("causal_bf", [P, P], BF16)
        self.causal01 = sb("causal01", [P, P], F)
        self.ones_f = sb("ones_f", [P, P], F)
        self.ones_row = self.ones_f[0:1, :]
        self.ones_bf = sb("ones_bf", [P, P], BF16)
        self.before_bf = sb("before_bf", [P, P], BF16)
        self.tile_rowi = sb("tile_rowi", [1, SLOT_TILES], I32)
        self.tile_row = sb("tile_row", [1, SLOT_TILES], F)
        self.tile_expert = sb("tile_expert", [1, SLOT_TILES], I32)
        self.slots = sb("slots", [P, 2, NT], mybir.dt.uint32)
        self.zeros = sb("zeros", [P, D], F)
        self.slot_x = nc.dram_tensor("slot_x", (SLOT_TILES * P, D), F, kind="Internal").ap()
        self.slot_y = nc.dram_tensor("slot_y", (SLOT_TILES * P, D), F, kind="Internal").ap()
        self.slots_zeroed = self.sem("slots_zeroed")
        self.weights_landed = self.sem("weights_landed")
        self.weights_due = 0
        self.prow = sb("prow", [P, 1], I32)
        self.pbits = sb("pbits", [P, 2], I32)
        self.pbitsf = sb("pbitsf", [P, 2], F)
        self.head16 = sb("head16", [P, 8], F)
        self.strip = sb("strip", [P, 4], F)
        self.halves = sb("halves", [P, 2], F)

        self.setup_loaded = self.sem("setup_loaded")
        self.setup_dve = self.sem("setup_dve")
        self.setup_pool = self.sem("setup_pool")
        self.setup_tanh = self.sem("setup_tanh")
        self.passed = self.sem("passed")
        self.stored = self.sem("stored")
        self.over = {e: self.sem(e + "_over") for e in ("pe", "act", "dve", "pool", "sp")}

    def sb(self, name, shape, dt):
        return self.ctx.enter_context(self.nc.sbuf_tensor(name, shape, dt))

    def ln_buffers(self, tag, rows=2):
        self.b.ln_stats = self.scoped(tag + "_ln_stats", [P, NT * 6], F32)
        self.b.ln_mv = self.scoped(tag + "_ln_mv", [P, NT, 2], F32)
        self.b.ln_mean = self.scoped(tag + "_ln_mean", [P, NT], F32)
        self.b.ln_inv = self.scoped(tag + "_ln_inv", [P, NT], F32)
        self.b.ln_rstd = self.scoped(tag + "_ln_rstd", [P, NT], F32)
        self.b.ln_x = [self.scoped(tag + f"_ln_x{u}", [P, 4, D], F32) for u in range(rows)]

    def router_buffers(self, tag):
        self.b.wg = self.scoped(tag + "_wg", [P, KC, E], F32)
        self.b.bg = self.scoped(tag + "_bg", [P, E], F32)
        self.b.rt = self.scoped(tag + "_rt", [P, 6, NT, E], F32)
        self.b.rs = self.scoped(tag + "_rs", [P, 6, NT], F32)
        self.b.rexp = self.scoped(tag + "_rexp", [P, NT], F32)
        self.b.gate = self.scoped(tag + "_gate", [P, NT * E], F32)
        self.b.gate3 = self.b.gate[:].rearrange("p (t e) -> p t e", e=E)

    def bias_buffers(self, tag):
        self.b.gateT = self.scoped(tag + "_gateT", [E, T], F32)
        self.b.ebias = self.scoped(tag + "_ebias", [E, D], F32)

    def expert_weights(self, tag, up, down, b1=None):
        up = up.rearrange("e (c p) f -> e p c f", p=P)
        down = down.rearrange("e (c p) h -> e p c h", p=P)
        self.b.w_up = self.scoped(tag + "_w_up", [P, E * KC * up.shape[3]], F32)
        self.b.w_down = self.scoped(tag + "_w_down", [P, E * down.shape[2] * D], F32)
        by_expert = lambda w, like: w[:].rearrange("p (e c f) -> p e c f", e=E, c=like.shape[2])
        loads = [(by_expert(self.b.w_up, up)[:, e], up[e]) for e in range(E)]
        loads += [(by_expert(self.b.w_down, down)[:, e], down[e]) for e in range(E)]
        if b1 is not None:
            self.b.b1_all = self.scoped(tag + "_b1_all", [P, E * up.shape[3]], F32)
            loads.append((self.b.b1_all[:], b1.rearrange("e f -> (e f)").partition_broadcast(P)))
        self.weights_due += 16 * len(loads)
        return loads

    def scoped(self, name, shape, dt):
        return self.scope.enter_context(self.nc.sbuf_tensor(name, shape, dt))

    def shared_sem(self, name):
        if name not in self.stage_sems:
            self.stage_sems[name] = self.sem(name)
        return self.stage_sems[name]

    def sem(self, name):
        return self.ctx.enter_context(self.nc.semaphore(name))


class Setup(Stage):

    def sync(self, sp):
        k = self.k
        x = k.ins["x"].rearrange("b s d -> (b s) d").rearrange("(t p) d -> p t d", p=P)
        sp.dma_start(k.x[:].rearrange("p (t d) -> p t d", d=D), x).then_inc(k.setup_loaded, 16)
        sp.dma_start(k.graw[:, 0:4], k.ins["g_xattn"].partition_broadcast(P)).then_inc(k.setup_loaded, 16)
        sp.dma_start(k.graw[:, 4:8], k.ins["g_ffn"].partition_broadcast(P)).then_inc(k.setup_loaded, 16)
        sp.wait_ge(k.setup_pool, 13 + E)
        sp.dma_start(k.slot_x.rearrange("(j p) d -> p j d", p=P),
                     k.zeros[:].unsqueeze(1).to_broadcast([P, SLOT_TILES, D])).then_inc(k.slots_zeroed, 16)
        sp.wait_ge(k.setup_loaded, 48)

    def gpsimd(self, pool):
        k = self.k
        pool.memset(k.ident[:], 0.0).then_inc(k.setup_pool, 1)
        pool.wait_ge(k.setup_pool, 1)
        pool.affine_select(out=k.ident[:], in_=k.ident[:], compare_op=ALU.not_equal, fill=1.0, base=0,
                           pattern=[[-1, P]], channel_multiplier=1).then_inc(k.setup_pool, 1)
        for e in range(E):
            pool.memset(k.rank[:, e:e + 1], float(E - e)).then_inc(k.setup_pool, 1)
        pool.memset(k.causal_bf[:], 0.0).then_inc(k.setup_pool, 1)
        pool.memset(k.ones_f[:], 1.0).then_inc(k.setup_pool, 1)
        pool.memset(k.ones_bf[:], 1.0).then_inc(k.setup_pool, 1)
        pool.memset(k.before_bf[:], 1.0).then_inc(k.setup_pool, 1)
        pool.memset(k.zeros[:], 0.0).then_inc(k.setup_pool, 1)
        pool.iota(k.tile_rowi[:], pattern=[[1, SLOT_TILES]], base=0, channel_multiplier=0).then_inc(k.setup_pool, 1)
        pool.memset(k.causal01[:], 1.0).then_inc(k.setup_pool, 1)
        pool.iota(k.prow[:], pattern=[[0, 1]], base=0, channel_multiplier=1).then_inc(k.setup_pool, 1)
        pool.wait_ge(k.setup_pool, 10 + E)
        pool.affine_select(out=k.causal_bf[:], in_=k.causal_bf[:], compare_op=ALU.is_ge, fill=-BIG, base=0,
                           pattern=[[-1, P]], channel_multiplier=1).then_inc(k.setup_pool, 1)
        pool.affine_select(out=k.causal01[:], in_=k.causal01[:], compare_op=ALU.is_ge, fill=0.0, base=0,
                           pattern=[[1, P]], channel_multiplier=-1).then_inc(k.setup_pool, 1)
        pool.affine_select(out=k.before_bf[:], in_=k.before_bf[:], compare_op=ALU.is_ge, fill=0.0, base=-1,
                           pattern=[[1, P]], channel_multiplier=-1).then_inc(k.setup_pool, 1)

    def vector(self, dve):
        k = self.k
        chain = Chain(dve, k.setup_dve)
        dve.wait_ge(k.setup_pool, 13 + E)
        chain.link(dve.tensor_copy(k.ident_bf[:], k.ident[:]))
        chain.link(dve.tensor_copy(k.tile_row[:], k.tile_rowi[:]))
        chain.link(dve.tensor_scalar(k.pbits[:, 0:1], k.prow[:], 112, None, ALU.bitwise_and))
        chain.link(dve.tensor_scalar(k.pbits[:, 1:2], k.prow[:], 96, None, ALU.bitwise_and))
        chain.link(dve.tensor_copy(k.pbitsf[:], k.pbits[:]))
        for h in range(8):
            dve.tensor_scalar(k.head16[:, h:h + 1], k.pbitsf[:, 0:1], 16.0 * h, None, ALU.is_equal)
        for r in range(4):
            dve.tensor_scalar(k.strip[:, r:r + 1], k.pbitsf[:, 1:2], 32.0 * r, None, ALU.is_equal)
        for r in range(2):
            dve.tensor_scalar(k.halves[:, r:r + 1], k.pbitsf[:, 1:2], 64.0, float(r), ALU.is_ge, ALU.is_equal)

    def scalar(self, act):
        k = self.k
        act.wait_ge(k.setup_loaded, 48)
        act.activation(k.tanh_g[:], k.graw[:], ACT.Tanh).then_inc(k.setup_tanh, 1)


class Store(Stage):
    def sync(self, sp):
        k = self.k
        out = k.out.rearrange("b s d -> (b s) d").rearrange("(t p) d -> p t d", p=P)
        sp.dma_start(out, k.x[:].rearrange("p (t d) -> p t d", d=D)).then_inc(k.stored, 16)
        sp.wait_ge(k.stored, 16)


def make_stages(k):
    I = k.ins
    stages = [Setup(k)]

    @contextmanager
    def scope():
        with ExitStack() as k.scope:
            yield

    def layer_norm(tag):
        with scope():
            k.ln_buffers(tag)
            stages.append(LayerNorm(k, tag))

    def mlstm(tag, layer, NH, eps, g, shifted, w, b=None, rpe=None, hop_units=None):
        R = B * NH
        negm = k.nc.dram_tensor(tag + "_negm", (R, S), F32, kind="Internal").ap()
        with ExitStack() as held:
            sb = lambda n, shape: held.enter_context(k.nc.sbuf_tensor(f"{tag}_{n}", shape, F32))
            cols, var = sb("cols", [P, 4 * R]), sb("var", [P, HALVES * R])
            hops = kh = None
            with ExitStack() as until_hops:
                if rpe is not None:
                    k.held = lambda n, shape, dt: until_hops.enter_context(k.nc.sbuf_tensor(n, shape, dt))
                    kh_all = sb("kh", [P, (S + P) * 64])
                    hops, kh = Hops(k, tag + "_hp", kh_all, rpe, hop_units), kh_split(kh_all)
                with scope():
                    k.ln_buffers(tag + "_ln")
                    stages.append(LayerNorm(k, tag + "_ln", beside=hops))
                with scope():
                    stages.append(MlstmGates(k, tag + "_mg", NH, I[layer + "_gate_w"], I[layer + "_gate_b"], shifted, cols, negm,
                                             hops))
                if hops:
                    with scope():
                        hops.buffers(tag + "_hp")
                        stages.append(hops)
            with scope():
                stages.append(Mlstm(k, tag + "_ml", NH, eps, cols, negm, var, kh))
            with scope():
                stages.append(MlstmOut(k, tag + "_mo", NH, g, var, w, b))

    def moe(tag, n, wg, bg=None, bias=None, dense=None, kind=None, up=None, down=None, b1=None):
        with scope():
            k.ln_buffers(tag + "_ln", rows=2 if kind is None else 4)
            k.router_buffers(tag)
            if bias is not None:
                k.bias_buffers(tag)
            loads = None if kind is None else k.expert_weights(tag, up, down, b1)
            stages.append(LayerNorm(k, tag + "_ln", loads))
            stages.append(Router(k, tag + "_rt", wg, 4 + n, bg))
            if bias is not None:
                stages.append(GateBias(k, tag + "_gb", bias))
            if dense is not None:
                stages.append(LinearExperts(k, tag + "_ex", dense))
            else:
                stages.append(Dispatch(k, tag + "_di"))
                stages.append(ExpertTiles(k, tag + "_et", kind, up.shape[2] // P, down.shape[1] // P))
                stages.append(Combine(k, tag + "_co"))

    for n in SUBLAYERS:
        tag = f"s{n}"
        k.b = Buffers()
        if n in (2, 4):
            layer_norm(tag + "_ln")
        if n == 0:
            mlstm(tag, "L0", 4, 1e-8, 0, True, I["L0_xattn_out_w"])
        if n == 1:
            moe(tag, 0, I["L0_ffn_Wg"], bias=I["L0_ffn_be"], dense=I["L0_ffn_We"])
        if n == 2:
            with scope():
                stages.append(Attention(k, tag + "_at", 1, True, *(I["L1_xattn_w_" + m] for m in "qkvo"),
                                        *(I["L1_xattn_b_" + m] for m in "oqkv")))
        if n == 3:
            moe(tag, 1, I["L1_ffn_router_w"], kind="glu", up=I["L1_ffn_up_proj"], down=I["L1_ffn_down_proj"])
        if n == 4:
            with scope():
                stages.append(Attention(k, tag + "_at", 2, False, *(I["L2_xattn_W" + m] for m in "qkvo"),
                                        I["L2_xattn_bo"]))
        if n == 5:
            moe(tag, 2, I["L2_ffn_router_w"], kind="silu", up=I["L2_ffn_w1"], down=I["L2_ffn_w2"])
        if n == 6:
            mlstm(tag, "L3", 8, 1e-6, 3, False, I["L3_xattn_ln_w"], I["L3_xattn_ln_b"],
                  I["L3_xattn_rpe"], I["hop_units"])
        if n == 7:
            moe(tag, 3, I["L3_ffn_Wg"], bg=I["L3_ffn_bg"], bias=I["L3_ffn_b2"], kind="relu",
                up=I["L3_ffn_W1"], down=I["L3_ffn_W2"], b1=I["L3_ffn_b1"])
    stages.append(Store(k))
    return stages


def flamingo_stack(nc, ins, out):
    with ExitStack() as ctx:
        k = Kernel(nc, ctx, ins, out)
        stages = make_stages(k)
        block = ctx.enter_context(nc.Block())

        def between(eng, name, n):
            eng.drain().then_inc(k.over[name], 1)
            for other, over in k.over.items():
                eng.wait_ge(over, n + 1)

        @block.sync
        def _(sp):
            for n, stage in enumerate(stages):
                if n:
                    for sem in stages[n - 1].sems:
                        sp.sem_clear(sem)
                stage.sync(sp)
                between(sp, "sp", n)

        @block.gpsimd
        def _(pool):
            for n, stage in enumerate(stages):
                stage.gpsimd(pool)
                between(pool, "pool", n)

        @block.scalar
        def _(act):
            for n, stage in enumerate(stages):
                stage.scalar(act)
                between(act, "act", n)

        @block.vector
        def _(dve):
            for n, stage in enumerate(stages):
                stage.vector(dve)
                between(dve, "dve", n)

        @block.tensor
        def _(pe):
            for n, stage in enumerate(stages):
                stage.tensor(pe)
                between(pe, "pe", n)


def laid_out(inputs):
    import numpy as _np

    T_ = lambda a, *d: _np.ascontiguousarray(_np.transpose(_np.asarray(a), d))
    keep = {n: _np.ascontiguousarray(a) for n, a in inputs.items()}
    keep["L1_ffn_router_w"] = T_(inputs["L1_ffn_router_w"], 1, 0)
    keep["L3_ffn_Wg"] = T_(inputs["L3_ffn_Wg"], 1, 0)
    keep["L3_ffn_W1"] = T_(inputs["L3_ffn_W1"], 0, 2, 1)
    keep["L3_ffn_W2"] = T_(inputs["L3_ffn_W2"], 0, 2, 1)
    for l in ("L0", "L3"):
        keep[l + "_gate_w"] = _np.ascontiguousarray(_np.concatenate(
            [_np.asarray(inputs[f"{l}_xattn_{g}gate_w"]).T for g in "if"], axis=1))
        keep[l + "_gate_b"] = _np.concatenate([_np.asarray(inputs[f"{l}_xattn_{g}gate_b"]) for g in "if"])
    hops = _np.asarray(inputs["itok_SxS2_0_2016"])
    units = []
    for h in range(2):
        for g in range(16):
            v = lambda q, e: 128 * h + 32 * q + 2 * g + e
            part = lambda q, e: hops[v(q, e), 128 * h:128 * h + 32 * (q + 1)]
            units += [part(3, 0), part(3, 1)] + [_np.concatenate([part(2, e), part(0, e)]) for e in range(2)]
            units.append(_np.concatenate([part(1, 0), part(1, 1)]))
            if h:
                units += [hops[v(q, e), :128] for q in range(4) for e in range(2)]
    keep["hop_units"] = _np.ascontiguousarray(_np.stack(units, axis=1))
    keep["ctxT"] = _np.ascontiguousarray(_np.asarray(inputs["ctx_1024"]).reshape(T, D).T)
    for n in [f"L1_xattn_w_{m}" for m in "qkvo"] + [f"L2_xattn_W{m}" for m in "qkvo"]:
        keep[n] = T_(inputs[n], 1, 0)
    for n in ("L1_xattn_b_q", "L1_xattn_b_k"):
        keep[n] = T_(_np.asarray(inputs[n]).reshape(2, 128), 1, 0)
    return keep


def kernel(**inputs):
    import numpy as _np
    import concourse.bacc as _bacc
    from concourse import mybir as _mybir
    from concourse.bass_utils import run_bass_kernel_spmd as _run

    nc = _bacc.Bacc("TRN2", target_bir_lowering=False, num_devices=1)
    arrays, ins = {}, {}
    for name, a in laid_out(inputs).items():
        arrays[f"in_{name}"] = a
        ins[name] = nc.dram_tensor(f"in_{name}", a.shape, _mybir.dt.from_np(a.dtype), kind="ExternalInput").ap()
    out = nc.dram_tensor("out", (8, 256, 256), F32, kind="ExternalOutput").ap()
    flamingo_stack(nc, ins, out)
    r = _run(nc, [arrays], core_ids=[0])
    return r.results[0]["out"]
```
